# Optimizing a Trainium2 kernel written in Bass

```python
import numpy as np
import jax
import jax.numpy as jnp

def _softmax(x, axis=-1):
    return jax.nn.softmax(x, axis=axis)

def _gelu(x):
    return jax.nn.gelu(x, approximate=True)

def _silu(x):
    return jax.nn.silu(x)

def _sigmoid(x):
    return jax.nn.sigmoid(x)

def _layernorm(x, axis=-1, eps=1e-05):
    m = jnp.mean(x, axis=axis, keepdims=True)
    v = jnp.var(x, axis=axis, keepdims=True)
    return (x - m) / jnp.sqrt(v + eps)

def _scatter_add(tgt, idx, src, axis=0):
    return tgt.at[idx].add(src)

def _segment_sum(src, seg, n):
    return jax.ops.segment_sum(src, seg, n)
kernel_name = 'mk_lm_tower_d1_tok_ids1024_r4_72865e'

def setup_inputs(seed: int=0):
    np.random.seed(seed)
    _w = jnp.asarray

    def _rec_inputs():
        import jax
        import jax.numpy as jnp
        _rk = jax.random.key(seed)
        x = jax.random.randint(jax.random.fold_in(_rk, 1), (16, 512), 0, 8000, jnp.int32)
        return x
    x = _rec_inputs()

    def _L0_tok_setup():
        import jax, jax.numpy as jnp
        import numpy as np
        VOCAB = 8000
        HIDDEN = 128
        OUT = 256
        B, S = (8, 1024)
        key = jax.random.key(seed)
        k_ids, k_emb, k_proj = jax.random.split(key, 3)
        inputs = jax.random.randint(k_ids, (B, S), 0, VOCAB, dtype=jnp.int32)
        embeddings = jax.random.uniform(k_emb, (VOCAB, HIDDEN), dtype=jnp.float32, minval=-0.05, maxval=0.05)
        limit = float(np.sqrt(6.0 / (HIDDEN + OUT)))
        project_kernel = jax.random.uniform(k_proj, (HIDDEN, OUT), dtype=jnp.float32, minval=-limit, maxval=limit)
        return {'inputs': inputs, 'embeddings': embeddings, 'project_kernel': project_kernel}
    _L0_tok_all = _L0_tok_setup()
    _L0_tok_in = {k: v for k, v in _L0_tok_all.items() if k in ('embeddings', 'project_kernel')}
    del _L0_tok_all

    def _L0_attn_setup():
        import jax, jax.numpy as jnp
        import numpy as np
        NUM_HEADS = 16
        BLOCK = 64
        key = jax.random.key(seed)
        k0, k1, k2 = jax.random.split(key, 3)
        B, N, C = (2, 512, 256)
        x = jax.random.normal(k0, (B, N, C), dtype=jnp.float32)
        w_qkv = jax.random.normal(k1, (3 * C, C), dtype=jnp.float32) * 0.02
        w_proj = jax.random.normal(k2, (C, C), dtype=jnp.float32) * 0.02
        b_proj = jnp.zeros((C,), dtype=jnp.float32)
        return {'x': x, 'w_qkv': w_qkv, 'w_proj': w_proj, 'b_proj': b_proj}
    _L0_attn_all = _L0_attn_setup()
    _L0_attn_in = {k: v for k, v in _L0_attn_all.items() if k in ('w_qkv', 'w_proj', 'b_proj')}
    del _L0_attn_all

    def _L0_ffn_setup():
        import jax, jax.numpy as jnp
        import numpy as np
        BLOCK = 32
        W_BITS = 4
        ACT_BITS = 16

        def act_qdq(x):
            qmax = 2.0 ** (ACT_BITS - 1) - 1.0
            scale = jnp.maximum(jnp.max(jnp.abs(x)) / qmax, 1e-12)
            return jnp.clip(jnp.round(x / scale), -qmax - 1.0, qmax) * scale

        def fixed_qdq_u16(x):
            scale = 1.0 / 65536.0
            return jnp.clip(jnp.round(x / scale), 0.0, 65535.0) * scale

        def lpbq_dequant(w):
            O, I = w.shape
            qmax = 2.0 ** (W_BITS - 1) - 1.0
            wb = w.reshape(O, I // BLOCK, BLOCK)
            s = jnp.maximum(jnp.max(jnp.abs(wb), axis=-1, keepdims=True) / qmax, 1e-12)
            wq = jnp.clip(jnp.round(wb / s), -qmax - 1.0, qmax) * s
            return wq.reshape(O, I)
        key = jax.random.key(seed)
        k1, k2, k3, k4 = jax.random.split(key, 4)
        B, S, H, I = (2, 1024, 256, 768)
        x = jax.random.normal(k1, (B, S, H), jnp.float32)
        w_gate = jax.random.normal(k2, (I, H), jnp.float32) * 0.02
        w_up = jax.random.normal(k3, (I, H), jnp.float32) * 0.02
        w_down = jax.random.normal(k4, (H, I), jnp.float32) * 0.02
        return {'x': x, 'w_gate': w_gate, 'w_up': w_up, 'w_down': w_down}
    _L0_ffn_all = _L0_ffn_setup()
    _L0_ffn_in = {k: v for k, v in _L0_ffn_all.items() if k in ('w_gate', 'w_up', 'w_down')}
    del _L0_ffn_all
    return {'x': x, 'L0_tok_embeddings': _L0_tok_in['embeddings'], 'L0_tok_project_kernel': _L0_tok_in['project_kernel'], 'L0_attn_w_qkv': _L0_attn_in['w_qkv'], 'L0_attn_w_proj': _L0_attn_in['w_proj'], 'L0_attn_b_proj': _L0_attn_in['b_proj'], 'L0_ffn_w_gate': _L0_ffn_in['w_gate'], 'L0_ffn_w_up': _L0_ffn_in['w_up'], 'L0_ffn_w_down': _L0_ffn_in['w_down']}

def reference(x, L0_tok_embeddings, L0_tok_project_kernel, L0_attn_w_qkv, L0_attn_w_proj, L0_attn_b_proj, L0_ffn_w_gate, L0_ffn_w_up, L0_ffn_w_down):
    import jax
    import jax.numpy as jnp

    def _L0_tok_ref(inputs, embeddings, project_kernel):
        import jax, jax.numpy as jnp
        import numpy as np
        VOCAB = 8000
        HIDDEN = 128
        OUT = 256
        B, S = (8, 1024)
        gathered = jnp.take(embeddings, inputs, axis=0)
        return jnp.einsum('bsh,ho->bso', gathered, project_kernel)

    def _L0_attn_ref(x, w_qkv, w_proj, b_proj):
        import jax, jax.numpy as jnp
        import numpy as np
        NUM_HEADS = 16
        BLOCK = 64
        B, N, C = x.shape
        H = NUM_HEADS
        hd = C // H
        bs = min(BLOCK, N)
        scale = hd ** (-0.5)
        qkv = (x @ w_qkv.T).reshape(B, N, 3, H, hd).transpose(2, 0, 3, 1, 4)
        q, k, v = (qkv[0], qkv[1], qkv[2])
        blk = jnp.arange(N) // bs
        mask = blk[:, None] >= blk[None, :]
        scores = jnp.einsum('bhqd,bhkd->bhqk', q, k) * scale
        scores = jnp.where(mask, scores, -jnp.inf)
        weights = jax.nn.softmax(scores, axis=-1)
        out = jnp.einsum('bhqk,bhkd->bhqd', weights, v)
        out = out.transpose(0, 2, 1, 3).reshape(B, N, C)
        return out @ w_proj.T + b_proj

    def _L0_ffn_ref(x, w_gate, w_up, w_down):
        import jax, jax.numpy as jnp
        import numpy as np
        BLOCK = 32
        W_BITS = 4
        ACT_BITS = 16

        def act_qdq(x):
            qmax = 2.0 ** (ACT_BITS - 1) - 1.0
            scale = jnp.maximum(jnp.max(jnp.abs(x)) / qmax, 1e-12)
            return jnp.clip(jnp.round(x / scale), -qmax - 1.0, qmax) * scale

        def fixed_qdq_u16(x):
            scale = 1.0 / 65536.0
            return jnp.clip(jnp.round(x / scale), 0.0, 65535.0) * scale

        def lpbq_dequant(w):
            O, I = w.shape
            qmax = 2.0 ** (W_BITS - 1) - 1.0
            wb = w.reshape(O, I // BLOCK, BLOCK)
            s = jnp.maximum(jnp.max(jnp.abs(wb), axis=-1, keepdims=True) / qmax, 1e-12)
            wq = jnp.clip(jnp.round(wb / s), -qmax - 1.0, qmax) * s
            return wq.reshape(O, I)
        x = act_qdq(x)
        up = act_qdq(x @ lpbq_dequant(w_up).T)
        gate = act_qdq(x @ lpbq_dequant(w_gate).T)
        sig = fixed_qdq_u16(jax.nn.sigmoid(gate))
        gate = act_qdq(gate * sig)
        o = act_qdq(gate * up)
        return o @ lpbq_dequant(w_down).T
    h = _L0_tok_ref(x, L0_tok_embeddings, L0_tok_project_kernel)
    h = h + _L0_attn_ref(_layernorm(h, axis=-1), L0_attn_w_qkv, L0_attn_w_proj, L0_attn_b_proj)
    h = h + _L0_ffn_ref(_layernorm(h, axis=-1), L0_ffn_w_gate, L0_ffn_w_up, L0_ffn_w_down)
    return h

_drawn_inputs = setup_inputs


def setup_inputs(seed=0):
    import zlib

    import numpy as np

    out = dict(_drawn_inputs(seed))
    spreads = {'L0_attn_b_proj': (0.0, 0.1)}
    factors = {}
    for name, (base, spread) in spreads.items():
        noise = np.random.default_rng([zlib.crc32(name.encode()), seed]).standard_normal(out[name].shape)
        drawn = base * np.exp(spread * noise) if base else spread * noise
        out[name] = jnp.asarray(drawn.astype(out[name].dtype))
    for name, factor in factors.items():
        out[name] = (out[name] * factor).astype(out[name].dtype)
    return out
```

```python
class Sizes:
    B, N, HID, C, HEADS, HD, I = 16, 512, 128, 256, 16, 16, 768
    WB = 32


def sizes():
    s = Sizes()
    s.T = s.N // 128
    s.KC = s.C // 128
    s.MI = s.I // 128
    s.GROUPS = [list(range(0, 6)), list(range(6, 12)), list(range(12, 16))]
    s.GROWS = 96
    s.EPS = 1e-5
    s.QMAX = 32767.0
    s.SEED, s.DMA_SEED = 1, 16
    s.WSCALE = 1024.0
    return s


def pass_waits(eng, passed):
    eng.sem_inc(passed, 1)


def attention_block(nc, io, keep):
    from contextlib import ExitStack
    import concourse.bass as bass
    import concourse.mybir as mybir
    S = sizes()
    SEED = S.SEED
    F, H16, BF, I32 = mybir.dt.float32, mybir.dt.float16, mybir.dt.bfloat16, mybir.dt.int32
    ACT, ALU, AX = mybir.ActivationFunctionType, mybir.AluOpType, mybir.AxisListType
    B, N, T, C, KC, HEADS, HD = S.B, S.N, S.T, S.C, S.KC, S.HEADS, S.HD
    NG, GR = len(S.GROUPS), S.GROWS
    SCALE = HD ** -0.5
    group_of = {h: (g, hs.index(h)) for g, hs in enumerate(S.GROUPS) for h in hs}

    MAX_TILES = [(3, 0, 0, 512), (2, 1, 0, 384), (0, 1, 384, 128), (1, 2, 0, 256)]
    KEY_TILES = [(0, 0, 0, 512), (1, 1, 0, 384), (3, 1, 384, 128), (2, 2, 0, 256)]
    P_COL = {0: 0, 1: 512, 3: 896, 2: 1024}

    order = [("max", h) for h in range(8)] + [("neg", 0)]
    for k in range(8):
        if k == 6:
            order.append(("neg", 1))
        order.append(("key", k))
        order.append(("max", 8 + k))
        if k == 5:
            order.append(("pv", 0))
    order.append(("neg", 2))
    for k in range(8, 16):
        order.append(("key", k))
        if k == 9:
            order.append(("pv", 1))
        if k == 13:
            order.append(("pv", 2))
    order.append(("pv", 3))

    with ExitStack() as ctx:
        def sb(name, shape, dt=F):
            return ctx.enter_context(nc.sbuf_tensor(name, shape, dt))

        def sem(name):
            return ctx.enter_context(nc.semaphore(name))

        h_all = keep["h_all"]
        ids_all = sb("ids_all", [128, B * T], I32)
        ids = sb("ids", [128, T], I32)
        emb = sb("emb", [128, T, S.HID])
        embT = sb("embT", [128, N])
        w_tok = sb("w_tok", [128, C])
        w_q = sb("w_q", [128, KC, NG * GR])
        w_k = sb("w_k", [128, KC, NG * GR])
        w_v = sb("w_v", [128, KC, C])
        w_p = sb("w_p", [128, KC, C])
        bias = sb("bias", [1, C])
        ones_row = sb("ones_row", [1, 128])
        ident = sb("ident", [128, 128])
        neg_ident = sb("neg_ident", [128, 128], H16)
        head_mask = sb("head_mask", [128, 6])
        tri = sb("tri", [128, 256], BF)
        stats = sb("stats", [128, T, 6])
        moments = sb("moments", [128, T, 2])
        rstd = sb("rstd", [128, T])
        minus_half = sb("minus_half", [128, T])
        xn = sb("xn", [128, T, C])
        xT = sb("xT", [128, KC, N])
        q_hi = sb("q_hi", [128, NG, N], H16)
        q_lo = sb("q_lo", [128, NG, N], H16)
        k_hi = sb("k_hi", [128, NG, N], H16)
        k_lo = sb("k_lo", [128, NG, N], H16)
        km = sb("km", [128, HEADS, 2, N], H16)
        v = sb("v", [128, T, HEADS, 32])
        maxima = sb("maxima", [128, T, NG, 32], H16)
        probs = sb("probs", [128, 8, 1280])
        av = sb("av", [128, 4, N])
        recip = sb("recip", [128, T, HEADS])
        attn = sb("attn", [128, T, C])
        attnT = sb("attnT", [128, KC, N])
        ps = [ctx.enter_context(nc.psum_tensor(f"bank{i}", [128, 512], F)) for i in range(8)]

        loaded, ids_copied, gathered = sem("loaded"), sem("ids_copied"), sem("gathered")
        consts_dve, consts_pool = sem("consts_dve"), sem("consts_pool")
        embT_made, embT_copied = sem("embT_made"), sem("embT_copied")
        h_made, h_copied = sem("h_made"), sem("h_copied")
        stat_step, moments_made, rstd_step, xn_made = sem("stat_step"), sem("moments_made"), sem("rstd_step"), sem("xn_made")
        xT_made, xT_copied = sem("xT_made"), sem("xT_copied")
        qkv_made, q_hi_made, k_hi_made = sem("qkv_made"), sem("q_hi_made"), sem("k_hi_made")
        q_lo_made, k_lo_made, v_copied, km_made = sem("q_lo_made"), sem("k_lo_made"), sem("v_copied"), sem("km_made")
        max_ready = [sem(f"max_ready{b}") for b in range(3)]
        max_read = [sem(f"max_read{b}") for b in range(3)]
        pool_passed, dve_passed = sem("pool_passed"), sem("dve_passed")
        neg_made, neg_ready, tri_step = sem("neg_made"), sem("neg_ready"), sem("tri_step")
        key_ready = [sem(f"key_ready{b}") for b in range(3)]
        key_read = [sem(f"key_read{b}") for b in range(3)]
        pv_ready, av_copied = sem("pv_ready"), sem("av_copied")
        avT_made, recip_made, attn_made = sem("avT_made"), sem("recip_made"), sem("attn_made")
        attnT_made, attnT_copied = sem("attnT_made"), sem("attnT_copied")
        proj_made, h2_made = sem("proj_made"), sem("h2_made")

        loads = [(ids_all, "ids"), (w_tok, "w_tok"), (w_q, "w_q"), (w_k, "w_k"), (w_v, "w_v"), (w_p, "w_p"),
                 (bias, "bias"), (head_mask, "head_mask"), (ident, "ident")]
        ALL_LOADED = 16 * len(loads)
        block = ctx.enter_context(nc.Block())

        @block.sync
        def _(sp):
            for tile, name in loads:
                sp.dma_start(tile[:], io[name]).then_inc(loaded, 16)
            sp.wait_ge(loaded, ALL_LOADED)

        @block.gpsimd
        def _(pool):
            nc.gpsimd.memset(minus_half[:], -0.5).then_inc(consts_pool, 1)
            nc.gpsimd.memset(v[:], 1.0).then_inc(consts_pool, 1)
            pool.wait_ge(loaded, ALL_LOADED)
            pool.wait_ge(consts_pool, 2)
            pool.wait_ge(consts_dve, 8)
            with pool.Fori(0, B) as i:
                pool.wait_ge(embT_made, SEED + i)
                nc.gpsimd.tensor_copy(ids[:], ids_all[:, bass.ds(i * T, T)]).then_inc(ids_copied, 1)
                pool.wait_ge(ids_copied, i + 1)
                pass_waits(pool, pool_passed)
                for t in range(T):
                    nc.gpsimd.indirect_dma_start(
                        emb[:, t, :], None, io["table"],
                        bass.IndirectOffsetOnAxis(ap=ids[:, t:t + 1], axis=0)).then_inc(gathered, 16)
                pool.wait_ge(moments_made, T * (i + 1))
                pass_waits(pool, pool_passed)
                nc.gpsimd.tensor_scalar(rstd[:], moments[:, :, 1], S.EPS, 1.0, ALU.add, ALU.mult).then_inc(rstd_step, 1)
                pool.wait_ge(rstd_step, 2 * i + 1)
                nc.gpsimd.tensor_tensor(rstd[:], rstd[:], minus_half[:], ALU.pow).then_inc(rstd_step, 1)
                for g, heads in enumerate(S.GROUPS):
                    pool.wait_ge(k_hi_made, NG * i + g + 1)
                    pool.wait_ge(k_lo_made, NG * i + g + 1)
                    pass_waits(pool, pool_passed)
                    for j, h in enumerate(heads):
                        for part, src in enumerate((k_hi, k_lo)):
                            nc.gpsimd.tensor_scalar(km[:, h, part, :], src[:, g, :], head_mask[:, j:j + 1], 1.0,
                                                    ALU.mult, ALU.mult).then_inc(km_made, 1)

        @block.tensor
        def _(pe):
            pe.sem_inc(embT_made, SEED)
            pe.wait_ge(loaded, ALL_LOADED)
            pe.wait_ge(consts_pool, 2)
            pe.wait_ge(consts_dve, 8)
            with pe.Fori(0, B) as i:
                pe.wait_ge(gathered, (i + 1) * (16 * T))
                pe.wait_ge(h2_made, SEED + T * i)
                for t in range(T):
                    last = nc.tensor.transpose(ps[0][:, t * 128:(t + 1) * 128], emb[:, t, :], ident[:])
                last.then_inc(embT_made, 1)
                pe.wait_ge(embT_copied, i + 1)
                for t in range(T):
                    nc.tensor.matmul(ps[1 + t // 2][:, t % 2 * C:t % 2 * C + C], embT[:, t * 128:(t + 1) * 128],
                                     w_tok[:], start=True, stop=True).then_inc(h_made, 1)
                for t in range(T):
                    pe.wait_ge(xn_made, T * i + t + 1)
                    for c in range(KC):
                        last = nc.tensor.transpose(ps[3 + c][:, t * 128:(t + 1) * 128],
                                                   xn[:, t, c * 128:(c + 1) * 128], ident[:])
                last.then_inc(xT_made, 1)
                pe.wait_ge(xT_copied, KC * (i + 1))
                pe.wait_ge(h_copied, 2 * i + 2)
                for w, first_bank in ((w_k, 0), (w_q, 5)):
                    for g in range(NG):
                        for c in range(KC):
                            last = nc.tensor.matmul(ps[first_bank + g][0:GR, :], w[:, c, g * GR:(g + 1) * GR],
                                                    xT[:, c, :], start=c == 0, stop=c == KC - 1)
                        last.then_inc(qkv_made, 1)
                for t in range(T):
                    for c in range(KC):
                        last = nc.tensor.matmul(ps[3 + t // 2][:, t % 2 * C:t % 2 * C + C],
                                                xT[:, c, t * 128:(t + 1) * 128], w_v[:, c, :],
                                                start=c == 0, stop=c == KC - 1)
                    if t % 2:
                        last.then_inc(qkv_made, 1)
                maxed, neg_done = 0, 0
                pe.wait_ge(k_lo_made, NG * (i + 1))
                pe.wait_ge(q_lo_made, NG * (i + 1))
                pe.wait_ge(v_copied, 2 * (i + 1))
                for what, n in order:
                    if what == "max":
                        g, j = group_of[n]
                        pe.wait_ge(km_made, 2 * HEADS * i + 2 * n + 2)
                        for t, b, col, width in MAX_TILES:
                            if col == 0:
                                pe.wait_ge(max_read[b], SEED + HEADS * i + maxed)
                                if b == 0 and neg_done:
                                    pe.wait_ge(neg_ready, NG * i + neg_done)
                            nc.tensor.matmul(ps[b][:, col:col + width], q_hi[0:GR, g, t * 128:(t + 1) * 128],
                                             km[0:GR, n, 0, 0:width], start=True, stop=True)
                            last = nc.tensor.matmul(ps[b][:, col + width - 64:col + width], tri[:, 128:256],
                                                    tri[:, 64:128], start=False, stop=True, skip_group_check=True)
                            if (b, col) in ((0, 0), (1, 384), (2, 0)):
                                last.then_inc(max_ready[b], 1)
                        maxed += 1
                    elif what == "neg":
                        for b in range(3):
                            pe.wait_ge(max_read[b], SEED + HEADS * i + (maxed if b == 0 else S.GROUPS[n][-1] + 1))
                        for t in range(T):
                            last = nc.tensor.matmul(ps[0][GR:128, t * 128:(t + 1) * 128], maxima[:, t, n, :],
                                                    neg_ident[:], start=True, stop=True, skip_group_check=True)
                        last.then_inc(neg_made, 1)
                        neg_done += 1
                    elif what == "key":
                        g, j = group_of[n]
                        if j == 0:
                            pe.wait_ge(neg_ready, NG * i + g + 1)
                        for t, b, col, width in KEY_TILES:
                            if col == 0:
                                pe.wait_ge(key_read[b], SEED + HEADS * i + n)
                            keys = slice(t * 128, (t + 1) * 128)
                            out = ps[3 + b][:, col:col + width]
                            nc.tensor.matmul(out, km[:, n, 0, keys], q_hi[:, g, t * 128:N], start=True, stop=False)
                            nc.tensor.matmul(out, km[:, n, 0, keys], q_lo[:, g, t * 128:N], start=False, stop=False)
                            nc.tensor.matmul(out, km[:, n, 1, keys], q_hi[:, g, t * 128:N], start=False, stop=True)
                            last = nc.tensor.matmul(ps[3 + b][:, col:col + 64], tri[:, 0:128],
                                                    tri[:, 128:192], start=False, stop=True, skip_group_check=True)
                            if (b, col) in ((0, 0), (1, 384), (2, 0)):
                                last.then_inc(key_ready[b], 1)
                    else:
                        for b in range(3):
                            pe.wait_ge(key_read[b], SEED + HEADS * i + 4 * n + 4)
                        if n >= 2:
                            pe.wait_ge(av_copied, 4 * i + n - 1)
                        for at, (t, _, _, width) in enumerate(KEY_TILES):
                            for j in range(4):
                                h = 4 * n + j
                                last = nc.tensor.matmul(ps[6 + n % 2][32 * j:32 * j + 32, t * 128:N], v[:, t, h, :],
                                                        probs[:, h % 8, P_COL[t]:P_COL[t] + width],
                                                        start=at == 0, stop=at == 3, skip_group_check=True)
                        last.then_inc(pv_ready, 1)
                for t in range(T):
                    for q in range(4):
                        pe.wait_ge(av_copied, 4 * i + q + 1)
                        last = nc.tensor.transpose(ps[t][:, q * 128:(q + 1) * 128],
                                                   av[:, q, t * 128:(t + 1) * 128], ident[:])
                    last.then_inc(avT_made, 1)
                for t in range(T):
                    pe.wait_ge(attn_made, T * i + t + 1)
                    for c in range(KC):
                        last = nc.tensor.transpose(ps[4 + c][:, t * 128:(t + 1) * 128],
                                                   attn[:, t, c * 128:(c + 1) * 128], ident[:])
                last.then_inc(attnT_made, 1)
                pe.wait_ge(attnT_copied, KC * (i + 1))
                for t in range(T):
                    out = ps[6 + t // 2][:, t % 2 * C:t % 2 * C + C]
                    for c in range(KC):
                        nc.tensor.matmul(out, attnT[:, c, t * 128:(t + 1) * 128], w_p[:, c, :], start=c == 0, stop=False)
                    nc.tensor.matmul(out, ones_row[:], bias[:], start=False, stop=True).then_inc(proj_made, 1)

        @block.scalar
        def _(act):
            for s in key_read:
                act.sem_inc(s, SEED)
            act.wait_ge(consts_pool, 2)
            with act.Fori(0, B) as i:
                act.wait_ge(embT_made, SEED + i + 1)
                nc.scalar.activation(embT[:], ps[0][:], ACT.Copy).then_inc(embT_copied, 1)
                act.wait_ge(h_made, T * (i + 1))
                nc.scalar.activation(h_all[:, i, 0:2, :], ps[1][:].rearrange("p (t c) -> p t c", t=2), ACT.Copy).then_inc(h_copied, 1)
                nc.scalar.activation(h_all[:, i, 2:4, :], ps[2][:].rearrange("p (t c) -> p t c", t=2), ACT.Copy).then_inc(h_copied, 1)
                act.wait_ge(xT_made, i + 1)
                nc.scalar.activation(xT[:, 0, :], ps[3][:], ACT.Copy).then_inc(xT_copied, 1)
                for src_bank, dst, made, at in ((0, k_hi, k_hi_made, 0), (5, q_hi, q_hi_made, NG)):
                    for g in range(NG):
                        act.wait_ge(qkv_made, (2 * NG + 2) * i + at + g + 1)
                        nc.scalar.activation(dst[0:GR, g, :], ps[src_bank + g][0:GR, :], ACT.Copy).then_inc(made, 1)
                for half in range(2):
                    act.wait_ge(qkv_made, (2 * NG + 2) * i + 2 * NG + half + 1)
                    nc.scalar.activation(v[:, 2 * half:2 * half + 2, :, 0:HD],
                                         ps[3 + half][:].rearrange("p (t h d) -> p t h d", t=2, d=HD),
                                         ACT.Copy).then_inc(v_copied, 1)
                for h in range(HEADS):
                    if h >= 8 and h % 4 == 0:
                        act.wait_ge(pv_ready, 4 * i + h // 4 - 1)
                    for b, col, width in ((0, 0, 512), (1, 512, 512), (2, 1024, 256)):
                        act.wait_ge(key_ready[b], HEADS * i + h + 1)
                        nc.scalar.activation(probs[:, h % 8, col:col + width], ps[3 + b][:, 0:width], ACT.Exp,
                                             scale=SCALE).then_inc(key_read[b], 1)
                    for q in range(4):
                        if h == min(4 * q + 7, HEADS - 1):
                            act.wait_ge(pv_ready, 4 * i + q + 1)
                            nc.scalar.activation(av[:, q, :], ps[6 + q % 2][:], ACT.Copy).then_inc(av_copied, 1)
                act.wait_ge(attnT_made, i + 1)
                nc.scalar.activation(attnT[:, 0, :], ps[4][:], ACT.Copy).then_inc(attnT_copied, 1)
                act.wait_ge(attnT_copied, KC * i + 1)
                nc.scalar.activation(attnT[:, 1, :], ps[5][:], ACT.Copy).then_inc(attnT_copied, 1)

        @block.vector
        def _(dve):
            dve.sem_inc(h2_made, SEED)
            for s in max_read:
                dve.sem_inc(s, SEED)
            nc.vector.memset(ones_row[:], 1.0).then_inc(consts_dve, 1)
            nc.vector.memset(maxima[:], 0.0).then_inc(consts_dve, 1)
            nc.vector.memset(k_hi[GR:128, :, :], 1.0).then_inc(consts_dve, 1)
            nc.vector.memset(k_lo[GR:128, :, :], 0.0).then_inc(consts_dve, 1)
            nc.vector.memset(q_lo[GR:128, :, :], 0.0).then_inc(consts_dve, 1)
            nc.vector.memset(tri[:], 0.0).then_inc(tri_step, 1)
            dve.wait_ge(tri_step, 1)
            nc.vector.memset(tri[0:1, 64:128], 1.0).then_inc(consts_dve, 1)
            nc.vector.memset(tri[0:1, 128:192], -1e30).then_inc(consts_dve, 1)
            dve.wait_ge(loaded, ALL_LOADED)
            nc.vector.tensor_scalar(neg_ident[:], ident[:], -1.0, None, ALU.mult).then_inc(consts_dve, 1)
            dve.wait_ge(consts_pool, 2)
            dve.wait_ge(consts_dve, 8)
            with dve.Fori(0, B) as i:
                for t in range(T):
                    if t == 0:
                        dve.wait_ge(h_copied, 2 * i + 2)
                    nc.vector.bn_stats(stats[:, t, :], h_all[:, i, t, :]).then_inc(stat_step, 1)
                for t in range(T):
                    dve.wait_ge(stat_step, T * i + t + 1)
                    pass_waits(dve, dve_passed)
                    nc.vector.bn_aggr(moments[:, t, :], stats[:, t, :]).then_inc(moments_made, 1)
                dve.wait_ge(rstd_step, 2 * i + 2)
                dve.wait_ge(moments_made, T * (i + 1))
                for t in range(T):
                    nc.vector.tensor_scalar(xn[:, t, :], h_all[:, i, t, :], moments[:, t, 0:1], rstd[:, t:t + 1],
                                            ALU.subtract, ALU.mult).then_inc(xn_made, 1)
                dve.wait_ge(xT_made, i + 1)
                nc.vector.tensor_copy(xT[:, 1, :], ps[4][:]).then_inc(xT_copied, 1)
                for bank, hi, lo, hi_made, lo_made in ((0, k_hi, k_lo, k_hi_made, k_lo_made),
                                                       (5, q_hi, q_lo, q_hi_made, q_lo_made)):
                    for g in range(NG):
                        dve.wait_ge(hi_made, NG * i + g + 1)
                        nc.vector.tensor_tensor(lo[0:GR, g, :], ps[bank + g][0:GR, :], hi[0:GR, g, :],
                                                ALU.subtract).then_inc(lo_made, 1)
                for what, n in order:
                    if what == "max":
                        g, j = group_of[n]
                        for at, (t, b, col, width) in enumerate(MAX_TILES):
                            if col == 0:
                                dve.wait_ge(max_ready[b], HEADS * i + n + 1)
                            last = nc.vector.tensor_reduce(maxima[:, t, g, j:j + 1], ps[b][:, col:col + width],
                                                           AX.X, ALU.max)
                            if (b, col) == (1, 0):
                                continue
                            last.then_inc(max_read[b], 1)
                    elif what == "neg":
                        dve.wait_ge(neg_made, NG * i + n + 1)
                        nc.vector.tensor_copy(q_hi[GR:128, n, :], ps[0][GR:128, :]).then_inc(neg_ready, 1)
                for t in range(T):
                    dve.wait_ge(avT_made, T * i + t + 1)
                    heads = ps[t][:].rearrange("p (h d) -> p h d", d=32)
                    nc.vector.reciprocal(recip[:, t, :], heads[:, :, HD]).then_inc(recip_made, 1)
                for t in range(T):
                    heads = ps[t][:].rearrange("p (h d) -> p h d", d=32)
                    dve.wait_ge(recip_made, T * i + t + 1)
                    nc.vector.tensor_tensor(attn[:, t, :].rearrange("p (h d) -> p h d", d=HD), heads[:, :, 0:HD],
                                            recip[:, t, :].unsqueeze(2).broadcast_to([128, HEADS, HD]),
                                            ALU.mult).then_inc(attn_made, 1)
                for t in range(T):
                    dve.wait_ge(proj_made, T * i + t + 1) if t % 2 else dve.wait_ge(proj_made, T * i + t + 2)
                    nc.vector.tensor_tensor(h_all[:, i, t, :], ps[6 + t // 2][:, t % 2 * C:t % 2 * C + C],
                                            h_all[:, i, t, :], ALU.add).then_inc(h2_made, 1)


def weights_block(nc, io, keep):
    from contextlib import ExitStack
    import concourse.mybir as mybir
    S = sizes()
    F, H16, I16 = mybir.dt.float32, mybir.dt.float16, mybir.dt.int16
    ACT, ALU, AX = mybir.ActivationFunctionType, mybir.AluOpType, mybir.AxisListType
    C, KC, MI = S.C, S.KC, S.MI
    NAMES = ["w_up", "w_gate", "w_down"]
    BLOCKS = MI * C // S.WB
    with ExitStack() as ctx:
        def sb(name, shape, dt=F):
            return ctx.enter_context(nc.sbuf_tensor(name, shape, dt))

        def sem(name):
            return ctx.enter_context(nc.semaphore(name))

        raw = {n: sb(n, [128, MI, C] if n != "w_down" else [128, KC, S.I]) for n in NAMES}
        levels = sb("levels", [128, MI * C], I16)
        amax = sb("amax", [128, BLOCKS])
        scale = sb("scale", [128, BLOCKS])
        inverse = sb("inverse", [128, BLOCKS])
        ident = sb("ident_w", [128, 128])
        ps = [ctx.enter_context(nc.psum_tensor(f"wbank{i}", [128, 512], F)) for i in range(8)]
        loaded, step, quantized = sem("w_loaded"), sem("w_step"), sem("w_quantized")
        turned, hi_made, lo_made = sem("w_turned"), sem("w_hi_made"), sem("w_lo_made")

        jobs = []
        for n in ("w_up", "w_gate"):
            col = 0 if n == "w_up" else S.I
            for c in range(KC):
                for m in range(0, MI, 3):
                    pieces = [raw[n][:, m + k, c * 128:(c + 1) * 128] for k in range(3)]
                    at = slice(col + m * 128, col + (m + 3) * 128)
                    jobs.append((n, pieces, keep["wi_hi"][:, c, at], keep["wi_lo"][:, c, at]))
        for m in range(MI):
            pieces = [raw["w_down"][:, c, m * 128:(m + 1) * 128] for c in range(KC)]
            jobs.append(("w_down", pieces, keep["wo_hi"][:, m, :], keep["wo_lo"][:, m, :]))

        block = ctx.enter_context(nc.Block())

        @block.sync
        def _(sp):
            sp.dma_start(ident[:], io["ident"]).then_inc(loaded, 16)
            for n in NAMES:
                sp.dma_start(raw[n][:], io[n]).then_inc(loaded, 16)
            sp.wait_ge(loaded, 64)

        @block.vector
        def _(dve):
            dve.wait_ge(loaded, 64)
            steps = 0
            for n in NAMES:
                flat = raw[n][:].rearrange("p a b -> p (a b)")
                parts = flat.rearrange("p (s w) -> p s w", w=S.WB)

                def spread(t):
                    return t[:].unsqueeze(2).broadcast_to([128, BLOCKS, S.WB])

                nc.vector.tensor_reduce(amax[:], parts, AX.X, ALU.max, apply_absolute_value=True).then_inc(step, 1)
                dve.wait_ge(step, steps + 1)
                nc.vector.tensor_scalar(scale[:], amax[:], 1.0 / 7.0, 1e-12, ALU.mult, ALU.max).then_inc(step, 1)
                dve.wait_ge(step, steps + 2)
                nc.vector.reciprocal(inverse[:], scale[:]).then_inc(step, 1)
                dve.wait_ge(step, steps + 3)
                nc.vector.tensor_tensor(parts, parts, spread(inverse), ALU.mult).then_inc(step, 1)
                dve.wait_ge(step, steps + 4)
                nc.vector.tensor_scalar(levels[:], flat, 7.0, -8.0, ALU.min, ALU.max).then_inc(step, 1)
                dve.wait_ge(step, steps + 5)
                nc.vector.tensor_tensor(parts, levels[:].rearrange("p (s w) -> p s w", w=S.WB), spread(scale),
                                        ALU.mult).then_inc(step, 1)
                steps += 6
                dve.wait_ge(step, steps)
            nc.vector.engine_nop().then_inc(quantized, 1)
            for k, (_, pieces, hi, lo) in enumerate(jobs):
                width = 128 * len(pieces)
                dve.wait_ge(hi_made, k + 1)
                nc.vector.scalar_tensor_tensor(out=lo, in0=ps[k % 8][:, 0:width], scalar=S.WSCALE, in1=hi,
                                               op0=ALU.mult, op1=ALU.subtract).then_inc(lo_made, 1)

        @block.tensor
        def _(pe):
            pe.wait_ge(quantized, 1)
            for k, (_, pieces, _, _) in enumerate(jobs):
                if k >= 8:
                    pe.wait_ge(lo_made, k - 7)
                for j, piece in enumerate(pieces):
                    last = nc.tensor.transpose(ps[k % 8][:, j * 128:(j + 1) * 128], piece, ident[:])
                last.then_inc(turned, 1)

        @block.scalar
        def _(act):
            for k, (_, pieces, hi, _) in enumerate(jobs):
                act.wait_ge(turned, k + 1)
                nc.scalar.activation(hi, ps[k % 8][:, 0:128 * len(pieces)], ACT.Copy,
                                     scale=S.WSCALE).then_inc(hi_made, 1)


def norm_block(nc, keep):
    from contextlib import ExitStack
    import concourse.mybir as mybir
    S = sizes()
    SEED = S.SEED
    F = mybir.dt.float32
    ALU, AX = mybir.AluOpType, mybir.AxisListType
    B, T, C = S.B, S.T, S.C
    h_all, xn, peak = keep["h_all"], keep["xn"], keep["peak_x"]
    with ExitStack() as ctx:
        def sb(name, shape, dt=F):
            return ctx.enter_context(nc.sbuf_tensor(name, shape, dt))

        def sem(name):
            return ctx.enter_context(nc.semaphore(name))

        stats = sb("n_stats", [128, T, 6])
        batch_moments = sb("n_batch_moments", [128, T, 2])
        moments = sb("n_moments", [128, B, T, 2])
        rstd = sb("n_rstd", [128, B, T])
        minus_half = sb("n_minus_half", [128, B, T])
        const_made, stat_made, aggregated = sem("n_const"), sem("n_stat"), sem("n_aggregated")
        moments_made, rstd_step, passed = sem("n_moments_made"), sem("n_rstd_step"), sem("n_passed")
        xn_made, peak_made, stored = sem("n_xn_made"), sem("n_peak_made"), sem("n_stored")
        block = ctx.enter_context(nc.Block())

        @block.sync
        def _(sp):
            sp.dma_start(keep["h_dram"], h_all[:]).then_inc(stored, 16)
            sp.wait_ge(stored, 16)

        @block.gpsimd
        def _(pool):
            nc.gpsimd.memset(minus_half[:], -0.5).then_inc(const_made, 1)
            pool.wait_ge(const_made, 1)
            pool.wait_ge(moments_made, SEED + B)
            nc.gpsimd.tensor_scalar(rstd[:], moments[:, :, :, 1], S.EPS, 1.0, ALU.add, ALU.mult).then_inc(rstd_step, 1)
            pool.wait_ge(rstd_step, 1)
            nc.gpsimd.tensor_tensor(rstd[:], rstd[:], minus_half[:], ALU.pow).then_inc(rstd_step, 1)

        @block.vector
        def _(dve):
            dve.sem_inc(moments_made, SEED)
            with dve.Fori(0, B) as i:
                for t in range(T):
                    nc.vector.bn_stats(stats[:, t, :], h_all[:, i, t, :]).then_inc(stat_made, 1)
                dve.wait_ge(moments_made, SEED + i)
                dve.wait_ge(stat_made, T * (i + 1))
                pass_waits(dve, passed)
                for t in range(T):
                    nc.vector.bn_aggr(batch_moments[:, t, :], stats[:, t, :]).then_inc(aggregated, 1)
                dve.wait_ge(aggregated, T * (i + 1))
                nc.vector.tensor_copy(moments[:, i, :, :], batch_moments[:]).then_inc(moments_made, 1)
            dve.wait_ge(rstd_step, 2)
            with dve.Fori(0, B) as i:
                for t in range(T):
                    nc.vector.tensor_scalar(xn[:, i, t, :], h_all[:, i, t, :], moments[:, i, t, 0:1], rstd[:, i, t:t + 1],
                                            ALU.subtract, ALU.mult).then_inc(xn_made, 1)
                dve.wait_ge(xn_made, T * (i + 1))
                nc.vector.tensor_reduce(peak[:, i, :], xn[:, i, :, :], AX.XY, ALU.max,
                                        apply_absolute_value=True).then_inc(peak_made, 1)


def global_scale(nc, keep, peaks, unit, name, outputs):
    from contextlib import ExitStack
    import concourse.mybir as mybir
    import concourse.bass as bass
    S = sizes()
    F = mybir.dt.float32
    ALU, AX = mybir.AluOpType, mybir.AxisListType
    scale, ratio = keep["scale_" + name], keep["ratio_" + name]
    with ExitStack() as ctx:
        own = ctx.enter_context(nc.sbuf_tensor(f"own_{name}", [128, 1], F))
        top = ctx.enter_context(nc.sbuf_tensor(f"top_{name}", [128, 1], F))
        inverse = ctx.enter_context(nc.sbuf_tensor(f"inverse_{name}", [128, 1], F))
        step = ctx.enter_context(nc.semaphore(f"step_{name}"))
        reduced = ctx.enter_context(nc.semaphore(f"reduced_{name}"))
        block = ctx.enter_context(nc.Block())

        @block.gpsimd
        def _(pool):
            pool.wait_ge(step, 1)
            nc.gpsimd.partition_all_reduce(top[:], own[:], 128, bass.bass_isa.ReduceOp.max).then_inc(reduced, 1)

        @block.vector
        def _(dve):
            nc.vector.tensor_reduce(own[:], peaks, AX.X, ALU.max).then_inc(step, 1)
            dve.wait_ge(reduced, 1)
            u = 1.0 if unit is None else unit[:, 0:1]
            nc.vector.tensor_scalar(scale[:], top[:], u, 1.0 / S.QMAX, ALU.mult, ALU.mult).then_inc(step, 1)
            dve.wait_ge(step, 2)
            nc.vector.tensor_scalar(scale[:], scale[:], 1e-12, None, ALU.max).then_inc(step, 1)
            dve.wait_ge(step, 3)
            nc.vector.reciprocal(inverse[:], scale[:]).then_inc(step, 1)
            dve.wait_ge(step, 4)
            nc.vector.tensor_scalar(ratio[:], inverse[:], u, None, ALU.mult).then_inc(step, 1)
            for tile, factor, other in outputs:
                o = 1.0 if other is None else other[:, 0:1]
                nc.vector.tensor_scalar(tile[:], scale[:], factor, o, ALU.mult, ALU.mult).then_inc(step, 1)


def turn_block(nc, io, keep):
    from contextlib import ExitStack
    import concourse.mybir as mybir
    S = sizes()
    SEED = S.SEED
    F, I16 = mybir.dt.float32, mybir.dt.int16
    ACT, ALU = mybir.ActivationFunctionType, mybir.AluOpType
    B, T, C, KC, N = S.B, S.T, S.C, S.KC, S.N
    xn, x_hi, x_lo = keep["xn"], keep["x_hi"], keep["x_lo"]
    with ExitStack() as ctx:
        def sb(name, shape, dt=F):
            return ctx.enter_context(nc.sbuf_tensor(name, shape, dt))

        def sem(name):
            return ctx.enter_context(nc.semaphore(name))

        levels = sb("t_levels", [128, 2, T, C], I16)
        whole = sb("t_whole", [128, 2, T, C])
        ident = sb("ident_t", [128, 128])
        ps = [ctx.enter_context(nc.psum_tensor(f"tbank{i}", [128, 512], F)) for i in range(4)]
        loaded, rounded, widened, turned = sem("t_loaded"), sem("t_rounded"), sem("t_widened"), sem("t_turned")
        hi_made, lo_made = sem("t_hi"), sem("t_lo")
        block = ctx.enter_context(nc.Block())

        @block.sync
        def _(sp):
            sp.dma_start(ident[:], io["ident"]).then_inc(loaded, 16)
            sp.wait_ge(loaded, 16)

        @block.scalar
        def _(act):
            act.sem_inc(widened, SEED)
            with act.Fori(0, B // 2) as i:
                for s in range(2):
                    act.wait_ge(rounded, 2 * i + s + 1)
                    act.wait_ge(turned, SEED + 2 * (i * 2))
                    nc.scalar.activation(whole[:, s, :, :], levels[:, s, :, :], ACT.Copy).then_inc(widened, 1)
                for s in range(2):
                    for c in range(KC):
                        act.wait_ge(turned, SEED + 2 * (2 * i + s) + c + 1)
                        nc.scalar.activation(x_hi[:, c, 2 * i + s, :], ps[2 * s + c][:], ACT.Copy).then_inc(hi_made, 1)

        @block.vector
        def _(dve):
            dve.sem_inc(lo_made, SEED)
            with dve.Fori(0, B // 2) as i:
                for s in range(2):
                    dve.wait_ge(widened, SEED + 2 * i)
                    nc.vector.tensor_scalar(levels[:, s, :, :], xn[:, 2 * i + s, :, :], keep["ratio_x"][:, 0:1], None,
                                            ALU.mult).then_inc(rounded, 1)
                for s in range(2):
                    for c in range(KC):
                        dve.wait_ge(hi_made, 2 * (2 * i + s) + c + 1)
                        nc.vector.tensor_tensor(x_lo[:, c, 2 * i + s, :], ps[2 * s + c][:], x_hi[:, c, 2 * i + s, :],
                                                ALU.subtract).then_inc(lo_made, 1)

        @block.tensor
        def _(pe):
            pe.sem_inc(turned, SEED)
            pe.wait_ge(loaded, 16)
            with pe.Fori(0, B // 2) as i:
                for s in range(2):
                    pe.wait_ge(widened, SEED + 2 * i + s + 1)
                    for c in range(KC):
                        pe.wait_ge(lo_made, SEED + 4 * i)
                        for t in range(T):
                            last = nc.tensor.transpose(ps[2 * s + c][:, t * 128:(t + 1) * 128],
                                                       whole[:, s, t, c * 128:(c + 1) * 128], ident[:])
                        last.then_inc(turned, 1)


def inner_products(nc, keep, out, col, i):
    S = sizes()
    x_hi, x_lo, w_hi, w_lo = keep["x_hi"], keep["x_lo"], keep["wi_hi"], keep["wi_lo"]
    pairs = [(c, w, x) for c in range(S.KC) for w, x in ((w_hi, x_hi), (w_hi, x_lo), (w_lo, x_hi))]
    for k, (c, w, x) in enumerate(pairs):
        last = nc.tensor.matmul(out, w[:, c, col:col + 128], x[:, c, i, :], start=k == 0, stop=k == len(pairs) - 1)
    return last


def peak_block(nc, keep):
    from contextlib import ExitStack
    import concourse.mybir as mybir
    S = sizes()
    SEED = S.SEED
    F = mybir.dt.float32
    ALU, AX = mybir.AluOpType, mybir.AxisListType
    with ExitStack() as ctx:
        ps = [ctx.enter_context(nc.psum_tensor(f"kbank{i}", [128, 2, 512], F)) for i in range(4)]
        ready = [ctx.enter_context(nc.semaphore(f"k_ready{i}")) for i in range(3)]
        read = [ctx.enter_context(nc.semaphore(f"k_read{i}")) for i in range(3)]
        block = ctx.enter_context(nc.Block())

        @block.tensor
        def _(pe):
            with pe.Fori(0, S.B) as i:
                for m in range(S.MI):
                    b = m % 3
                    pe.wait_ge(read[b], SEED + 2 * i + m // 3)
                    for half in range(2):
                        last = inner_products(nc, keep, ps[b][:, half, :], half * S.I + m * 128, i)
                    last.then_inc(ready[b], 1)

        @block.vector
        def _(dve):
            for s in read:
                dve.sem_inc(s, SEED)
            with dve.Fori(0, S.B) as i:
                for m in range(S.MI):
                    b = m % 3
                    dve.wait_ge(ready[b], 2 * i + m // 3 + 1)
                    nc.vector.tensor_reduce(keep["peak_ug"][:, i, m, :], ps[b][:, :, :], AX.X, ALU.max,
                                            apply_absolute_value=True).then_inc(read[b], 1)


def gate_block(nc, keep):
    from contextlib import ExitStack
    import concourse.mybir as mybir
    S = sizes()
    SEED = S.SEED
    F, I16 = mybir.dt.float32, mybir.dt.int16
    ACT, ALU, AX = mybir.ActivationFunctionType, mybir.AluOpType, mybir.AxisListType
    PAIRS = S.MI // 2
    gate = keep["gate"]
    with ExitStack() as ctx:
        def sb(name, shape, dt=F):
            return ctx.enter_context(nc.sbuf_tensor(name, shape, dt))

        def sem(name):
            return ctx.enter_context(nc.semaphore(name))

        ps = [ctx.enter_context(nc.psum_tensor(f"gbank{i}", [128, 2, 512], F)) for i in range(3)]
        tanh = sb("g_tanh", [128, PAIRS, 2, 512])
        sig = sb("g_sig", [128, PAIRS, 2, 512], I16)
        ready, levels_made, tanh_made, sig_made, product_made, peak_made = (
            [sem(f"g_{n}{k}") for k in range(PAIRS)]
            for n in ("ready", "levels", "tanh", "sig", "product", "peak"))
        passed = sem("g_passed")
        block = ctx.enter_context(nc.Block())

        @block.tensor
        def _(pe):
            with pe.Fori(0, S.B) as i:
                for k in range(PAIRS):
                    pe.wait_ge(levels_made[k], SEED + i)
                    for half in range(2):
                        last = inner_products(nc, keep, ps[k][:, half, :], S.I + (2 * k + half) * 128, i)
                    last.then_inc(ready[k], 1)

        @block.scalar
        def _(act):
            for s in levels_made:
                act.sem_inc(s, SEED)
            with act.Fori(0, S.B) as i:
                for k in range(PAIRS):
                    act.wait_ge(ready[k], i + 1)
                    nc.scalar.activation(gate[:, i, 2 * k:2 * k + 2, :], ps[k][:, :, :], ACT.Copy,
                                         scale=keep["ratio_gate"][:, 0:1]).then_inc(levels_made[k], 1)
                    act.wait_ge(levels_made[k], SEED + i + 1)
                    act.wait_ge(peak_made[k], SEED + i)
                    pass_waits(act, passed)
                    nc.scalar.activation(tanh[:, k, :, :], gate[:, i, 2 * k:2 * k + 2, :], ACT.Tanh,
                                         scale=keep["half_gate"][:, 0:1]).then_inc(tanh_made[k], 1)

        @block.vector
        def _(dve):
            for s in peak_made:
                dve.sem_inc(s, SEED)
            with dve.Fori(0, S.B) as i:
                for k in range(PAIRS):
                    dve.wait_ge(tanh_made[k], i + 1)
                    nc.vector.tensor_scalar(sig[:, k, :, :], tanh[:, k, :, :], 32768.0, 32767.0, ALU.mult,
                                            ALU.min).then_inc(sig_made[k], 1)
                    dve.wait_ge(sig_made[k], i + 1)
                    nc.vector.scalar_tensor_tensor(out=tanh[:, k, :, :], in0=sig[:, k, :, :], scalar=32768.0,
                                                   in1=gate[:, i, 2 * k:2 * k + 2, :], op0=ALU.add,
                                                   op1=ALU.mult).then_inc(product_made[k], 1)
                    dve.wait_ge(product_made[k], i + 1)
                    nc.vector.tensor_reduce(keep["peak_g2"][:, i, k:k + 1], tanh[:, k, :, :], AX.XY, ALU.max,
                                            apply_absolute_value=True).then_inc(peak_made[k], 1)


def product_block(nc, keep):
    from contextlib import ExitStack
    import concourse.mybir as mybir
    S = sizes()
    SEED = S.SEED
    DMA_SEED = S.DMA_SEED
    F, I16 = mybir.dt.float32, mybir.dt.int16
    ACT, ALU, AX = mybir.ActivationFunctionType, mybir.AluOpType, mybir.AxisListType
    PAIRS = S.MI // 2
    gate = keep["gate"]
    with ExitStack() as ctx:
        def sb(name, shape, dt=F):
            return ctx.enter_context(nc.sbuf_tensor(name, shape, dt))

        def sem(name):
            return ctx.enter_context(nc.semaphore(name))

        ps = [ctx.enter_context(nc.psum_tensor(f"pbank{i}", [128, 2, 512], F)) for i in range(3)]
        up = sb("p_up", [128, PAIRS, 2, 512], I16)
        tanh = sb("p_tanh", [128, PAIRS, 2, 512])
        sig = sb("p_sig", [128, PAIRS, 2, 512], I16)
        gated, levels = tanh, sig
        ready, up_made, tanh_made, sig_made, gated_made, levels_made, product_made, peak_made, stored = (
            [sem(f"p_{n}{k}") for k in range(PAIRS)]
            for n in ("ready", "up", "tanh", "sig", "gated", "levels", "product", "peak", "stored"))
        block = ctx.enter_context(nc.Block())

        @block.tensor
        def _(pe):
            with pe.Fori(0, S.B) as i:
                for k in range(PAIRS):
                    pe.wait_ge(up_made[k], SEED + i)
                    for half in range(2):
                        last = inner_products(nc, keep, ps[k][:, half, :], (2 * k + half) * 128, i)
                    last.then_inc(ready[k], 1)

        @block.scalar
        def _(act):
            for s in up_made:
                act.sem_inc(s, SEED)
            with act.Fori(0, S.B) as i:
                for k in range(PAIRS):
                    act.wait_ge(peak_made[k], SEED + i)
                    act.wait_ge(stored[k], DMA_SEED + 16 * i)
                    nc.scalar.activation(tanh[:, k, :, :], gate[:, i, 2 * k:2 * k + 2, :], ACT.Tanh,
                                         scale=keep["half_gate"][:, 0:1]).then_inc(tanh_made[k], 1)
                    act.wait_ge(ready[k], i + 1)
                    act.wait_ge(product_made[k], SEED + i)
                    nc.scalar.activation(up[:, k, :, :], ps[k][:, :, :], ACT.Copy,
                                         scale=keep["ratio_up"][:, 0:1]).then_inc(up_made[k], 1)

        @block.vector
        def _(dve):
            for s in peak_made:
                dve.sem_inc(s, SEED)
            for s in product_made:
                dve.sem_inc(s, SEED)
            with dve.Fori(0, S.B) as i:
                for k in range(PAIRS):
                    dve.wait_ge(tanh_made[k], i + 1)
                    nc.vector.tensor_scalar(sig[:, k, :, :], tanh[:, k, :, :], 32768.0, 32767.0, ALU.mult,
                                            ALU.min).then_inc(sig_made[k], 1)
                    dve.wait_ge(sig_made[k], i + 1)
                    nc.vector.scalar_tensor_tensor(out=gated[:, k, :, :], in0=sig[:, k, :, :], scalar=32768.0,
                                                   in1=gate[:, i, 2 * k:2 * k + 2, :], op0=ALU.add,
                                                   op1=ALU.mult).then_inc(gated_made[k], 1)
                    dve.wait_ge(gated_made[k], i + 1)
                    nc.vector.tensor_scalar(levels[:, k, :, :], gated[:, k, :, :], keep["ratio_g2"][:, 0:1], None,
                                            ALU.mult).then_inc(levels_made[k], 1)
                    dve.wait_ge(levels_made[k], i + 1)
                    dve.wait_ge(up_made[k], SEED + i + 1)
                    nc.vector.tensor_tensor(gated[:, k, :, :], levels[:, k, :, :], up[:, k, :, :],
                                            ALU.mult).then_inc(product_made[k], 1)
                    dve.wait_ge(product_made[k], SEED + i + 1)
                    nc.vector.tensor_reduce(keep["peak_o"][:, i, k:k + 1], gated[:, k, :, :], AX.XY, ALU.max,
                                            apply_absolute_value=True).then_inc(peak_made[k], 1)

        @block.sync
        def _(sp):
            for s in stored:
                sp.sem_inc(s, DMA_SEED)
            with sp.Fori(0, S.B) as i:
                for k in range(PAIRS):
                    sp.wait_ge(product_made[k], SEED + i + 1)
                    sp.dma_start(keep["o_dram"][:, i, 2 * k:2 * k + 2, :], gated[:, k, :, :]).then_inc(stored[k], 16)
            for k in range(PAIRS):
                sp.wait_ge(stored[k], DMA_SEED + 16 * S.B)


def down_block(nc, keep, out):
    from contextlib import ExitStack
    import concourse.mybir as mybir
    S = sizes()
    SEED = S.SEED
    F, H16, I16 = mybir.dt.float32, mybir.dt.float16, mybir.dt.int16
    ACT, ALU = mybir.ActivationFunctionType, mybir.AluOpType
    B, T, C, MI = S.B, S.T, S.C, S.MI
    out_v = out.rearrange("b (t p) c -> p b t c", p=128)
    with ExitStack() as ctx:
        def sb(name, shape, dt=F):
            return ctx.enter_context(nc.sbuf_tensor(name, shape, dt))

        def sem(name):
            return ctx.enter_context(nc.semaphore(name))

        ps = [[ctx.enter_context(nc.psum_tensor(f"dbank{s}{i}", [128, 2, C], F)) for i in range(2)] for s in range(2)]
        o = sb("d_o", [128, 2, MI, 512])
        h = sb("d_h", [128, 2, T, C])
        levels = sb("d_levels", [128, 2, MI, 512], I16)
        hi = sb("d_hi", [128, 2, MI, 512], H16)
        lo = sb("d_lo", [128, 2, MI, 512], H16)
        y = sb("d_y", [128, 2, T, C])
        loaded, rounded, hi_made, lo_made, ready, summed, stored, y_free = (
            [sem(f"d_{n}{s}") for s in range(2)]
            for n in ("loaded", "rounded", "hi", "lo", "ready", "summed", "stored", "y_free"))
        passed = sem("d_passed")
        block = ctx.enter_context(nc.Block())

        @block.sync
        def _(sp):
            with sp.Fori(0, B // 2) as i:
                for s in range(2):
                    sp.wait_ge(rounded[s], SEED + i)
                    pass_waits(sp, passed)
                    sp.wait_ge(summed[s], SEED + 2 * i)
                    pass_waits(sp, passed)
                    sp.dma_start(o[:, s, :, :], keep["o_dram"][:, 2 * i + s, :, :]).then_inc(loaded[s], 16)
                    sp.dma_start(h[:, s, :, :], keep["h_dram"][:, 2 * i + s, :, :]).then_inc(loaded[s], 16)

        @block.gpsimd
        def _(pool):
            for s in y_free:
                pool.sem_inc(s, SEED)
            with pool.Fori(0, B // 2) as i:
                for s in range(2):
                    pool.wait_ge(summed[s], SEED + 2 * i + 2)
                    pool.dma_start(out_v[:, 2 * i + s, :, :], y[:, s, :, :]).then_inc(stored[s], 16)
                    pool.wait_ge(stored[s], 16 * (i + 1))
                    pool.sem_inc(y_free[s], 1)

        @block.scalar
        def _(act):
            with act.Fori(0, B // 2) as i:
                for s in range(2):
                    act.wait_ge(rounded[s], SEED + i + 1)
                    act.wait_ge(ready[s], SEED + 2 * i)
                    nc.scalar.activation(hi[:, s, :, :], levels[:, s, :, :], ACT.Copy).then_inc(hi_made[s], 1)

        @block.vector
        def _(dve):
            for s in rounded:
                dve.sem_inc(s, SEED)
            for s in summed:
                dve.sem_inc(s, SEED)
            with dve.Fori(0, B // 2) as i:
                for s in range(2):
                    dve.wait_ge(loaded[s], 32 * (i + 1))
                    nc.vector.tensor_scalar(levels[:, s, :, :], o[:, s, :, :], keep["ratio_o"][:, 0:1], None,
                                            ALU.mult).then_inc(rounded[s], 1)
                    dve.wait_ge(hi_made[s], i + 1)
                    nc.vector.tensor_tensor(lo[:, s, :, :], levels[:, s, :, :], hi[:, s, :, :],
                                            ALU.subtract).then_inc(lo_made[s], 1)
                for s in range(2):
                    dve.wait_ge(y_free[s], SEED + i)
                    for half in range(2):
                        dve.wait_ge(ready[s], SEED + 2 * i + half + 1)
                        nc.vector.scalar_tensor_tensor(out=y[:, s, 2 * half:2 * half + 2, :], in0=ps[s][half][:, :, :],
                                                       scalar=keep["out_unit"][:, 0:1],
                                                       in1=h[:, s, 2 * half:2 * half + 2, :], op0=ALU.mult,
                                                       op1=ALU.add).then_inc(summed[s], 1)

        @block.tensor
        def _(pe):
            for s in ready:
                pe.sem_inc(s, SEED)
            with pe.Fori(0, B // 2) as i:
                for s in range(2):
                    pe.wait_ge(hi_made[s], i + 1)
                    pe.wait_ge(lo_made[s], i + 1)
                    pe.wait_ge(summed[s], SEED + 2 * i)
                    for t in range(T):
                        tok = slice(t * 128, (t + 1) * 128)
                        pairs = [(m, a, w) for m in range(MI) for a, w in
                                 ((hi, keep["wo_hi"]), (lo, keep["wo_hi"]), (hi, keep["wo_lo"]))]
                        for k, (m, a, w) in enumerate(pairs):
                            last = nc.tensor.matmul(ps[s][t // 2][:, t % 2, :], a[:, s, m, tok], w[:, m, :],
                                                    start=k == 0, stop=k == len(pairs) - 1)
                        if t % 2:
                            last.then_inc(ready[s], 1)


def ffn(nc, io, keep, out):
    from contextlib import ExitStack
    import concourse.mybir as mybir
    S = sizes()
    F, H16, I16 = mybir.dt.float32, mybir.dt.float16, mybir.dt.int16
    B, T, C, KC, MI, N = S.B, S.T, S.C, S.KC, S.MI, S.N
    keep["h_dram"] = nc.dram_tensor("h_stream", (128, B, T, C), F, kind="Internal").ap()
    keep["o_dram"] = nc.dram_tensor("products", (128, B, MI, N), F, kind="Internal").ap()
    with ExitStack() as ctx:
        def sb(name, shape, dt=F):
            keep[name] = ctx.enter_context(nc.sbuf_tensor(name, shape, dt))
            return keep[name]

        for name in ("x", "up", "gate", "g2", "o"):
            sb("scale_" + name, [128, 1])
            sb("ratio_" + name, [128, 1])
        for name in ("unit_x", "half_gate", "unit_g2", "unit_o", "out_unit"):
            sb(name, [128, 1])
        sb("peak_x", [128, B, 1])
        sb("peak_ug", [128, B, MI, 2])
        sb("peak_g2", [128, B, MI // 2])
        sb("peak_o", [128, B, MI // 2])
        sb("wi_hi", [128, KC, 2 * S.I], H16)
        sb("wi_lo", [128, KC, 2 * S.I], H16)
        sb("wo_hi", [128, MI, C], H16)
        sb("wo_lo", [128, MI, C], H16)
        weights_block(nc, io, keep)
        with nc.sbuf_tensor("xn_all", [128, B, T, C], F) as xn:
            keep["xn"] = xn
            norm_block(nc, keep)
            global_scale(nc, keep, keep["peak_x"][:, :, 0], None, "x", [(keep["unit_x"], 1.0 / S.WSCALE, None)])
            halves = keep["h_all"][:].rearrange("p b t c -> p (b t c)").bitcast(H16).rearrange(
                "p (k b n) -> p k b n", k=2 * KC, b=B)
            keep["x_hi"], keep["x_lo"] = halves[:, 0:KC], halves[:, KC:2 * KC]
            turn_block(nc, io, keep)
        with nc.sbuf_tensor("gate_levels", [128, B, MI, N], I16) as gate:
            keep["gate"] = gate
            peak_block(nc, keep)
            peaks = keep["peak_ug"]
            global_scale(nc, keep, peaks[:, :, :, 0].rearrange("p b m -> p (b m)"), keep["unit_x"], "up", [])
            global_scale(nc, keep, peaks[:, :, :, 1].rearrange("p b m -> p (b m)"), keep["unit_x"], "gate",
                         [(keep["half_gate"], 0.5, None), (keep["unit_g2"], 1.0 / 65536.0, None)])
            gate_block(nc, keep)
            global_scale(nc, keep, keep["peak_g2"][:].rearrange("p b m -> p (b m)"), keep["unit_g2"], "g2",
                         [(keep["unit_o"], 1.0, keep["scale_up"])])
            product_block(nc, keep)
        global_scale(nc, keep, keep["peak_o"][:].rearrange("p b m -> p (b m)"), keep["unit_o"], "o",
                     [(keep["out_unit"], 1.0 / S.WSCALE, None)])
        down_block(nc, keep, out)


def build(nc, io, out):
    import concourse.mybir as mybir
    S = sizes()
    F = mybir.dt.float32
    with nc.sbuf_tensor("h_all", [128, S.B, S.T, S.C], F) as h_all:
        keep = {"h_all": h_all}
        attention_block(nc, io, keep)
        ffn(nc, io, keep, out)


def kernel(x, L0_tok_embeddings, L0_tok_project_kernel, L0_attn_w_qkv, L0_attn_w_proj, L0_attn_b_proj,
           L0_ffn_w_gate, L0_ffn_w_up, L0_ffn_w_down):
    import numpy as np
    import concourse.bacc as bacc
    from concourse import mybir
    from concourse.bass_utils import run_bass_kernel_spmd

    S = sizes()

    def rows_to_partitions(a):
        return np.ascontiguousarray(a.reshape(-1, 128, a.shape[1]).transpose(1, 0, 2))

    def head_columns(w):
        cols = np.zeros((S.C, len(S.GROUPS) * S.GROWS), np.float32)
        for g, heads in enumerate(S.GROUPS):
            part = w[heads[0] * S.HD:(heads[-1] + 1) * S.HD].T
            cols[:, g * S.GROWS:g * S.GROWS + part.shape[1]] = part
        return rows_to_partitions(cols)

    w_qkv = np.asarray(L0_attn_w_qkv)
    head_mask = np.zeros((128, 6), np.float32)
    for j in range(6):
        head_mask[j * S.HD:(j + 1) * S.HD, j] = 1.0
        head_mask[S.GROWS + j, j] = 1.0
    arrays = {
        "ids": np.ascontiguousarray(np.asarray(x).reshape(S.B * S.T, 128).T),
        "table": np.asarray(L0_tok_embeddings),
        "w_tok": np.asarray(L0_tok_project_kernel),
        "w_q": head_columns(w_qkv[0:S.C]),
        "w_k": head_columns(w_qkv[S.C:2 * S.C]),
        "w_v": rows_to_partitions(w_qkv[2 * S.C:].T),
        "w_p": rows_to_partitions(np.asarray(L0_attn_w_proj).T),
        "bias": np.asarray(L0_attn_b_proj).reshape(1, S.C),
        "head_mask": head_mask,
        "ident": np.eye(128, dtype=np.float32),
        "w_up": rows_to_partitions(np.asarray(L0_ffn_w_up)),
        "w_gate": rows_to_partitions(np.asarray(L0_ffn_w_gate)),
        "w_down": rows_to_partitions(np.asarray(L0_ffn_w_down)),
    }
    nc = bacc.Bacc("TRN2", target_bir_lowering=False, num_devices=1)
    io = {n: nc.dram_tensor(f"in_{n}", a.shape, mybir.dt.from_np(a.dtype), kind="ExternalInput").ap()
          for n, a in arrays.items()}
    out = nc.dram_tensor("out", (S.B, S.N, S.C), mybir.dt.float32, kind="ExternalOutput").ap()
    build(nc, io, out)
    r = run_bass_kernel_spmd(nc, [{f"in_{n}": a for n, a in arrays.items()}], core_ids=[0])
    return r.results[0]["out"]
```

```python
class Sizes:
    B, N, HID, C, HEADS, HD, I = 16, 512, 128, 256, 16, 16, 768
    WB = 32


def sizes():
    s = Sizes()
    s.T = s.N // 128
    s.KC = s.C // 128
    s.MI = s.I // 128
    s.BLOCK = 64
    s.EPS = 1e-5
    s.QMAX = 32767.0
    s.SEED, s.DMA_SEED = 1, 16
    s.WSCALE = 1024.0
    return s


def pass_waits(eng, passed):
    eng.sem_inc(passed, 1)


def wait_past(eng, sem, n):
    if isinstance(n, int) and n <= 0:
        return
    eng.wait_ge(sem, n)


def attention_block(nc, io, keep):
    from contextlib import ExitStack
    import concourse.bass as bass
    import concourse.mybir as mybir
    S = sizes()
    F, H16, BF, I32 = mybir.dt.float32, mybir.dt.float16, mybir.dt.bfloat16, mybir.dt.int32
    ACT, ALU, AX = mybir.ActivationFunctionType, mybir.AluOpType, mybir.AxisListType
    B, N, T, C, KC, HEADS, HD = S.B, S.N, S.T, S.C, S.KC, S.HEADS, S.HD
    SCALE = HD ** -0.5
    PAIRS = HEADS // 2
    MROW = 96
    MASK_END = MROW + T
    Q_PARTS, K_PARTS = (0, 1, 0), (0, 0, 1)

    MAX_TILES = [(3, 0, 0, 512), (2, 1, 0, 384), (0, 1, 384, 128), (1, 2, 0, 256)]
    KEY_TILES = [(0, 0, 0, 512), (1, 1, 0, 384), (3, 1, 384, 128), (2, 2, 0, 256)]
    P_COL = {0: 0, 1: 512, 3: 896, 2: 1024}

    NEG_LAG, KEY_LAG = 8, 11
    PIECES = {"embed": [0], "project": [2, 3, 4, 5], "pv_last": [3, 4, 5, 6], "turn": [9, 10, 11, 12],
              "norm": [13, 14, 15, 16], "rows": [15, 16], "columns": [17, 18], "out": [19, 20, 21, 22],
              "kq": list(range(24, 40, 2)), "v": [40, 42, 44, 46],
              "pv": [25, 27, 29, 31] + [37, 39, 41, 43] + [49, 51, 53, 55]}
    PARTS = 3 * HEADS
    ORDER = []
    for slot in range(PARTS + KEY_LAG):
        ORDER += [(what, n) for what, at in PIECES.items() for n, s in enumerate(at) if s == slot]
        if slot >= NEG_LAG and (slot - NEG_LAG) % 6 == 0 and (slot - NEG_LAG) // 6 < PAIRS:
            ORDER.append(("neg", (slot - NEG_LAG) // 6))
        if slot >= KEY_LAG:
            ORDER.append(("key", slot - KEY_LAG))
        if slot < PARTS:
            ORDER.append(("max", slot))
    NEXT = ("embed", "project", "norm", "columns", "kq", "v")
    BEFORE = ("pv_last", "turn", "rows", "out")

    def steps(scores, next_batch, batch_before):
        return [(w, n) for w, n in ORDER
                if (next_batch if w in NEXT else batch_before if w in BEFORE else scores)]

    def turns(engine, turn):
        lead, first, full = steps(False, True, False), steps(True, True, False), steps(True, True, True)
        last, end = steps(True, False, True), steps(False, False, True)
        turn(-1, lead, [], 1)
        turn(0, first, lead, 0)
        with engine.Fori(0, (B - 2) // 2) as j:
            turn(2 * j + 1, full, first, 1)
            turn(2 * j + 2, full, full, 0)
        turn(B - 1, last, full, 1)
        turn(B, end, last, 0)

    RING = [(w, n) for w, n in ORDER if w in ("max", "neg")]
    assert len(RING) % 2 == 0

    def scores_before(at, b):
        return sum(w == "max" for w, _ in RING[b:at:2])

    PER_BATCH = [scores_before(len(RING), b) for b in range(2)]

    with ExitStack() as ctx:
        def sb(name, shape, dt=F):
            return ctx.enter_context(nc.sbuf_tensor(name, shape, dt))

        def sem(name):
            return ctx.enter_context(nc.semaphore(name))

        ids_all = sb("ids_all", [128, B * T], I32)
        ids = sb("ids", [128, T], I32)
        emb = sb("emb", [128, T, S.HID])
        embT = sb("embT", [128, N])
        w_tok = sb("w_tok", [128, C])
        w_q = sb("w_q", [128, KC, C])
        w_k = sb("w_k", [128, KC, C])
        w_v = sb("w_v", [128, KC, C])
        w_p = sb("w_p", [128, KC, C])
        bias = sb("bias", [1, C])
        ones_row = sb("ones_row", [1, 128])
        ident = sb("ident", [128, 128])
        neg_ident = sb("neg_ident", [128, 128], H16)
        tail = sb("tail", [128, 3, N], H16)
        early = sb("early", [128, T, T], H16)
        h_new = sb("h_new", [128, T, C])
        h = sb("h", [128, 2, T, C])
        h2 = sb("h2", [128, T, C])
        stats = sb("stats", [128, T, 6])
        moments = sb("moments", [128, T, 2])
        rstd = sb("rstd", [128, T])
        minus_half = sb("minus_half", [128, T])
        xn = sb("xn", [128, T, C])
        xT = sb("xT", [128, KC, N])
        split = sb("split", [128, 2, 2, 2, N], H16)
        q_rows = sb("q_rows", [128, 2, PAIRS, N], H16)
        k_rows = sb("k_rows", [128, 2, HEADS, N], H16)
        v = sb("v", [128, 2, T, HEADS, 32])
        maxima = sb("maxima", [128, T, PAIRS, 32], H16)
        probs = sb("probs", [128, 8, 1280])
        av = sb("av", [128, 4, N])
        recip = sb("recip", [128, T, HEADS])
        attn = sb("attn", [128, T, C])
        attnT = sb("attnT", [128, KC, N])
        split_dram = nc.dram_tensor("split_dram", (2, 2, 128, 2, N), H16, kind="Internal").ap()
        max_bank = [ctx.enter_context(nc.psum_tensor(f"max{i}", [128, 512], F)) for i in range(2)]
        key_bank = [ctx.enter_context(nc.psum_tensor(f"key{i}", [128, 512], F)) for i in range(2)]
        pv_bank = ctx.enter_context(nc.psum_tensor("pv", [128, 512], F))
        bank = [ctx.enter_context(nc.psum_tensor(f"bank{i}", [128, 512], F)) for i in range(3)]

        loaded, ids_copied, gathered = sem("loaded"), sem("ids_copied"), sem("gathered")
        consts_dve, consts_pool, zeroed = sem("consts_dve"), sem("consts_pool"), sem("zeroed")
        embT_made, embT_copied = sem("embT_made"), sem("embT_copied")
        h_made, h_copied = sem("h_made"), sem("h_copied")
        stat_step, moments_made, rstd_step, xn_made = sem("stat_step"), sem("moments_made"), sem("rstd_step"), sem("xn_made")
        xT_made, xT_copied = sem("xT_made"), [sem("xT_copied0"), sem("xT_copied1")]
        kq_made, hi_made, lo_made = sem("kq_made"), sem("hi_made"), sem("lo_made")
        split_stored, k_loaded = sem("split_stored"), sem("k_loaded")
        v_made, v_copied = sem("v_made"), sem("v_copied")
        max_ready, max_read = [sem(f"max_ready{b}") for b in range(2)], [sem(f"max_read{b}") for b in range(2)]
        neg_made, neg_ready = sem("neg_made"), sem("neg_ready")
        key_ready, key_read = [sem(f"key_ready{b}") for b in range(2)], [sem(f"key_read{b}") for b in range(2)]
        pv_ready, av_copied = sem("pv_ready"), sem("av_copied")
        avT_made, recip_made, attn_made = sem("avT_made"), sem("recip_made"), sem("attn_made")
        attnT_made, attnT_copied = sem("attnT_made"), sem("attnT_copied")
        proj_made, h2_made, h2_stored = sem("proj_made"), sem("h2_made"), sem("h2_stored")
        h_kept = sem("h_kept")
        pool_passed, dve_passed = sem("pool_passed"), sem("dve_passed")

        READERS = {"embed": (1, 1, embT_copied, 1), "turn": (1, -1, attn_made, 1), "rows": (1, -1, attnT_copied, 1),
                   "out": (2, -1, h2_made, 2), "project": (2, 1, h_copied, 1), "columns": (1, 1, None, 1),
                   "kq": (2, 1, lo_made, 1), "v": (2, 1, v_copied, 1)}
        USES = []
        for what, n in ORDER:
            pieces, of, sem_read, counts = READERS.get(what, (1, 0, None, 0))
            if counts and n % pieces == 0:
                per_batch = len(PIECES[what]) // pieces * counts
                if what == "columns":
                    USES.append((what, of, xT_copied[n], 1, 1))
                else:
                    USES.append((what, of, sem_read, per_batch, (n // pieces + 1) * counts))
        FIRST_USE = {name: [u[0] for u in USES].index(name) for name, *_ in USES}
        assert all(USES[FIRST_USE[u[0]]:][k][0] == u[0] for u in USES
                   for k in range(sum(w[0] == u[0] for w in USES)))

        def bank_of(name, k):
            return bank[(FIRST_USE[name] + k) % 3]

        def take_bank(pe, i, todo, previous, name, k):
            at = FIRST_USE[name] + k
            here = [u for u in range(at) if u % 3 == at % 3 and USES[u][0] in [w for w, _ in todo]]
            there = [u for u in range(len(USES)) if u % 3 == at % 3 and USES[u][0] in [w for w, _ in previous]]
            if here:
                _, of, sem_read, per_batch, count = USES[here[-1]]
                pe.wait_ge(sem_read, per_batch * (i + of) + count)
            elif there:
                _, of, sem_read, per_batch, count = USES[there[-1]]
                pe.wait_ge(sem_read, per_batch * (i - 1 + of) + count)
            return bank[at % 3]

        loads = [(ids_all[:], "ids"), (w_tok[:], "w_tok"), (w_q[:], "w_q"), (w_k[:], "w_k"), (w_v[:], "w_v"),
                 (w_p[:], "w_p"), (bias[:], "bias"), (ident[:], "ident"), (tail[MROW:128], "tail"), (early[:], "early")]
        ALL_LOADED = 16 * len(loads)
        CONSTS = 7
        ROW_LOADS = 12
        block = ctx.enter_context(nc.Block())

        def take_ring(pe, i, at):
            before, turn_of = (at - 2, i) if at >= 2 else (at - 2 + len(RING), i - 1)
            what, n = RING[before]
            if what == "neg":
                wait_past(pe, neg_ready, PAIRS * turn_of + n + 1)
            else:
                wait_past(pe, max_read[at % 2], PER_BATCH[at % 2] * turn_of + scores_before(before + 1, at % 2))
            return max_bank[at % 2]

        @block.sync
        def _(sp):
            for tile, name in loads:
                sp.dma_start(tile, io[name]).then_inc(loaded, 16)
            sp.wait_ge(loaded, ALL_LOADED)
            sp.wait_ge(zeroed, 2)
            sp.wait_ge(consts_dve, CONSTS)

            def turn(i, todo, previous, parity):
                for what, n in todo:
                    if what == "out" and n == T - 1:
                        sp.wait_ge(h2_made, T * i)
                        sp.dma_start(keep["h_dram"][:, bass.ds(i - 1, 1), :, :].rearrange("p b t c -> p (b t c)"),
                                     h2[:].rearrange("p t c -> p (t c)")).then_inc(h2_stored, 16)
                    elif what == "kq" and n in (3, 7):
                        w = n // 4
                        sp.wait_ge(lo_made, 4 * (i + 1) + n // 2 + 1)
                        for part in range(2):
                            sp.dma_start(split_dram[w, part], split[:, w, part, :, :]).then_inc(split_stored, 16)
                        sp.wait_ge(split_stored, 64 * (i + 1) + 32 * (w + 1))
                        for e in range(2):
                            for slot in range(3):
                                rows = slice(48 * e + 16 * slot, 48 * e + 16 * slot + HD)
                                part = (K_PARTS, Q_PARTS)[w][slot]
                                src = split_dram[w, part].rearrange("(j e d) g n -> e d g j n", e=2, d=HD)[e]
                                if w == 0:
                                    dst = k_rows[rows, 1 - parity, :, :].rearrange("d (g j e) n -> d g j e n", g=2, e=2)[:, :, :, e, :]
                                else:
                                    dst = q_rows[rows, 1 - parity, :, :].rearrange("d (g j) n -> d g j n", g=2)
                                sp.dma_start(dst, src).then_inc(k_loaded, 16)

            turns(sp, turn)
            sp.wait_ge(h2_stored, S.DMA_SEED + 16 * B)

        @block.gpsimd
        def _(pool):
            nc.gpsimd.memset(minus_half[:], -0.5).then_inc(consts_pool, 1)
            nc.gpsimd.memset(v[:], 1.0).then_inc(consts_pool, 1)
            nc.gpsimd.memset(k_rows[:].rearrange("p a h n -> p (a h n)").bitcast(F), 0.0).then_inc(zeroed, 1)
            nc.gpsimd.memset(q_rows[:].rearrange("p a h n -> p (a h n)").bitcast(F), 0.0).then_inc(zeroed, 1)
            pool.wait_ge(loaded, ALL_LOADED)
            pool.wait_ge(consts_pool, 2)

            def gather_and_scale(b, parity):
                wait_past(pool, embT_made, b)
                nc.gpsimd.tensor_copy(ids[:], ids_all[:, bass.ds(b * T, T)]).then_inc(ids_copied, 1)
                pool.wait_ge(ids_copied, b + 1)
                pass_waits(pool, pool_passed)
                for t in range(T):
                    nc.gpsimd.indirect_dma_start(
                        emb[:, t, :], None, io["table"],
                        bass.IndirectOffsetOnAxis(ap=ids[:, t:t + 1], axis=0)).then_inc(gathered, 16)
                pool.wait_ge(moments_made, T * (b + 1))
                pass_waits(pool, pool_passed)
                nc.gpsimd.tensor_scalar(rstd[:], moments[:, :, 1], S.EPS, 1.0, ALU.add, ALU.mult).then_inc(rstd_step, 1)
                pool.wait_ge(rstd_step, 2 * b + 1)
                nc.gpsimd.tensor_tensor(rstd[:], rstd[:], minus_half[:], ALU.pow).then_inc(rstd_step, 1)

                pool.wait_ge(h_copied, 2 * (b + 1))
                wait_past(pool, h2_made, T * (b - 1))
                pass_waits(pool, pool_passed)
                nc.gpsimd.tensor_copy(h[:, parity, :, :], h_new[:]).then_inc(h_kept, 1)

            gather_and_scale(0, 0)
            gather_and_scale(1, 1)
            with pool.Fori(0, (B - 2) // 2) as j:
                gather_and_scale(2 * j + 2, 0)
                gather_and_scale(2 * j + 3, 1)

        @block.tensor
        def _(pe):
            pe.wait_ge(loaded, ALL_LOADED)
            pe.wait_ge(consts_pool, 2)
            pe.wait_ge(consts_dve, CONSTS)
            pe.wait_ge(zeroed, 2)

            def turn(i, todo, previous, parity):
                for what, n in todo:
                    if what == "embed":
                        pe.wait_ge(gathered, 16 * T * (i + 2))
                        ps = take_bank(pe, i, todo, previous, what, 0)
                        for t in range(T):
                            last = nc.tensor.transpose(ps[:, t * 128:(t + 1) * 128], emb[:, t, :], ident[:])
                        last.then_inc(embT_made, 1)
                    elif what == "project":
                        pe.wait_ge(embT_copied, i + 2)
                        if n % 2 == 0:
                            take_bank(pe, i, todo, previous, what, n // 2)
                        last = nc.tensor.matmul(bank_of(what, n // 2)[:, n % 2 * C:n % 2 * C + C],
                                                embT[:, n * 128:(n + 1) * 128], w_tok[:], start=True, stop=True)
                        if n % 2:
                            last.then_inc(h_made, 1)
                    elif what == "columns":
                        pe.wait_ge(xn_made, T * (i + 2))
                        ps = take_bank(pe, i, todo, previous, what, n)
                        for t in range(T):
                            last = nc.tensor.transpose(ps[:, t * 128:(t + 1) * 128],
                                                       xn[:, t, n * 128:(n + 1) * 128], ident[:])
                        last.then_inc(xT_made, 1)
                    elif what == "kq":
                        c, w, half = n % 2, (w_k, w_q)[n // 4], n // 2 % 2
                        pe.wait_ge(xT_copied[c], i + 2)
                        if c == 0:
                            take_bank(pe, i, todo, previous, what, n // 2)
                        last = nc.tensor.matmul(bank_of(what, n // 2)[:], w[:, c, half * 128:(half + 1) * 128],
                                                xT[:, c, :], start=c == 0, stop=c == KC - 1)
                        if c == KC - 1:
                            last.then_inc(kq_made, 1)
                    elif what == "v":
                        if n % 2 == 0:
                            take_bank(pe, i, todo, previous, what, n // 2)
                        for c in range(KC):
                            last = nc.tensor.matmul(bank_of(what, n // 2)[:, n % 2 * C:n % 2 * C + C],
                                                    xT[:, c, n * 128:(n + 1) * 128],
                                                    w_v[:, c, :], start=c == 0, stop=c == KC - 1)
                        if n % 2:
                            last.then_inc(v_made, 1)
                    elif what == "max":
                        if n == 0:
                            pe.wait_ge(k_loaded, 16 * ROW_LOADS * (i + 1))
                        head, rows = n // 3, slice(0, MASK_END)
                        at = RING.index((what, n))
                        ps = take_ring(pe, i, at)
                        for t, part, col, width in MAX_TILES:
                            if part == n % 3:
                                last = nc.tensor.matmul(ps[:, col:col + width],
                                                        q_rows[rows, parity, head // 2, t * 128:(t + 1) * 128],
                                                        k_rows[rows, parity, head, 0:width], start=True, stop=True)
                        last.then_inc(max_ready[at % 2], 1)
                    elif what == "neg":
                        for b in range(2):
                            pe.wait_ge(max_read[b], PER_BATCH[b] * i
                                       + scores_before(RING.index(("max", 6 * n + 5)) + 1, b))
                        ps = take_ring(pe, i, RING.index(("neg", n)))
                        for t in range(T):
                            last = nc.tensor.matmul(ps[MROW:128, t * 128:(t + 1) * 128], maxima[:, t, n, :],
                                                    neg_ident[:], start=True, stop=True, skip_group_check=True)
                        last.then_inc(neg_made, 1)
                    elif what == "key":
                        head = n // 3
                        pe.wait_ge(neg_ready, PAIRS * i + head // 2 + 1)
                        wait_past(pe, key_read[n % 2], 24 * i + n // 2)
                        for t, part, col, width in KEY_TILES:
                            if part == n % 3:
                                last = nc.tensor.matmul(key_bank[n % 2][:, col:col + width],
                                                        k_rows[:, parity, head, t * 128:(t + 1) * 128],
                                                        q_rows[:, parity, head // 2, t * 128:N], start=True, stop=True)
                        last.then_inc(key_ready[n % 2], 1)
                    elif what in ("pv", "pv_last"):
                        of, quad, at = (i, n // 4, n % 4) if what == "pv" else (i - 1, 3, n)
                        if at == 0:
                            pe.wait_ge(v_copied, 2 * (of + 1))
                            for b in range(2):
                                pe.wait_ge(key_read[b], 24 * of + 6 * (quad + 1))
                            wait_past(pe, av_copied, 4 * of + quad)
                        t, _, _, width = KEY_TILES[at]
                        for j in range(4):
                            head = 4 * quad + j
                            last = nc.tensor.matmul(pv_bank[32 * j:32 * j + 32, t * 128:N],
                                                    v[:, parity if what == "pv" else 1 - parity, t, head, :],
                                                    probs[:, head % 8, P_COL[t]:P_COL[t] + width],
                                                    start=at == 0, stop=at == 3, skip_group_check=True)
                        if at == 3:
                            last.then_inc(pv_ready, 1)
                    elif what == "turn":
                        pe.wait_ge(av_copied, 4 * i)
                        ps = take_bank(pe, i, todo, previous, what, n)
                        for q in range(4):
                            last = nc.tensor.transpose(ps[:, q * 128:(q + 1) * 128],
                                                       av[:, q, n * 128:(n + 1) * 128], ident[:])
                        last.then_inc(avT_made, 1)
                    elif what == "rows":
                        pe.wait_ge(attn_made, T * i)
                        ps = take_bank(pe, i, todo, previous, what, n)
                        for t in range(T):
                            last = nc.tensor.transpose(ps[:, t * 128:(t + 1) * 128],
                                                       attn[:, t, n * 128:(n + 1) * 128], ident[:])
                        last.then_inc(attnT_made, 1)
                    elif what == "out":
                        pe.wait_ge(attnT_copied, KC * i)
                        if n % 2 == 0:
                            take_bank(pe, i, todo, previous, what, n // 2)
                        out = bank_of(what, n // 2)[:, n % 2 * C:n % 2 * C + C]
                        for c in range(KC):
                            nc.tensor.matmul(out, attnT[:, c, n * 128:(n + 1) * 128], w_p[:, c, :],
                                             start=c == 0, stop=False)
                        last = nc.tensor.matmul(out, ones_row[:], bias[:], start=False, stop=True)
                        if n % 2:
                            last.then_inc(proj_made, 1)

            turns(pe, turn)

        @block.scalar
        def _(act):
            act.wait_ge(consts_pool, 2)
            act.wait_ge(zeroed, 2)

            def turn(i, todo, previous, parity):
                for what, n in todo:
                    if what == "embed":
                        act.wait_ge(embT_made, i + 2)
                        nc.scalar.activation(embT[:], bank_of(what, 0)[:], ACT.Copy).then_inc(embT_copied, 1)
                    elif what == "project":
                        half = n // 2
                        if n == 1:
                            wait_past(act, h_kept, i + 1)
                        if n % 2:
                            act.wait_ge(h_made, 2 * (i + 1) + half + 1)
                            nc.scalar.activation(h_new[:, 2 * half:2 * half + 2, :],
                                                 bank_of(what, half)[:].rearrange("p (t c) -> p t c", t=2),
                                                 ACT.Copy).then_inc(h_copied, 1)
                    elif what == "columns":
                        if n == 0:
                            act.wait_ge(xT_made, KC * (i + 1) + 1)
                            nc.scalar.activation(xT[:, 0, :], bank_of(what, 0)[:], ACT.Copy).then_inc(xT_copied[0], 1)
                    elif what == "kq":
                        if n % 2:
                            k = n // 2
                            act.wait_ge(kq_made, 4 * (i + 1) + k + 1)
                            if k == 0:
                                wait_past(act, split_stored, 64 * (i + 1))
                            nc.scalar.activation(split[:, k // 2, 0, k % 2, :], bank_of(what, k)[:],
                                                 ACT.Copy).then_inc(hi_made, 1)
                    elif what == "v":
                        if n % 2:
                            half = n // 2
                            act.wait_ge(v_made, 2 * (i + 1) + half + 1)
                            nc.scalar.activation(v[:, 1 - parity, 2 * half:2 * half + 2, :, 0:HD],
                                                 bank_of(what, half)[:].rearrange("p (t h d) -> p t h d", t=2, d=HD),
                                                 ACT.Copy).then_inc(v_copied, 1)
                    elif what == "neg":
                        act.wait_ge(neg_made, PAIRS * i + n + 1)
                        nc.scalar.activation(q_rows[MROW:128, parity, n, :], max_bank[RING.index(("neg", n)) % 2][MROW:128, :],
                                             ACT.Copy).then_inc(neg_ready, 1)
                    elif what == "key":
                        head, part = n // 3, n % 3
                        width = (512, 512, 256)[part]
                        if n % 12 == 0:
                            wait_past(act, pv_ready, 4 * i + n // 12 - 1)
                        act.wait_ge(key_ready[n % 2], 24 * i + n // 2 + 1)
                        nc.scalar.activation(probs[:, head % 8, 512 * part:512 * part + width],
                                             key_bank[n % 2][:, 0:width], ACT.Exp,
                                             scale=SCALE).then_inc(key_read[n % 2], 1)
                    elif what in ("pv", "pv_last"):
                        of, quad, at = (i, n // 4, n % 4) if what == "pv" else (i - 1, 3, n)
                        if at == 3:
                            act.wait_ge(pv_ready, 4 * of + quad + 1)
                            nc.scalar.activation(av[:, quad, :], pv_bank[:], ACT.Copy).then_inc(av_copied, 1)
                    elif what == "rows":
                        act.wait_ge(attnT_made, KC * (i - 1) + n + 1)
                        nc.scalar.activation(attnT[:, n, :], bank_of(what, n)[:], ACT.Copy).then_inc(attnT_copied, 1)

            turns(act, turn)

        @block.vector
        def _(dve):
            nc.vector.memset(ones_row[:], 1.0).then_inc(consts_dve, 1)
            nc.vector.memset(maxima[:], 0.0).then_inc(consts_dve, 1)
            dve.sem_inc(h2_stored, S.DMA_SEED)
            dve.wait_ge(loaded, ALL_LOADED)
            nc.vector.tensor_scalar(neg_ident[:], ident[:], -1.0, None, ALU.mult).then_inc(consts_dve, 1)
            dve.wait_ge(zeroed, 2)
            rows = k_rows[MROW:128, :, :, :].rearrange("p a (j e) n -> p (a j) e n", e=2)
            for e in range(2):
                nc.vector.tensor_copy(rows[:, :, e, :], tail[MROW:128, e, :].unsqueeze(1).broadcast_to([32, 2 * PAIRS, N]))\
                  .then_inc(consts_dve, 1)
            nc.vector.tensor_copy(q_rows[MROW:128, :, :, :].rearrange("p a j n -> p (a j) n"),
                                  tail[MROW:128, 2, :].unsqueeze(1).broadcast_to([32, 2 * PAIRS, N])).then_inc(consts_dve, 1)
            dve.wait_ge(consts_dve, 6)
            nc.vector.tensor_copy(maxima[:, :, :, 0:T], early[:].unsqueeze(2).broadcast_to([128, T, PAIRS, T]))\
              .then_inc(consts_dve, 1)
            dve.wait_ge(consts_pool, 2)
            dve.wait_ge(consts_dve, CONSTS)

            def turn(i, todo, previous, parity):
                for what, n in todo:
                    if what == "project":
                        if n % 2:
                            dve.wait_ge(h_copied, 2 * (i + 1) + n // 2 + 1)
                            for t in (n - 1, n):
                                nc.vector.bn_stats(stats[:, t, :], h_new[:, t, :]).then_inc(stat_step, 1)
                        if n == T - 1:
                            dve.wait_ge(stat_step, T * (i + 2))
                            pass_waits(dve, dve_passed)
                            for t in range(T):
                                nc.vector.bn_aggr(moments[:, t, :], stats[:, t, :]).then_inc(moments_made, 1)
                    elif what == "norm":
                        if n == 0:
                            dve.wait_ge(rstd_step, 2 * (i + 2))
                            dve.wait_ge(moments_made, T * (i + 2))
                        nc.vector.tensor_scalar(xn[:, n, :], h_new[:, n, :], moments[:, n, 0:1],
                                                rstd[:, n:n + 1], ALU.subtract, ALU.mult).then_inc(xn_made, 1)
                    elif what == "columns":
                        if n == 1:
                            dve.wait_ge(xT_made, KC * (i + 2))
                            nc.vector.tensor_copy(xT[:, 1, :], bank_of(what, 1)[:]).then_inc(xT_copied[1], 1)
                    elif what == "kq":
                        if n % 2:
                            k = n // 2
                            dve.wait_ge(hi_made, 4 * (i + 1) + k + 1)
                            nc.vector.tensor_tensor(split[:, k // 2, 1, k % 2, :], bank_of(what, k)[:],
                                                    split[:, k // 2, 0, k % 2, :], ALU.subtract).then_inc(lo_made, 1)
                    elif what == "max":
                        head, at = n // 3, RING.index((what, n))
                        dve.wait_ge(max_ready[at % 2], PER_BATCH[at % 2] * i + scores_before(at + 1, at % 2))
                        for t, part, col, width in MAX_TILES:
                            if part == n % 3:
                                last = nc.vector.tensor_reduce(
                                    maxima[:, t, head // 2, T + head % 2:T + head % 2 + 1],
                                    max_bank[at % 2][:, col:col + width], AX.X, ALU.max)
                        last.then_inc(max_read[at % 2], 1)
                    elif what == "turn":
                        heads = bank_of(what, n)[:].rearrange("p (h d) -> p h d", d=32)
                        dve.wait_ge(avT_made, T * (i - 1) + n + 1)
                        nc.vector.reciprocal(recip[:, n, :], heads[:, :, HD]).then_inc(recip_made, 1)
                        dve.wait_ge(recip_made, T * (i - 1) + n + 1)
                        nc.vector.tensor_tensor(attn[:, n, :].rearrange("p (h d) -> p h d", d=HD), heads[:, :, 0:HD],
                                                recip[:, n, :].unsqueeze(2).broadcast_to([128, HEADS, HD]),
                                                ALU.mult).then_inc(attn_made, 1)
                    elif what == "out":
                        if n % 2:
                            if n == 1:
                                dve.wait_ge(h2_stored, S.DMA_SEED + 16 * (i - 1))
                                dve.wait_ge(h_kept, i)
                            dve.wait_ge(proj_made, 2 * (i - 1) + n // 2 + 1)
                            for t in (n - 1, n):
                                nc.vector.tensor_tensor(h2[:, t, :], bank_of(what, n // 2)[:, t % 2 * C:t % 2 * C + C],
                                                        h[:, 1 - parity, t, :], ALU.add).then_inc(h2_made, 1)

            turns(dve, turn)


def weights_block(nc, io, keep):
    from contextlib import ExitStack
    import concourse.mybir as mybir
    S = sizes()
    F, H16, I16 = mybir.dt.float32, mybir.dt.float16, mybir.dt.int16
    ACT, ALU, AX = mybir.ActivationFunctionType, mybir.AluOpType, mybir.AxisListType
    C, KC, MI = S.C, S.KC, S.MI
    NAMES = ["w_up", "w_gate", "w_down"]
    BLOCKS = MI * C // S.WB
    with ExitStack() as ctx:
        def sb(name, shape, dt=F):
            return ctx.enter_context(nc.sbuf_tensor(name, shape, dt))

        def sem(name):
            return ctx.enter_context(nc.semaphore(name))

        raw = {n: sb(n, [128, MI, C] if n != "w_down" else [128, KC, S.I]) for n in NAMES}
        levels = sb("levels", [128, MI * C], I16)
        amax = sb("amax", [128, BLOCKS])
        scale = sb("scale", [128, BLOCKS])
        inverse = sb("inverse", [128, BLOCKS])
        ident = sb("ident_w", [128, 128])
        ps = [ctx.enter_context(nc.psum_tensor(f"wbank{i}", [128, 512], F)) for i in range(8)]
        loaded, step, quantized = sem("w_loaded"), sem("w_step"), sem("w_quantized")
        stream_loaded, turned, hi_made, lo_made = sem("w_stream_loaded"), sem("w_turned"), sem("w_hi_made"), sem("w_lo_made")

        jobs = []
        for n in ("w_up", "w_gate"):
            col = 0 if n == "w_up" else S.I
            for c in range(KC):
                for m in range(0, MI, 3):
                    pieces = [raw[n][:, m + k, c * 128:(c + 1) * 128] for k in range(3)]
                    at = slice(col + m * 128, col + (m + 3) * 128)
                    jobs.append((n, pieces, keep["wi_hi"][:, c, at], keep["wi_lo"][:, c, at]))
        for m in range(MI):
            pieces = [raw["w_down"][:, c, m * 128:(m + 1) * 128] for c in range(KC)]
            jobs.append(("w_down", pieces, keep["wo_hi"][:, m, :], keep["wo_lo"][:, m, :]))

        block = ctx.enter_context(nc.Block())

        @block.sync
        def _(sp):
            sp.dma_start(ident[:], io["ident"]).then_inc(loaded, 16)
            for n in NAMES:
                sp.dma_start(raw[n][:], io[n]).then_inc(loaded, 16)
            sp.wait_ge(loaded, 64)
            sp.dma_start(keep["h_all"][:], keep["h_dram"]).then_inc(stream_loaded, 16)
            sp.wait_ge(stream_loaded, 16)

        @block.vector
        def _(dve):
            dve.wait_ge(loaded, 64)
            steps = 0
            for n in NAMES:
                flat = raw[n][:].rearrange("p a b -> p (a b)")
                parts = flat.rearrange("p (s w) -> p s w", w=S.WB)

                def spread(t):
                    return t[:].unsqueeze(2).broadcast_to([128, BLOCKS, S.WB])

                nc.vector.tensor_reduce(amax[:], parts, AX.X, ALU.max, apply_absolute_value=True).then_inc(step, 1)
                dve.wait_ge(step, steps + 1)
                nc.vector.tensor_scalar(scale[:], amax[:], 1.0 / 7.0, 1e-12, ALU.mult, ALU.max).then_inc(step, 1)
                dve.wait_ge(step, steps + 2)
                nc.vector.reciprocal(inverse[:], scale[:]).then_inc(step, 1)
                dve.wait_ge(step, steps + 3)
                nc.vector.tensor_tensor(parts, parts, spread(inverse), ALU.mult).then_inc(step, 1)
                dve.wait_ge(step, steps + 4)
                nc.vector.tensor_scalar(levels[:], flat, 7.0, -8.0, ALU.min, ALU.max).then_inc(step, 1)
                dve.wait_ge(step, steps + 5)
                nc.vector.tensor_tensor(parts, levels[:].rearrange("p (s w) -> p s w", w=S.WB), spread(scale),
                                        ALU.mult).then_inc(step, 1)
                steps += 6
                dve.wait_ge(step, steps)
            nc.vector.engine_nop().then_inc(quantized, 1)
            for k, (_, pieces, hi, lo) in enumerate(jobs):
                width = 128 * len(pieces)
                dve.wait_ge(hi_made, k + 1)
                nc.vector.scalar_tensor_tensor(out=lo, in0=ps[k % 8][:, 0:width], scalar=S.WSCALE, in1=hi,
                                               op0=ALU.mult, op1=ALU.subtract).then_inc(lo_made, 1)

        @block.tensor
        def _(pe):
            pe.wait_ge(quantized, 1)
            for k, (_, pieces, _, _) in enumerate(jobs):
                if k >= 8:
                    pe.wait_ge(lo_made, k - 7)
                for j, piece in enumerate(pieces):
                    last = nc.tensor.transpose(ps[k % 8][:, j * 128:(j + 1) * 128], piece, ident[:])
                last.then_inc(turned, 1)

        @block.scalar
        def _(act):
            for k, (_, pieces, hi, _) in enumerate(jobs):
                act.wait_ge(turned, k + 1)
                nc.scalar.activation(hi, ps[k % 8][:, 0:128 * len(pieces)], ACT.Copy,
                                     scale=S.WSCALE).then_inc(hi_made, 1)


def norm_block(nc, keep):
    from contextlib import ExitStack
    import concourse.mybir as mybir
    S = sizes()
    SEED = S.SEED
    F = mybir.dt.float32
    ALU, AX = mybir.AluOpType, mybir.AxisListType
    B, T, C = S.B, S.T, S.C
    h_all, xn, peak = keep["h_all"], keep["xn"], keep["peak_x"]
    with ExitStack() as ctx:
        def sb(name, shape, dt=F):
            return ctx.enter_context(nc.sbuf_tensor(name, shape, dt))

        def sem(name):
            return ctx.enter_context(nc.semaphore(name))

        stats = sb("n_stats", [128, T, 6])
        batch_moments = sb("n_batch_moments", [128, T, 2])
        moments = sb("n_moments", [128, B, T, 2])
        rstd = sb("n_rstd", [128, B, T])
        minus_half = sb("n_minus_half", [128, B, T])
        const_made, stat_made, aggregated = sem("n_const"), sem("n_stat"), sem("n_aggregated")
        moments_made, rstd_step, passed = sem("n_moments_made"), sem("n_rstd_step"), sem("n_passed")
        xn_made, peak_made = sem("n_xn_made"), sem("n_peak_made")
        block = ctx.enter_context(nc.Block())

        @block.gpsimd
        def _(pool):
            nc.gpsimd.memset(minus_half[:], -0.5).then_inc(const_made, 1)
            pool.wait_ge(const_made, 1)
            pool.wait_ge(moments_made, SEED + B)
            nc.gpsimd.tensor_scalar(rstd[:], moments[:, :, :, 1], S.EPS, 1.0, ALU.add, ALU.mult).then_inc(rstd_step, 1)
            pool.wait_ge(rstd_step, 1)
            nc.gpsimd.tensor_tensor(rstd[:], rstd[:], minus_half[:], ALU.pow).then_inc(rstd_step, 1)

        @block.vector
        def _(dve):
            dve.sem_inc(moments_made, SEED)
            with dve.Fori(0, B) as i:
                for t in range(T):
                    nc.vector.bn_stats(stats[:, t, :], h_all[:, i, t, :]).then_inc(stat_made, 1)
                dve.wait_ge(moments_made, SEED + i)
                dve.wait_ge(stat_made, T * (i + 1))
                pass_waits(dve, passed)
                for t in range(T):
                    nc.vector.bn_aggr(batch_moments[:, t, :], stats[:, t, :]).then_inc(aggregated, 1)
                dve.wait_ge(aggregated, T * (i + 1))
                nc.vector.tensor_copy(moments[:, i, :, :], batch_moments[:]).then_inc(moments_made, 1)
            dve.wait_ge(rstd_step, 2)
            with dve.Fori(0, B) as i:
                for t in range(T):
                    nc.vector.tensor_scalar(xn[:, i, t, :], h_all[:, i, t, :], moments[:, i, t, 0:1], rstd[:, i, t:t + 1],
                                            ALU.subtract, ALU.mult).then_inc(xn_made, 1)
                dve.wait_ge(xn_made, T * (i + 1))
                nc.vector.tensor_reduce(peak[:, i, :], xn[:, i, :, :], AX.XY, ALU.max,
                                        apply_absolute_value=True).then_inc(peak_made, 1)


def global_scale(nc, keep, peaks, unit, name, outputs):
    from contextlib import ExitStack
    import concourse.mybir as mybir
    import concourse.bass as bass
    S = sizes()
    F = mybir.dt.float32
    ALU, AX = mybir.AluOpType, mybir.AxisListType
    scale, ratio = keep["scale_" + name], keep["ratio_" + name]
    with ExitStack() as ctx:
        own = ctx.enter_context(nc.sbuf_tensor(f"own_{name}", [128, 1], F))
        top = ctx.enter_context(nc.sbuf_tensor(f"top_{name}", [128, 1], F))
        inverse = ctx.enter_context(nc.sbuf_tensor(f"inverse_{name}", [128, 1], F))
        step = ctx.enter_context(nc.semaphore(f"step_{name}"))
        reduced = ctx.enter_context(nc.semaphore(f"reduced_{name}"))
        block = ctx.enter_context(nc.Block())

        @block.gpsimd
        def _(pool):
            pool.wait_ge(step, 1)
            nc.gpsimd.partition_all_reduce(top[:], own[:], 128, bass.bass_isa.ReduceOp.max).then_inc(reduced, 1)

        @block.vector
        def _(dve):
            nc.vector.tensor_reduce(own[:], peaks, AX.X, ALU.max).then_inc(step, 1)
            dve.wait_ge(reduced, 1)
            u = 1.0 if unit is None else unit[:, 0:1]
            nc.vector.tensor_scalar(scale[:], top[:], u, 1.0 / S.QMAX, ALU.mult, ALU.mult).then_inc(step, 1)
            dve.wait_ge(step, 2)
            nc.vector.tensor_scalar(scale[:], scale[:], 1e-12, None, ALU.max).then_inc(step, 1)
            dve.wait_ge(step, 3)
            nc.vector.reciprocal(inverse[:], scale[:]).then_inc(step, 1)
            dve.wait_ge(step, 4)
            nc.vector.tensor_scalar(ratio[:], inverse[:], u, None, ALU.mult).then_inc(step, 1)
            for tile, factor, other in outputs:
                o = 1.0 if other is None else other[:, 0:1]
                nc.vector.tensor_scalar(tile[:], scale[:], factor, o, ALU.mult, ALU.mult).then_inc(step, 1)


def turn_block(nc, io, keep):
    from contextlib import ExitStack
    import concourse.mybir as mybir
    S = sizes()
    SEED = S.SEED
    F, I16 = mybir.dt.float32, mybir.dt.int16
    ACT, ALU = mybir.ActivationFunctionType, mybir.AluOpType
    B, T, C, KC, N = S.B, S.T, S.C, S.KC, S.N
    xn, x_hi, x_lo = keep["xn"], keep["x_hi"], keep["x_lo"]
    with ExitStack() as ctx:
        def sb(name, shape, dt=F):
            return ctx.enter_context(nc.sbuf_tensor(name, shape, dt))

        def sem(name):
            return ctx.enter_context(nc.semaphore(name))

        levels = sb("t_levels", [128, 2, T, C], I16)
        whole = sb("t_whole", [128, 2, T, C])
        ident = sb("ident_t", [128, 128])
        ps = [ctx.enter_context(nc.psum_tensor(f"tbank{i}", [128, 512], F)) for i in range(4)]
        loaded, rounded, widened, turned = sem("t_loaded"), sem("t_rounded"), sem("t_widened"), sem("t_turned")
        hi_made, lo_made = sem("t_hi"), sem("t_lo")
        block = ctx.enter_context(nc.Block())

        @block.sync
        def _(sp):
            sp.dma_start(ident[:], io["ident"]).then_inc(loaded, 16)
            sp.wait_ge(loaded, 16)

        @block.scalar
        def _(act):
            act.sem_inc(widened, SEED)
            with act.Fori(0, B // 2) as i:
                for s in range(2):
                    act.wait_ge(rounded, 2 * i + s + 1)
                    act.wait_ge(turned, SEED + 2 * (i * 2))
                    nc.scalar.activation(whole[:, s, :, :], levels[:, s, :, :], ACT.Copy).then_inc(widened, 1)
                for s in range(2):
                    for c in range(KC):
                        act.wait_ge(turned, SEED + 2 * (2 * i + s) + c + 1)
                        nc.scalar.activation(x_hi[:, c, 2 * i + s, :], ps[2 * s + c][:], ACT.Copy).then_inc(hi_made, 1)

        @block.vector
        def _(dve):
            dve.sem_inc(lo_made, SEED)
            with dve.Fori(0, B // 2) as i:
                for s in range(2):
                    dve.wait_ge(widened, SEED + 2 * i)
                    nc.vector.tensor_scalar(levels[:, s, :, :], xn[:, 2 * i + s, :, :], keep["ratio_x"][:, 0:1], None,
                                            ALU.mult).then_inc(rounded, 1)
                for s in range(2):
                    for c in range(KC):
                        dve.wait_ge(hi_made, 2 * (2 * i + s) + c + 1)
                        nc.vector.tensor_tensor(x_lo[:, c, 2 * i + s, :], ps[2 * s + c][:], x_hi[:, c, 2 * i + s, :],
                                                ALU.subtract).then_inc(lo_made, 1)

        @block.tensor
        def _(pe):
            pe.sem_inc(turned, SEED)
            pe.wait_ge(loaded, 16)
            with pe.Fori(0, B // 2) as i:
                for s in range(2):
                    pe.wait_ge(widened, SEED + 2 * i + s + 1)
                    for c in range(KC):
                        pe.wait_ge(lo_made, SEED + 4 * i)
                        for t in range(T):
                            last = nc.tensor.transpose(ps[2 * s + c][:, t * 128:(t + 1) * 128],
                                                       whole[:, s, t, c * 128:(c + 1) * 128], ident[:])
                        last.then_inc(turned, 1)


def inner_products(nc, keep, out, col, i):
    S = sizes()
    x_hi, x_lo, w_hi, w_lo = keep["x_hi"], keep["x_lo"], keep["wi_hi"], keep["wi_lo"]
    pairs = [(c, w, x) for c in range(S.KC) for w, x in ((w_hi, x_hi), (w_hi, x_lo), (w_lo, x_hi))]
    for k, (c, w, x) in enumerate(pairs):
        last = nc.tensor.matmul(out, w[:, c, col:col + 128], x[:, c, i, :], start=k == 0, stop=k == len(pairs) - 1)
    return last


def peak_block(nc, keep):
    from contextlib import ExitStack
    import concourse.mybir as mybir
    S = sizes()
    SEED = S.SEED
    F = mybir.dt.float32
    ALU, AX = mybir.AluOpType, mybir.AxisListType
    with ExitStack() as ctx:
        ps = [ctx.enter_context(nc.psum_tensor(f"kbank{i}", [128, 2, 512], F)) for i in range(4)]
        ready = [ctx.enter_context(nc.semaphore(f"k_ready{i}")) for i in range(3)]
        read = [ctx.enter_context(nc.semaphore(f"k_read{i}")) for i in range(3)]
        block = ctx.enter_context(nc.Block())

        @block.tensor
        def _(pe):
            with pe.Fori(0, S.B) as i:
                for m in range(S.MI):
                    b = m % 3
                    pe.wait_ge(read[b], SEED + 2 * i + m // 3)
                    for half in range(2):
                        last = inner_products(nc, keep, ps[b][:, half, :], half * S.I + m * 128, i)
                    last.then_inc(ready[b], 1)

        @block.vector
        def _(dve):
            for s in read:
                dve.sem_inc(s, SEED)
            with dve.Fori(0, S.B) as i:
                for m in range(S.MI):
                    b = m % 3
                    dve.wait_ge(ready[b], 2 * i + m // 3 + 1)
                    nc.vector.tensor_reduce(keep["peak_ug"][:, i, m, :], ps[b][:, :, :], AX.X, ALU.max,
                                            apply_absolute_value=True).then_inc(read[b], 1)


def gate_block(nc, keep):
    from contextlib import ExitStack
    import concourse.mybir as mybir
    S = sizes()
    SEED = S.SEED
    F, I16 = mybir.dt.float32, mybir.dt.int16
    ACT, ALU, AX = mybir.ActivationFunctionType, mybir.AluOpType, mybir.AxisListType
    PAIRS = S.MI // 2
    gate = keep["gate"]
    with ExitStack() as ctx:
        def sb(name, shape, dt=F):
            return ctx.enter_context(nc.sbuf_tensor(name, shape, dt))

        def sem(name):
            return ctx.enter_context(nc.semaphore(name))

        ps = [ctx.enter_context(nc.psum_tensor(f"gbank{i}", [128, 2, 512], F)) for i in range(3)]
        tanh = sb("g_tanh", [128, PAIRS, 2, 512])
        sig = sb("g_sig", [128, PAIRS, 2, 512], I16)
        ready, levels_made, tanh_made, sig_made, product_made, peak_made = (
            [sem(f"g_{n}{k}") for k in range(PAIRS)]
            for n in ("ready", "levels", "tanh", "sig", "product", "peak"))
        passed = sem("g_passed")
        block = ctx.enter_context(nc.Block())

        @block.tensor
        def _(pe):
            with pe.Fori(0, S.B) as i:
                for k in range(PAIRS):
                    pe.wait_ge(levels_made[k], SEED + i)
                    for half in range(2):
                        last = inner_products(nc, keep, ps[k][:, half, :], S.I + (2 * k + half) * 128, i)
                    last.then_inc(ready[k], 1)

        @block.scalar
        def _(act):
            for s in levels_made:
                act.sem_inc(s, SEED)
            with act.Fori(0, S.B) as i:
                for k in range(PAIRS):
                    act.wait_ge(ready[k], i + 1)
                    nc.scalar.activation(gate[:, i, 2 * k:2 * k + 2, :], ps[k][:, :, :], ACT.Copy,
                                         scale=keep["ratio_gate"][:, 0:1]).then_inc(levels_made[k], 1)
                    act.wait_ge(levels_made[k], SEED + i + 1)
                    act.wait_ge(peak_made[k], SEED + i)
                    pass_waits(act, passed)
                    nc.scalar.activation(tanh[:, k, :, :], gate[:, i, 2 * k:2 * k + 2, :], ACT.Tanh,
                                         scale=keep["half_gate"][:, 0:1]).then_inc(tanh_made[k], 1)

        @block.vector
        def _(dve):
            for s in peak_made:
                dve.sem_inc(s, SEED)
            with dve.Fori(0, S.B) as i:
                for k in range(PAIRS):
                    dve.wait_ge(tanh_made[k], i + 1)
                    nc.vector.tensor_scalar(sig[:, k, :, :], tanh[:, k, :, :], 32768.0, 32767.0, ALU.mult,
                                            ALU.min).then_inc(sig_made[k], 1)
                    dve.wait_ge(sig_made[k], i + 1)
                    nc.vector.scalar_tensor_tensor(out=tanh[:, k, :, :], in0=sig[:, k, :, :], scalar=32768.0,
                                                   in1=gate[:, i, 2 * k:2 * k + 2, :], op0=ALU.add,
                                                   op1=ALU.mult).then_inc(product_made[k], 1)
                    dve.wait_ge(product_made[k], i + 1)
                    nc.vector.tensor_reduce(keep["peak_g2"][:, i, k:k + 1], tanh[:, k, :, :], AX.XY, ALU.max,
                                            apply_absolute_value=True).then_inc(peak_made[k], 1)


def product_block(nc, keep):
    from contextlib import ExitStack
    import concourse.mybir as mybir
    S = sizes()
    SEED = S.SEED
    DMA_SEED = S.DMA_SEED
    F, I16 = mybir.dt.float32, mybir.dt.int16
    ACT, ALU, AX = mybir.ActivationFunctionType, mybir.AluOpType, mybir.AxisListType
    PAIRS = S.MI // 2
    gate = keep["gate"]
    with ExitStack() as ctx:
        def sb(name, shape, dt=F):
            return ctx.enter_context(nc.sbuf_tensor(name, shape, dt))

        def sem(name):
            return ctx.enter_context(nc.semaphore(name))

        ps = [ctx.enter_context(nc.psum_tensor(f"pbank{i}", [128, 2, 512], F)) for i in range(3)]
        up = sb("p_up", [128, PAIRS, 2, 512], I16)
        tanh = sb("p_tanh", [128, PAIRS, 2, 512])
        sig = sb("p_sig", [128, PAIRS, 2, 512], I16)
        gated, levels = tanh, sig
        ready, up_made, tanh_made, sig_made, gated_made, levels_made, product_made, peak_made, stored = (
            [sem(f"p_{n}{k}") for k in range(PAIRS)]
            for n in ("ready", "up", "tanh", "sig", "gated", "levels", "product", "peak", "stored"))
        block = ctx.enter_context(nc.Block())

        @block.tensor
        def _(pe):
            with pe.Fori(0, S.B) as i:
                for k in range(PAIRS):
                    pe.wait_ge(up_made[k], SEED + i)
                    for half in range(2):
                        last = inner_products(nc, keep, ps[k][:, half, :], (2 * k + half) * 128, i)
                    last.then_inc(ready[k], 1)

        @block.scalar
        def _(act):
            for s in up_made:
                act.sem_inc(s, SEED)
            with act.Fori(0, S.B) as i:
                for k in range(PAIRS):
                    act.wait_ge(peak_made[k], SEED + i)
                    act.wait_ge(stored[k], DMA_SEED + 16 * i)
                    nc.scalar.activation(tanh[:, k, :, :], gate[:, i, 2 * k:2 * k + 2, :], ACT.Tanh,
                                         scale=keep["half_gate"][:, 0:1]).then_inc(tanh_made[k], 1)
                    act.wait_ge(ready[k], i + 1)
                    act.wait_ge(product_made[k], SEED + i)
                    nc.scalar.activation(up[:, k, :, :], ps[k][:, :, :], ACT.Copy,
                                         scale=keep["ratio_up"][:, 0:1]).then_inc(up_made[k], 1)

        @block.vector
        def _(dve):
            for s in peak_made:
                dve.sem_inc(s, SEED)
            for s in product_made:
                dve.sem_inc(s, SEED)
            with dve.Fori(0, S.B) as i:
                for k in range(PAIRS):
                    dve.wait_ge(tanh_made[k], i + 1)
                    nc.vector.tensor_scalar(sig[:, k, :, :], tanh[:, k, :, :], 32768.0, 32767.0, ALU.mult,
                                            ALU.min).then_inc(sig_made[k], 1)
                    dve.wait_ge(sig_made[k], i + 1)
                    nc.vector.scalar_tensor_tensor(out=gated[:, k, :, :], in0=sig[:, k, :, :], scalar=32768.0,
                                                   in1=gate[:, i, 2 * k:2 * k + 2, :], op0=ALU.add,
                                                   op1=ALU.mult).then_inc(gated_made[k], 1)
                    dve.wait_ge(gated_made[k], i + 1)
                    nc.vector.tensor_scalar(levels[:, k, :, :], gated[:, k, :, :], keep["ratio_g2"][:, 0:1], None,
                                            ALU.mult).then_inc(levels_made[k], 1)
                    dve.wait_ge(levels_made[k], i + 1)
                    dve.wait_ge(up_made[k], SEED + i + 1)
                    nc.vector.tensor_tensor(gated[:, k, :, :], levels[:, k, :, :], up[:, k, :, :],
                                            ALU.mult).then_inc(product_made[k], 1)
                    dve.wait_ge(product_made[k], SEED + i + 1)
                    nc.vector.tensor_reduce(keep["peak_o"][:, i, k:k + 1], gated[:, k, :, :], AX.XY, ALU.max,
                                            apply_absolute_value=True).then_inc(peak_made[k], 1)

        @block.sync
        def _(sp):
            for s in stored:
                sp.sem_inc(s, DMA_SEED)
            with sp.Fori(0, S.B) as i:
                for k in range(PAIRS):
                    sp.wait_ge(product_made[k], SEED + i + 1)
                    sp.dma_start(keep["o_dram"][:, i, 2 * k:2 * k + 2, :], gated[:, k, :, :]).then_inc(stored[k], 16)
            for k in range(PAIRS):
                sp.wait_ge(stored[k], DMA_SEED + 16 * S.B)


def down_block(nc, keep, out):
    from contextlib import ExitStack
    import concourse.mybir as mybir
    S = sizes()
    SEED = S.SEED
    F, H16, I16 = mybir.dt.float32, mybir.dt.float16, mybir.dt.int16
    ACT, ALU = mybir.ActivationFunctionType, mybir.AluOpType
    B, T, C, MI = S.B, S.T, S.C, S.MI
    out_v = out.rearrange("b (t p) c -> p b t c", p=128)
    with ExitStack() as ctx:
        def sb(name, shape, dt=F):
            return ctx.enter_context(nc.sbuf_tensor(name, shape, dt))

        def sem(name):
            return ctx.enter_context(nc.semaphore(name))

        ps = [[ctx.enter_context(nc.psum_tensor(f"dbank{s}{i}", [128, 2, C], F)) for i in range(2)] for s in range(2)]
        o = sb("d_o", [128, 2, MI, 512])
        h = sb("d_h", [128, 2, T, C])
        levels = sb("d_levels", [128, 2, MI, 512], I16)
        hi = sb("d_hi", [128, 2, MI, 512], H16)
        lo = sb("d_lo", [128, 2, MI, 512], H16)
        y = sb("d_y", [128, 2, T, C])
        loaded, rounded, hi_made, lo_made, ready, summed, stored, y_free = (
            [sem(f"d_{n}{s}") for s in range(2)]
            for n in ("loaded", "rounded", "hi", "lo", "ready", "summed", "stored", "y_free"))
        passed = sem("d_passed")
        block = ctx.enter_context(nc.Block())

        @block.sync
        def _(sp):
            with sp.Fori(0, B // 2) as i:
                for s in range(2):
                    sp.wait_ge(rounded[s], SEED + i)
                    pass_waits(sp, passed)
                    sp.wait_ge(summed[s], SEED + 2 * i)
                    pass_waits(sp, passed)
                    sp.dma_start(o[:, s, :, :], keep["o_dram"][:, 2 * i + s, :, :]).then_inc(loaded[s], 16)
                    sp.dma_start(h[:, s, :, :], keep["h_dram"][:, 2 * i + s, :, :]).then_inc(loaded[s], 16)

        @block.gpsimd
        def _(pool):
            for s in y_free:
                pool.sem_inc(s, SEED)
            with pool.Fori(0, B // 2) as i:
                for s in range(2):
                    pool.wait_ge(summed[s], SEED + 2 * i + 2)
                    pool.dma_start(out_v[:, 2 * i + s, :, :], y[:, s, :, :]).then_inc(stored[s], 16)
                    pool.wait_ge(stored[s], 16 * (i + 1))
                    pool.sem_inc(y_free[s], 1)

        @block.scalar
        def _(act):
            with act.Fori(0, B // 2) as i:
                for s in range(2):
                    act.wait_ge(rounded[s], SEED + i + 1)
                    act.wait_ge(ready[s], SEED + 2 * i)
                    nc.scalar.activation(hi[:, s, :, :], levels[:, s, :, :], ACT.Copy).then_inc(hi_made[s], 1)

        @block.vector
        def _(dve):
            for s in rounded:
                dve.sem_inc(s, SEED)
            for s in summed:
                dve.sem_inc(s, SEED)
            with dve.Fori(0, B // 2) as i:
                for s in range(2):
                    dve.wait_ge(loaded[s], 32 * (i + 1))
                    nc.vector.tensor_scalar(levels[:, s, :, :], o[:, s, :, :], keep["ratio_o"][:, 0:1], None,
                                            ALU.mult).then_inc(rounded[s], 1)
                    dve.wait_ge(hi_made[s], i + 1)
                    nc.vector.tensor_tensor(lo[:, s, :, :], levels[:, s, :, :], hi[:, s, :, :],
                                            ALU.subtract).then_inc(lo_made[s], 1)
                for s in range(2):
                    dve.wait_ge(y_free[s], SEED + i)
                    for half in range(2):
                        dve.wait_ge(ready[s], SEED + 2 * i + half + 1)
                        nc.vector.scalar_tensor_tensor(out=y[:, s, 2 * half:2 * half + 2, :], in0=ps[s][half][:, :, :],
                                                       scalar=keep["out_unit"][:, 0:1],
                                                       in1=h[:, s, 2 * half:2 * half + 2, :], op0=ALU.mult,
                                                       op1=ALU.add).then_inc(summed[s], 1)

        @block.tensor
        def _(pe):
            for s in ready:
                pe.sem_inc(s, SEED)
            with pe.Fori(0, B // 2) as i:
                for s in range(2):
                    pe.wait_ge(hi_made[s], i + 1)
                    pe.wait_ge(lo_made[s], i + 1)
                    pe.wait_ge(summed[s], SEED + 2 * i)
                    for t in range(T):
                        tok = slice(t * 128, (t + 1) * 128)
                        pairs = [(m, a, w) for m in range(MI) for a, w in
                                 ((hi, keep["wo_hi"]), (lo, keep["wo_hi"]), (hi, keep["wo_lo"]))]
                        for k, (m, a, w) in enumerate(pairs):
                            last = nc.tensor.matmul(ps[s][t // 2][:, t % 2, :], a[:, s, m, tok], w[:, m, :],
                                                    start=k == 0, stop=k == len(pairs) - 1)
                        if t % 2:
                            last.then_inc(ready[s], 1)


def ffn(nc, io, keep, out):
    from contextlib import ExitStack
    import concourse.mybir as mybir
    S = sizes()
    F, H16, I16 = mybir.dt.float32, mybir.dt.float16, mybir.dt.int16
    B, T, C, KC, MI, N = S.B, S.T, S.C, S.KC, S.MI, S.N
    with ExitStack() as ctx:
        def sb(name, shape, dt=F):
            keep[name] = ctx.enter_context(nc.sbuf_tensor(name, shape, dt))
            return keep[name]

        for name in ("x", "up", "gate", "g2", "o"):
            sb("scale_" + name, [128, 1])
            sb("ratio_" + name, [128, 1])
        for name in ("unit_x", "half_gate", "unit_g2", "unit_o", "out_unit"):
            sb(name, [128, 1])
        sb("h_all", [128, B, T, C])
        sb("peak_x", [128, B, 1])
        sb("peak_ug", [128, B, MI, 2])
        sb("peak_g2", [128, B, MI // 2])
        sb("peak_o", [128, B, MI // 2])
        sb("wi_hi", [128, KC, 2 * S.I], H16)
        sb("wi_lo", [128, KC, 2 * S.I], H16)
        sb("wo_hi", [128, MI, C], H16)
        sb("wo_lo", [128, MI, C], H16)
        weights_block(nc, io, keep)
        with nc.sbuf_tensor("xn_all", [128, B, T, C], F) as xn:
            keep["xn"] = xn
            norm_block(nc, keep)
            global_scale(nc, keep, keep["peak_x"][:, :, 0], None, "x", [(keep["unit_x"], 1.0 / S.WSCALE, None)])
            halves = keep["h_all"][:].rearrange("p b t c -> p (b t c)").bitcast(H16).rearrange(
                "p (k b n) -> p k b n", k=2 * KC, b=B)
            keep["x_hi"], keep["x_lo"] = halves[:, 0:KC], halves[:, KC:2 * KC]
            turn_block(nc, io, keep)
        with nc.sbuf_tensor("gate_levels", [128, B, MI, N], I16) as gate:
            keep["gate"] = gate
            peak_block(nc, keep)
            peaks = keep["peak_ug"]
            global_scale(nc, keep, peaks[:, :, :, 0].rearrange("p b m -> p (b m)"), keep["unit_x"], "up", [])
            global_scale(nc, keep, peaks[:, :, :, 1].rearrange("p b m -> p (b m)"), keep["unit_x"], "gate",
                         [(keep["half_gate"], 0.5, None), (keep["unit_g2"], 1.0 / 65536.0, None)])
            gate_block(nc, keep)
            global_scale(nc, keep, keep["peak_g2"][:].rearrange("p b m -> p (b m)"), keep["unit_g2"], "g2",
                         [(keep["unit_o"], 1.0, keep["scale_up"])])
            product_block(nc, keep)
        global_scale(nc, keep, keep["peak_o"][:].rearrange("p b m -> p (b m)"), keep["unit_o"], "o",
                     [(keep["out_unit"], 1.0 / S.WSCALE, None)])
        down_block(nc, keep, out)


def build(nc, io, out):
    import concourse.mybir as mybir
    S = sizes()
    F = mybir.dt.float32
    keep = {"h_dram": nc.dram_tensor("h_stream", (128, S.B, S.T, S.C), F, kind="Internal").ap(),
            "o_dram": nc.dram_tensor("products", (128, S.B, S.MI, S.N), F, kind="Internal").ap()}
    attention_block(nc, io, keep)
    ffn(nc, io, keep, out)


def kernel(x, L0_tok_embeddings, L0_tok_project_kernel, L0_attn_w_qkv, L0_attn_w_proj, L0_attn_b_proj,
           L0_ffn_w_gate, L0_ffn_w_up, L0_ffn_w_down):
    import numpy as np
    import concourse.bacc as bacc
    from concourse import mybir
    from concourse.bass_utils import run_bass_kernel_spmd

    S = sizes()

    def rows_to_partitions(a):
        return np.ascontiguousarray(a.reshape(-1, 128, a.shape[1]).transpose(1, 0, 2))

    w_qkv = np.asarray(L0_attn_w_qkv)
    big, token = 60000.0, np.arange(S.N)
    tile_of = token // 128 == np.arange(S.T)[:, None]
    tail = np.zeros((32, 3, S.N), np.float16)
    tail[0:S.T, 0:2] = np.where(tile_of & (token % 128 >= S.BLOCK), big, 0.0)[:, None]
    tail[S.T, 0] = tail[S.T + 1, 1] = 1.0
    tail[0:S.T, 2] = np.where(tile_of & (token % 128 < S.BLOCK), -big, 0.0)
    early = np.ascontiguousarray(-tail[0:S.T, 2].reshape(S.T, S.T, 128).transpose(2, 1, 0))
    arrays = {
        "ids": np.ascontiguousarray(np.asarray(x).reshape(S.B * S.T, 128).T),
        "table": np.asarray(L0_tok_embeddings),
        "w_tok": np.asarray(L0_tok_project_kernel),
        "w_q": rows_to_partitions(w_qkv[0:S.C].T),
        "w_k": rows_to_partitions(w_qkv[S.C:2 * S.C].T),
        "w_v": rows_to_partitions(w_qkv[2 * S.C:].T),
        "w_p": rows_to_partitions(np.asarray(L0_attn_w_proj).T),
        "bias": np.asarray(L0_attn_b_proj).reshape(1, S.C),
        "tail": tail,
        "early": early,
        "ident": np.eye(128, dtype=np.float32),
        "w_up": rows_to_partitions(np.asarray(L0_ffn_w_up)),
        "w_gate": rows_to_partitions(np.asarray(L0_ffn_w_gate)),
        "w_down": rows_to_partitions(np.asarray(L0_ffn_w_down)),
    }
    nc = bacc.Bacc("TRN2", target_bir_lowering=False, num_devices=1)
    io = {n: nc.dram_tensor(f"in_{n}", a.shape, mybir.dt.from_np(a.dtype), kind="ExternalInput").ap()
          for n, a in arrays.items()}
    out = nc.dram_tensor("out", (S.B, S.N, S.C), mybir.dt.float32, kind="ExternalOutput").ap()
    build(nc, io, out)
    r = run_bass_kernel_spmd(nc, [{f"in_{n}": a for n, a in arrays.items()}], core_ids=[0])
    return r.results[0]["out"]
```

```python
class Sizes:
    B, N, HID, C, HEADS, HD, I = 16, 512, 128, 256, 16, 16, 768
    WB = 32


def sizes():
    s = Sizes()
    s.T = s.N // 128
    s.KC = s.C // 128
    s.MI = s.I // 128
    s.BLOCK = 64
    s.EPS = 1e-5
    s.QMAX = 32767.0
    s.SEED, s.DMA_SEED = 1, 16
    s.WSCALE = 1024.0
    return s


def pass_waits(eng, passed):
    eng.sem_inc(passed, 1)


def wait_past(eng, sem, n):
    if isinstance(n, int) and n <= 0:
        return
    eng.wait_ge(sem, n)


def attention_block(nc, io, keep):
    from contextlib import ExitStack
    import concourse.bass as bass
    import concourse.mybir as mybir
    S = sizes()
    F, H16, I32 = mybir.dt.float32, mybir.dt.float16, mybir.dt.int32
    ACT, ALU, AX = mybir.ActivationFunctionType, mybir.AluOpType, mybir.AxisListType
    B, N, T, C, KC, HEADS, HD = S.B, S.N, S.T, S.C, S.KC, S.HEADS, S.HD
    SCALE = HD ** -0.5
    PAIRS = HEADS // 2
    MROW = 96
    MASK_END = MROW + T
    Q_PARTS, K_PARTS = (0, 1, 0), (0, 0, 1)

    MAX_TILES = [(3, 0, 0, 512), (2, 1, 0, 384), (0, 1, 384, 128), (1, 2, 0, 256)]
    KEY_TILES = [(0, 0, 0, 512), (1, 1, 0, 384), (3, 1, 384, 128), (2, 2, 0, 256)]
    P_COL = {0: 0, 1: 512, 3: 896, 2: 1024}

    NEG_LAG, KEY_LAG = 7, 11
    SLOTS = 3 * HEADS
    PIECES = {"embed": [0], "project": [2, 3, 5, 6], "pv_last": [None] * 8 + [1, 4, 6, 7] + [12, 13, 14, 15],
              "stats": [4, 5, 7, 8, 9], "norm": [11, 12, 13, 14], "columns": [16, 17], "turn": [18, 19, 20, 21],
              "kq": [22, 23, 24, 25, 28, 29, 30, 31], "rows": [26, 27], "pv": [26, 27, 29, 31] + [38, 40, 42, 44],
              "out": [32, 33, 34, 35], "v": [36, 37, 39, 41], "stats2": [34, 35, 36, 37, 37],
              "norm2": [40, 41, 42, 43, 44], "turn2": [45, 46]}
    ORDER = []
    for slot in range(SLOTS):
        ORDER += [(what, n) for what, at in PIECES.items() for n, s in enumerate(at) if s == slot]
        ORDER += [("neg" if 6 * n + NEG_LAG < SLOTS else "neg_last", n) for n in range(PAIRS)
                  if (6 * n + NEG_LAG) % SLOTS == slot]
        ORDER.append(("key" if slot >= KEY_LAG else "key_last", (slot - KEY_LAG) % SLOTS))
        ORDER.append(("max", slot))
    NEXT = ("embed", "project", "stats", "norm", "columns", "kq", "v")
    BEFORE = ("key_last", "neg_last", "pv_last", "turn", "rows", "out", "stats2", "norm2", "turn2")

    def of_which(what, i, parity):
        return (i - 1, 1 - parity) if what.endswith("_last") else (i, parity)

    def steps(scores, next_batch, batch_before):
        return [(w, n) for w, n in ORDER
                if (next_batch if w in NEXT else batch_before if w in BEFORE else scores)]

    def turns(engine, turn):
        lead, first, full = steps(False, True, False), steps(True, True, False), steps(True, True, True)
        last, end = steps(True, False, True), steps(False, False, True)
        turn(-1, lead, [], 1)
        turn(0, first, lead, 0)
        turn(1, full, first, 1)
        with engine.Fori(0, (B - 4) // 2) as j:
            turn(2 * j + 2, full, full, 0)
            turn(2 * j + 3, full, full, 1)
        turn(B - 2, full, full, 0)
        turn(B - 1, last, full, 1)
        turn(B, end, last, 0)

    with ExitStack() as ctx:
        def sb(name, shape, dt=F):
            return ctx.enter_context(nc.sbuf_tensor(name, shape, dt))

        def sem(name):
            return ctx.enter_context(nc.semaphore(name))

        ids_all = sb("ids_all", [128, B * T], I32)
        ids = sb("ids", [128, T], I32)
        emb = sb("emb", [128, T, S.HID])
        embT = sb("embT", [128, N])
        w_tok = sb("w_tok", [128, C])
        w_raw = sb("w_raw", [128, 4, KC, C])
        w_hi = sb("w_hi", [128, 4, KC, C], H16)
        w_lo = sb("w_lo", [128, 4, KC, C], H16)
        W_K, W_Q, W_V, W_P = range(4)
        bias = sb("bias", [128, C])
        ident = sb("ident", [128, 128])
        neg_ident = sb("neg_ident", [128, 128], H16)
        tail = sb("tail", [128, 3, N], H16)
        early = sb("early", [128, T, T], H16)
        h_new = sb("h_new", [128, T, C])
        h = sb("h", [128, 2, T, C])
        h2 = sb("h2", [128, T, C])
        stats = sb("stats", [128, T, 6])
        moments = sb("moments", [128, T, 2])
        rstd = sb("rstd", [128, T])
        minus_half = sb("minus_half", [128, T])
        xn = sb("xn", [128, T, C])
        xT_hi = sb("xT_hi", [128, KC, N], H16)
        xT_lo = sb("xT_lo", [128, KC, N], H16)
        split = sb("split", [128, 2, 2, 2, N], H16)
        q_rows = sb("q_rows", [128, 2, PAIRS, N], H16)
        k_rows = sb("k_rows", [128, 2, HEADS, N], H16)
        v = sb("v", [128, 2, T, HEADS, 32])
        maxima = sb("maxima", [128, T, PAIRS, 32], H16)
        probs = sb("probs", [128, 8, 1280])
        av = sb("av", [128, 4, N])
        recip = sb("recip", [128, T, HEADS])
        attn = sb("attn", [128, T, C])
        attnT_hi = sb("attnT_hi", [128, KC, N], H16)
        attnT_lo = sb("attnT_lo", [128, KC, N], H16)
        stats2 = sb("stats2", [128, T, 6])
        moments2 = sb("moments2", [128, T, 2])
        rstd2 = sb("rstd2", [128, T])
        xn2 = sb("xn2", [128, T, C])
        x2T = sb("x2T", [128, KC, N])
        split_dram = nc.dram_tensor("split_dram", (2, 2, 128, 2, N), H16, kind="Internal").ap()
        max_bank = [ctx.enter_context(nc.psum_tensor(f"max{i}", [128, 512], F)) for i in range(2)]
        key_bank = [ctx.enter_context(nc.psum_tensor(f"key{i}", [128, 512], F)) for i in range(2)]
        pv_bank = ctx.enter_context(nc.psum_tensor("pv", [128, 512], F))
        bank = [ctx.enter_context(nc.psum_tensor(f"bank{i}", [128, 512], F)) for i in range(3)]

        loaded, ids_loaded, ids_copied, gathered = sem("loaded"), sem("ids_loaded"), sem("ids_copied"), sem("gathered")
        consts_dve, consts_pool, zeroed = sem("consts_dve"), sem("consts_pool"), sem("zeroed")
        embT_made, embT_copied = sem("embT_made"), sem("embT_copied")
        h_made, h_copied = sem("h_made"), sem("h_copied")
        stat_step, moments_made, rstd_step, xn_made = sem("stat_step"), sem("moments_made"), sem("rstd_step"), sem("xn_made")
        xT_made, xT_hi_made, xT_lo_made = sem("xT_made"), sem("xT_hi_made"), sem("xT_lo_made")
        kq_made, hi_made, lo_made = sem("kq_made"), sem("hi_made"), sem("lo_made")
        split_stored, k_loaded = sem("split_stored"), sem("k_loaded")
        v_made, v_copied = sem("v_made"), sem("v_copied")
        max_ready, max_read = [sem(f"max_ready{b}") for b in range(2)], [sem(f"max_read{b}") for b in range(2)]
        neg_made, neg_ready = sem("neg_made"), sem("neg_ready")
        key_ready, key_read = [sem(f"key_ready{b}") for b in range(2)], [sem(f"key_read{b}") for b in range(2)]
        pv_ready, av_copied = sem("pv_ready"), sem("av_copied")
        avT_made, recip_made, attn_made = sem("avT_made"), sem("recip_made"), sem("attn_made")
        attnT_made, attnT_hi_made, attnT_lo_made = sem("attnT_made"), sem("attnT_hi_made"), sem("attnT_lo_made")
        w_hi_made, w_lo_made = sem("w_hi_made"), sem("w_lo_made")
        proj_made, h2_made, h2_stored = sem("proj_made"), sem("h2_made"), sem("h2_stored")
        h_kept = sem("h_kept")
        stat2_step, moments2_made, rstd2_step = sem("stat2_step"), sem("moments2_made"), sem("rstd2_step")
        xn2_made, peak_made = sem("xn2_made"), sem("peak_x_made")
        x2T_made, x2T_copied, x2T_stored = sem("x2T_made"), sem("x2T_copied"), sem("x2T_stored")
        pool_passed, dve_passed = sem("pool_passed"), sem("dve_passed")
        ffn_loaded, ffn_step, ffn_quantized = sem("ffn_loaded"), sem("ffn_step"), sem("ffn_quantized")
        ffn_turned, ffn_hi_made, ffn_lo_made = sem("ffn_turned"), sem("ffn_hi_made"), sem("ffn_lo_made")

        READERS = {"embed": (1, 1, embT_copied, 1), "turn": (1, -1, attn_made, 1), "rows": (1, -1, attnT_lo_made, 1),
                   "out": (2, -1, h2_made, 2), "project": (2, 1, h_copied, 1), "columns": (1, 1, xT_lo_made, 1),
                   "turn2": (1, -1, x2T_copied, 1), "kq": (2, 1, lo_made, 1), "v": (2, 1, v_copied, 1),
                   "neg": (1, 0, neg_ready, 1), "neg_last": (1, -1, neg_ready, 1)}
        USES = []
        for what, n in ORDER:
            pieces, of, sem_read, counts = READERS.get(what, (1, 0, None, 0))
            if counts and n % pieces == 0:
                per_batch = PAIRS if sem_read is neg_ready else len(PIECES[what]) // pieces * counts
                USES.append((what, of, sem_read, per_batch, (n // pieces + 1) * counts))

        def use_of(name, k):
            if name in ("neg", "neg_last"):
                return [j for j, u in enumerate(USES) if u[0] == name and u[4] == k + 1][0]
            return [j for j, u in enumerate(USES) if u[0] == name][k]

        def bank_of(name, k):
            return bank[use_of(name, k) % 3]

        def take_bank(pe, i, todo, previous, name, k):
            at = use_of(name, k)
            here = [u for u in range(at) if u % 3 == at % 3 and USES[u][0] in [w for w, _ in todo]]
            there = [u for u in range(len(USES)) if u % 3 == at % 3 and USES[u][0] in [w for w, _ in previous]]
            if here:
                _, of, sem_read, per_batch, count = USES[here[-1]]
                pe.wait_ge(sem_read, per_batch * (i + of) + count)
            elif there:
                _, of, sem_read, per_batch, count = USES[there[-1]]
                pe.wait_ge(sem_read, per_batch * (i - 1 + of) + count)
            return bank[at % 3]

        loads = [(ident[:], "ident"), (w_tok[:], "w_tok"), (w_raw[:], "w_attn"),
                 (tail[MROW:128], "tail"), (early[:], "early")]
        ALL_LOADED = 16 * (len(loads) + 1)
        CONSTS = 6
        ROW_LOADS = 12
        BLOCKS = S.MI * C // S.WB
        k_room = k_rows[:, 0, :, :].rearrange("p h n -> p (h n)").bitcast(F)
        q_room = q_rows[:, 0, :, :].rearrange("p h n -> p (h n)").bitcast(F)
        SIZE = S.MI * C
        raw = {"w_up": k_room[:, 0:SIZE].rearrange("p (a b) -> p a b", b=C),
               "w_gate": k_room[:, SIZE:2 * SIZE].rearrange("p (a b) -> p a b", b=C),
               "w_down": q_room[:, 0:SIZE].rearrange("p (a b) -> p a b", b=S.I)}
        quantize, turn_all, high_halves, low_halves = ffn_weights(
            nc, keep, raw, ident[:], max_bank + key_bank + [pv_bank], k_room[:, 2 * SIZE:2 * SIZE + SIZE // 2].bitcast(mybir.dt.int16),
            *(k_room[:, 3 * SIZE - SIZE // 2 + k * BLOCKS:3 * SIZE - SIZE // 2 + (k + 1) * BLOCKS] for k in range(3)))
        block = ctx.enter_context(nc.Block())

        @block.sync
        def _(sp):
            sp.dma_start(ids_all[:], io["ids"]).then_inc(ids_loaded, 16)
            for tile, name in loads:
                sp.dma_start(tile, io[name]).then_inc(loaded, 16)
            sp.dma_start(bias[:], io["bias"].broadcast_to([128, C])).then_inc(loaded, 16)
            sp.wait_ge(loaded, ALL_LOADED)
            sp.wait_ge(zeroed, 2)

            def turn(i, todo, previous, parity):
                for what, n in todo:
                    if isinstance(i, int) and i == B - 1 and (what, n) == ("out", 0):
                        sp.wait_ge(av_copied, 4 * (B - 1))
                        for name in raw:
                            sp.dma_start(raw[name], io[name]).then_inc(ffn_loaded, 16)
                    if what == "out" and n == T - 1:
                        sp.wait_ge(h2_made, T * i)
                        sp.dma_start(keep["h_dram"][:, bass.ds(i - 1, 1), :, :].rearrange("p b t c -> p (b t c)"),
                                     h2[:].rearrange("p t c -> p (t c)")).then_inc(h2_stored, 16)
                    elif what == "turn2" and n == KC - 1:
                        sp.wait_ge(x2T_copied, KC * i)
                        sp.dma_start(keep["xn_dram"][:, bass.ds(i - 1, 1), :, :].rearrange("p b c n -> p (b c n)"),
                                     x2T[:].rearrange("p c n -> p (c n)")).then_inc(x2T_stored, 16)
                    elif what == "kq" and n in (3, 7):
                        w = n // 4
                        sp.wait_ge(lo_made, 4 * (i + 1) + n // 2 + 1)
                        for part in range(2):
                            sp.dma_start(split_dram[w, part], split[:, w, part, :, :]).then_inc(split_stored, 16)
                        sp.wait_ge(split_stored, 64 * (i + 1) + 32 * (w + 1))
                        for e in range(2):
                            for slot in range(3):
                                rows = slice(48 * e + 16 * slot, 48 * e + 16 * slot + HD)
                                part = (K_PARTS, Q_PARTS)[w][slot]
                                src = split_dram[w, part].rearrange("(j e d) g n -> e d g j n", e=2, d=HD)[e]
                                if w == 0:
                                    dst = k_rows[rows, 1 - parity, :, :].rearrange("d (g j e) n -> d g j e n", g=2, e=2)[:, :, :, e, :]
                                else:
                                    dst = q_rows[rows, 1 - parity, :, :].rearrange("d (g j) n -> d g j n", g=2)
                                sp.dma_start(dst, src).then_inc(k_loaded, 16)

            turns(sp, turn)
            sp.wait_ge(h2_stored, S.DMA_SEED + 16 * B)
            sp.wait_ge(x2T_stored, S.DMA_SEED + 16 * B)

        @block.gpsimd
        def _(pool):
            nc.gpsimd.memset(minus_half[:], -0.5).then_inc(consts_pool, 1)
            pool.wait_ge(ids_loaded, 16)

            def gather_and_scale(b, parity):
                wait_past(pool, embT_made, b)
                nc.gpsimd.tensor_copy(ids[:], ids_all[:, bass.ds(b * T, T)]).then_inc(ids_copied, 1)
                pool.wait_ge(ids_copied, b + 1)
                pass_waits(pool, pool_passed)
                for t in range(T):
                    nc.gpsimd.indirect_dma_start(
                        emb[:, t, :], None, io["table"],
                        bass.IndirectOffsetOnAxis(ap=ids[:, t:t + 1], axis=0)).then_inc(gathered, 16)
                if isinstance(b, int) and b == 0:
                    nc.gpsimd.memset(v[:], 1.0).then_inc(consts_pool, 1)
                    nc.gpsimd.memset(q_rows[:].rearrange("p a h n -> p (a h n)").bitcast(F), 0.0).then_inc(zeroed, 1)
                    pool.wait_ge(consts_pool, 2)
                    pool.wait_ge(loaded, ALL_LOADED)
                pool.wait_ge(moments_made, T * (b + 1))
                pass_waits(pool, pool_passed)
                nc.gpsimd.tensor_scalar(rstd[:], moments[:, :, 1], S.EPS, 1.0, ALU.add, ALU.mult).then_inc(rstd_step, 1)
                pool.wait_ge(rstd_step, 2 * b + 1)
                nc.gpsimd.tensor_tensor(rstd[:], rstd[:], minus_half[:], ALU.pow).then_inc(rstd_step, 1)

                pool.wait_ge(h_copied, 2 * (b + 1))
                wait_past(pool, h2_made, T * (b - 1))
                pass_waits(pool, pool_passed)
                nc.gpsimd.tensor_tensor(h[:, parity, :, :], h_new[:], bias[:].unsqueeze(1).broadcast_to([128, T, C]),
                                        ALU.add).then_inc(h_kept, 1)

            def second_scale(b):
                pool.wait_ge(moments2_made, T * (b + 1))
                pass_waits(pool, pool_passed)
                nc.gpsimd.tensor_scalar(rstd2[:], moments2[:, :, 1], S.EPS, 1.0, ALU.add, ALU.mult).then_inc(rstd2_step, 1)
                pool.wait_ge(rstd2_step, 2 * b + 1)
                nc.gpsimd.tensor_tensor(rstd2[:], rstd2[:], minus_half[:], ALU.pow).then_inc(rstd2_step, 1)

            gather_and_scale(0, 0)
            gather_and_scale(1, 1)
            with pool.Fori(0, (B - 2) // 2) as j:
                for parity in range(2):
                    gather_and_scale(2 * j + 2 + parity, parity)
                    second_scale(2 * j + parity)
            second_scale(B - 2)
            second_scale(B - 1)

        @block.tensor
        def _(pe):
            pe.wait_ge(loaded, ALL_LOADED)

            def three_products(out, hi, lo, tokens, w):
                pairs = [(c, a, b) for c in range(KC) for a, b in ((hi, w_hi), (lo, w_hi), (hi, w_lo))]
                for k, (c, a, b) in enumerate(pairs):
                    last = nc.tensor.matmul(out, a[:, c, tokens], b[:, w, c, :], start=k == 0, stop=k == len(pairs) - 1)
                return last

            def turn(i, todo, previous, parity):
                if isinstance(i, int) and i == -1:
                    pe.wait_ge(w_lo_made, 4)
                if isinstance(i, int) and i == 0:
                    pe.wait_ge(consts_dve, CONSTS)
                    pe.wait_ge(consts_pool, 2)
                    pe.wait_ge(zeroed, 2)
                for what, n in todo:
                    if what == "embed":
                        pe.wait_ge(gathered, 16 * T * (i + 2))
                        ps = take_bank(pe, i, todo, previous, what, 0)
                        for t in range(T):
                            last = nc.tensor.transpose(ps[:, t * 128:(t + 1) * 128], emb[:, t, :], ident[:])
                        last.then_inc(embT_made, 1)
                    elif what == "project":
                        pe.wait_ge(embT_copied, i + 2)
                        if n % 2 == 0:
                            take_bank(pe, i, todo, previous, what, n // 2)
                        last = nc.tensor.matmul(bank_of(what, n // 2)[:, n % 2 * C:n % 2 * C + C],
                                                embT[:, n * 128:(n + 1) * 128], w_tok[:], start=True, stop=True)
                        if n % 2:
                            last.then_inc(h_made, 1)
                    elif what == "columns":
                        pe.wait_ge(xn_made, T * (i + 2))
                        ps = take_bank(pe, i, todo, previous, what, n)
                        for t in range(T):
                            last = nc.tensor.transpose(ps[:, t * 128:(t + 1) * 128],
                                                       xn[:, t, n * 128:(n + 1) * 128], ident[:])
                        last.then_inc(xT_made, 1)
                    elif what == "kq":
                        c, w, half = n % 2, (W_K, W_Q)[n // 4], n // 2 % 2
                        columns = slice(half * 128, (half + 1) * 128)
                        pe.wait_ge(xT_lo_made, KC * (i + 1) + c + 1)
                        if c == 0:
                            take_bank(pe, i, todo, previous, what, n // 2)
                        for k, (a, x) in enumerate(((w_hi, xT_hi), (w_hi, xT_lo), (w_lo, xT_hi))):
                            last = nc.tensor.matmul(bank_of(what, n // 2)[:], a[:, w, c, columns], x[:, c, :],
                                                    start=c == 0 and k == 0, stop=c == KC - 1 and k == 2)
                        if c == KC - 1:
                            last.then_inc(kq_made, 1)
                    elif what == "v":
                        if n % 2 == 0:
                            take_bank(pe, i, todo, previous, what, n // 2)
                        last = three_products(bank_of(what, n // 2)[:, n % 2 * C:n % 2 * C + C],
                                              xT_hi, xT_lo, slice(n * 128, (n + 1) * 128), W_V)
                        if n % 2:
                            last.then_inc(v_made, 1)
                    elif what == "max":
                        if n == 0:
                            pe.wait_ge(k_loaded, 16 * ROW_LOADS * (i + 1))
                        head, rows = n // 3, slice(0, MASK_END)
                        ps = max_bank[n % 2]
                        wait_past(pe, max_read[n % 2], 24 * i + n // 2)
                        for t, part, col, width in MAX_TILES:
                            if part == n % 3:
                                last = nc.tensor.matmul(ps[:, col:col + width],
                                                        q_rows[rows, parity, head // 2, t * 128:(t + 1) * 128],
                                                        k_rows[rows, parity, head, 0:width], start=True, stop=True)
                        last.then_inc(max_ready[n % 2], 1)
                    elif what in ("neg", "neg_last"):
                        of, par = of_which(what, i, parity)
                        for b in range(2):
                            pe.wait_ge(max_read[b], 24 * of + 3 * (n + 1))
                        ps = take_bank(pe, i, todo, previous, what, n)
                        for t in range(T):
                            last = nc.tensor.matmul(ps[MROW:128, t * 128:(t + 1) * 128], maxima[:, t, n, :],
                                                    neg_ident[:], start=True, stop=True, skip_group_check=True)
                        last.then_inc(neg_made, 1)
                    elif what in ("key", "key_last"):
                        head = n // 3
                        of, par = of_which(what, i, parity)
                        pe.wait_ge(neg_ready, PAIRS * of + head // 2 + 1)
                        wait_past(pe, key_read[n % 2], 24 * of + n // 2)
                        for t, part, col, width in KEY_TILES:
                            if part == n % 3:
                                last = nc.tensor.matmul(key_bank[n % 2][:, col:col + width],
                                                        k_rows[:, par, head, t * 128:(t + 1) * 128],
                                                        q_rows[:, par, head // 2, t * 128:N], start=True, stop=True)
                        last.then_inc(key_ready[n % 2], 1)
                    elif what in ("pv", "pv_last"):
                        quad, at = n // 4, n % 4
                        of, par = of_which(what, i, parity)
                        if at == 0:
                            pe.wait_ge(v_copied, 2 * (of + 1))
                            for b in range(2):
                                pe.wait_ge(key_read[b], 24 * of + 6 * (quad + 1))
                            wait_past(pe, av_copied, 4 * of + quad)
                        t, _, _, width = KEY_TILES[at]
                        for j in range(4):
                            head = 4 * quad + j
                            last = nc.tensor.matmul(pv_bank[32 * j:32 * j + 32, t * 128:N],
                                                    v[:, par, t, head, :],
                                                    probs[:, head % 8, P_COL[t]:P_COL[t] + width],
                                                    start=at == 0, stop=at == 3, skip_group_check=True)
                        if at == 3:
                            last.then_inc(pv_ready, 1)
                    elif what == "turn":
                        pe.wait_ge(av_copied, 4 * i)
                        ps = take_bank(pe, i, todo, previous, what, n)
                        for q in range(4):
                            last = nc.tensor.transpose(ps[:, q * 128:(q + 1) * 128],
                                                       av[:, q, n * 128:(n + 1) * 128], ident[:])
                        last.then_inc(avT_made, 1)
                    elif what == "rows":
                        pe.wait_ge(attn_made, T * i)
                        ps = take_bank(pe, i, todo, previous, what, n)
                        for t in range(T):
                            last = nc.tensor.transpose(ps[:, t * 128:(t + 1) * 128],
                                                       attn[:, t, n * 128:(n + 1) * 128], ident[:])
                        last.then_inc(attnT_made, 1)
                    elif what == "turn2":
                        pe.wait_ge(xn2_made, T * i)
                        ps = take_bank(pe, i, todo, previous, what, n)
                        for t in range(T):
                            last = nc.tensor.transpose(ps[:, t * 128:(t + 1) * 128],
                                                       xn2[:, t, n * 128:(n + 1) * 128], ident[:])
                        last.then_inc(x2T_made, 1)
                    elif what == "out":
                        pe.wait_ge(attnT_lo_made, KC * i)
                        if n % 2 == 0:
                            take_bank(pe, i, todo, previous, what, n // 2)
                        out = bank_of(what, n // 2)[:, n % 2 * C:n % 2 * C + C]
                        last = three_products(out, attnT_hi, attnT_lo, slice(n * 128, (n + 1) * 128), W_P)
                        if n % 2:
                            last.then_inc(proj_made, 1)

            turns(pe, turn)
            for b in range(2):
                pe.wait_ge(max_read[b], 24 * B)
                pe.wait_ge(key_read[b], 24 * B)
            pe.wait_ge(neg_ready, PAIRS * B)
            pe.wait_ge(av_copied, 4 * B)
            turn_all(pe, ffn_quantized, ffn_turned, ffn_lo_made)

        @block.scalar
        def _(act):
            act.wait_ge(loaded, ALL_LOADED)
            for w in range(4):
                nc.scalar.activation(w_hi[:, w, :, :], w_raw[:, w, :, :], ACT.Copy, scale=S.WSCALE).then_inc(w_hi_made, 1)

            def turn(i, todo, previous, parity):
                for what, n in todo:
                    if what == "embed":
                        act.wait_ge(embT_made, i + 2)
                        nc.scalar.activation(embT[:], bank_of(what, 0)[:], ACT.Copy).then_inc(embT_copied, 1)
                    elif what == "project":
                        half = n // 2
                        if n == 1:
                            wait_past(act, h_kept, i + 1)
                        if n % 2:
                            act.wait_ge(h_made, 2 * (i + 1) + half + 1)
                            nc.scalar.activation(h_new[:, 2 * half:2 * half + 2, :],
                                                 bank_of(what, half)[:].rearrange("p (t c) -> p t c", t=2),
                                                 ACT.Copy).then_inc(h_copied, 1)
                    elif what == "columns":
                        act.wait_ge(xT_made, KC * (i + 1) + n + 1)
                        nc.scalar.activation(xT_hi[:, n, :], bank_of(what, n)[:], ACT.Copy).then_inc(xT_hi_made, 1)
                    elif what == "kq":
                        if n % 2:
                            k = n // 2
                            act.wait_ge(kq_made, 4 * (i + 1) + k + 1)
                            if k == 0:
                                wait_past(act, split_stored, 64 * (i + 1))
                            nc.scalar.activation(split[:, k // 2, 0, k % 2, :], bank_of(what, k)[:],
                                                 ACT.Copy, scale=1.0 / S.WSCALE).then_inc(hi_made, 1)
                    elif what == "v":
                        if n % 2:
                            half = n // 2
                            if isinstance(i, int) and i == -1:
                                act.wait_ge(consts_pool, 2)
                            act.wait_ge(v_made, 2 * (i + 1) + half + 1)
                            nc.scalar.activation(v[:, 1 - parity, 2 * half:2 * half + 2, :, 0:HD],
                                                 bank_of(what, half)[:].rearrange("p (t h d) -> p t h d", t=2, d=HD),
                                                 ACT.Copy, scale=1.0 / S.WSCALE).then_inc(v_copied, 1)
                    elif what in ("neg", "neg_last"):
                        of, par = of_which(what, i, parity)
                        act.wait_ge(neg_made, PAIRS * of + n + 1)
                        nc.scalar.activation(q_rows[MROW:128, par, n, :], bank_of(what, n)[MROW:128, :],
                                             ACT.Copy).then_inc(neg_ready, 1)
                    elif what in ("key", "key_last"):
                        head, part = n // 3, n % 3
                        width = (512, 512, 256)[part]
                        of, _ = of_which(what, i, parity)
                        if n % 12 == 0:
                            wait_past(act, pv_ready, 4 * of + n // 12 - 1)
                        act.wait_ge(key_ready[n % 2], 24 * of + n // 2 + 1)
                        nc.scalar.activation(probs[:, head % 8, 512 * part:512 * part + width],
                                             key_bank[n % 2][:, 0:width], ACT.Exp,
                                             scale=SCALE).then_inc(key_read[n % 2], 1)
                    elif what in ("pv", "pv_last"):
                        of, _ = of_which(what, i, parity)
                        if n % 4 == 3:
                            act.wait_ge(pv_ready, 4 * of + n // 4 + 1)
                            nc.scalar.activation(av[:, n // 4, :], pv_bank[:], ACT.Copy).then_inc(av_copied, 1)
                    elif what == "rows":
                        act.wait_ge(attnT_made, KC * (i - 1) + n + 1)
                        nc.scalar.activation(attnT_hi[:, n, :], bank_of(what, n)[:], ACT.Copy).then_inc(attnT_hi_made, 1)
                    elif what == "turn2":
                        act.wait_ge(x2T_made, KC * (i - 1) + n + 1)
                        if n == 0:
                            act.wait_ge(x2T_stored, S.DMA_SEED + 16 * (i - 1))
                        nc.scalar.activation(x2T[:, n, :], bank_of(what, n)[:], ACT.Copy).then_inc(x2T_copied, 1)

            turns(act, turn)
            high_halves(act, ffn_turned, ffn_hi_made)

        @block.vector
        def _(dve):
            nc.vector.memset(k_rows[:].rearrange("p a h n -> p (a h n)").bitcast(F), 0.0).then_inc(zeroed, 1)
            nc.vector.memset(maxima[:], 0.0).then_inc(consts_dve, 1)
            for s in (h2_stored, x2T_stored):
                dve.sem_inc(s, S.DMA_SEED)

            for w in range(4):
                dve.wait_ge(w_hi_made, w + 1)
                nc.vector.scalar_tensor_tensor(out=w_lo[:, w, :, :], in0=w_raw[:, w, :, :], scalar=S.WSCALE,
                                               in1=w_hi[:, w, :, :], op0=ALU.mult,
                                               op1=ALU.subtract).then_inc(w_lo_made, 1)

            def finish_constants():
                dve.wait_ge(loaded, ALL_LOADED)
                nc.vector.tensor_scalar(neg_ident[:], ident[:], -1.0, None, ALU.mult).then_inc(consts_dve, 1)
                dve.wait_ge(zeroed, 2)
                rows = k_rows[MROW:128, :, :, :].rearrange("p a (j e) n -> p (a j) e n", e=2)
                for e in range(2):
                    nc.vector.tensor_copy(rows[:, :, e, :], tail[MROW:128, e, :].unsqueeze(1).broadcast_to(
                        [32, 2 * PAIRS, N])).then_inc(consts_dve, 1)
                nc.vector.tensor_copy(q_rows[MROW:128, :, :, :].rearrange("p a j n -> p (a j) n"),
                                      tail[MROW:128, 2, :].unsqueeze(1).broadcast_to(
                                          [32, 2 * PAIRS, N])).then_inc(consts_dve, 1)
                dve.wait_ge(consts_dve, CONSTS - 1)
                nc.vector.tensor_copy(maxima[:, :, :, 0:T], early[:].unsqueeze(2).broadcast_to(
                    [128, T, PAIRS, T])).then_inc(consts_dve, 1)
                dve.wait_ge(consts_dve, CONSTS)

            def turn(i, todo, previous, parity):
                if isinstance(i, int) and i == 0:
                    finish_constants()
                if isinstance(i, int) and i == B:
                    quantize(dve, "w_up", ffn_loaded, ffn_step, ffn_quantized)
                    quantize(dve, "w_gate", ffn_loaded, ffn_step, ffn_quantized)
                for what, n in todo:
                    if isinstance(i, int) and i == B and (what, n) == ("out", 0):
                        quantize(dve, "w_down", ffn_loaded, ffn_step, ffn_quantized)
                    if what == "stats":
                        if n < T:
                            dve.wait_ge(h_copied, 2 * (i + 1) + n // 2 + 1)
                            nc.vector.bn_stats(stats[:, n, :], h_new[:, n, :]).then_inc(stat_step, 1)
                        else:
                            dve.wait_ge(stat_step, T * (i + 2))
                            pass_waits(dve, dve_passed)
                            for t in range(T):
                                nc.vector.bn_aggr(moments[:, t, :], stats[:, t, :]).then_inc(moments_made, 1)
                    elif what == "norm":
                        if n == 0:
                            dve.wait_ge(rstd_step, 2 * (i + 2))
                            dve.wait_ge(moments_made, T * (i + 2))
                        nc.vector.tensor_scalar(xn[:, n, :], h_new[:, n, :], moments[:, n, 0:1],
                                                rstd[:, n:n + 1], ALU.subtract, ALU.mult).then_inc(xn_made, 1)
                    elif what == "columns":
                        dve.wait_ge(xT_hi_made, KC * (i + 1) + n + 1)
                        nc.vector.tensor_tensor(xT_lo[:, n, :], bank_of(what, n)[:], xT_hi[:, n, :],
                                                ALU.subtract).then_inc(xT_lo_made, 1)
                    elif what == "rows":
                        dve.wait_ge(attnT_hi_made, KC * (i - 1) + n + 1)
                        nc.vector.tensor_tensor(attnT_lo[:, n, :], bank_of(what, n)[:], attnT_hi[:, n, :],
                                                ALU.subtract).then_inc(attnT_lo_made, 1)
                    elif what == "kq":
                        if n % 2:
                            k = n // 2
                            dve.wait_ge(hi_made, 4 * (i + 1) + k + 1)
                            nc.vector.scalar_tensor_tensor(out=split[:, k // 2, 1, k % 2, :], in0=bank_of(what, k)[:],
                                                           scalar=1.0 / S.WSCALE, in1=split[:, k // 2, 0, k % 2, :],
                                                           op0=ALU.mult, op1=ALU.subtract).then_inc(lo_made, 1)
                    elif what == "max":
                        head = n // 3
                        dve.wait_ge(max_ready[n % 2], 24 * i + n // 2 + 1)
                        for t, part, col, width in MAX_TILES:
                            if part == n % 3:
                                last = nc.vector.tensor_reduce(
                                    maxima[:, t, head // 2, T + head % 2:T + head % 2 + 1],
                                    max_bank[n % 2][:, col:col + width], AX.X, ALU.max)
                        last.then_inc(max_read[n % 2], 1)
                    elif what == "turn":
                        heads = bank_of(what, n)[:].rearrange("p (h d) -> p h d", d=32)
                        dve.wait_ge(avT_made, T * (i - 1) + n + 1)
                        nc.vector.reciprocal(recip[:, n, :], heads[:, :, HD]).then_inc(recip_made, 1)
                        dve.wait_ge(recip_made, T * (i - 1) + n + 1)
                        nc.vector.tensor_tensor(attn[:, n, :].rearrange("p (h d) -> p h d", d=HD), heads[:, :, 0:HD],
                                                recip[:, n, :].unsqueeze(2).broadcast_to([128, HEADS, HD]),
                                                ALU.mult).then_inc(attn_made, 1)
                    elif what == "out":
                        if n % 2:
                            if n == 1:
                                dve.wait_ge(h2_stored, S.DMA_SEED + 16 * (i - 1))
                                dve.wait_ge(h_kept, i)
                            dve.wait_ge(proj_made, 2 * (i - 1) + n // 2 + 1)
                            for t in (n - 1, n):
                                nc.vector.scalar_tensor_tensor(
                                    out=h2[:, t, :], in0=bank_of(what, n // 2)[:, t % 2 * C:t % 2 * C + C],
                                    scalar=1.0 / S.WSCALE, in1=h[:, 1 - parity, t, :], op0=ALU.mult,
                                    op1=ALU.add).then_inc(h2_made, 1)
                    elif what == "stats2":
                        if n < T:
                            dve.wait_ge(h2_made, T * (i - 1) + n + 1)
                            nc.vector.bn_stats(stats2[:, n, :], h2[:, n, :]).then_inc(stat2_step, 1)
                        else:
                            dve.wait_ge(stat2_step, T * i)
                            pass_waits(dve, dve_passed)
                            for t in range(T):
                                nc.vector.bn_aggr(moments2[:, t, :], stats2[:, t, :]).then_inc(moments2_made, 1)
                    elif what == "norm2":
                        if n == 0:
                            dve.wait_ge(moments2_made, T * i)
                            dve.wait_ge(rstd2_step, 2 * i)
                        if n < T:
                            nc.vector.tensor_scalar(xn2[:, n, :], h2[:, n, :], moments2[:, n, 0:1],
                                                    rstd2[:, n:n + 1], ALU.subtract, ALU.mult).then_inc(xn2_made, 1)
                        else:
                            dve.wait_ge(xn2_made, T * i)
                            nc.vector.tensor_reduce(keep["peak_x"][:, bass.ds(i - 1, 1)], xn2[:, :, :], AX.XY, ALU.max,
                                                    apply_absolute_value=True).then_inc(peak_made, 1)

            turns(dve, turn)
            low_halves(dve, ffn_hi_made, ffn_lo_made)


def ffn_weights(nc, keep, raw, ident, banks, levels, amax, scale, inverse):
    import concourse.mybir as mybir
    S = sizes()
    ACT, ALU, AX = mybir.ActivationFunctionType, mybir.AluOpType, mybir.AxisListType
    KC, MI = S.KC, S.MI
    BLOCKS = MI * S.C // S.WB
    NAMES = list(raw)
    jobs = []
    for n in ("w_up", "w_gate"):
        col = 0 if n == "w_up" else S.I
        for c in range(KC):
            for m in range(0, MI, 3):
                pieces = [raw[n][:, m + k, c * 128:(c + 1) * 128] for k in range(3)]
                at = slice(col + m * 128, col + (m + 3) * 128)
                jobs.append((n, pieces, keep["wi_hi"][:, c, at], keep["wi_lo"][:, c, at]))
    for m in range(MI):
        pieces = [raw["w_down"][:, c, m * 128:(m + 1) * 128] for c in range(KC)]
        jobs.append(("w_down", pieces, keep["wo_hi"][:, m, :], keep["wo_lo"][:, m, :]))

    def quantize(dve, n, loaded, step, quantized):
        at = NAMES.index(n)
        dve.wait_ge(loaded, 16 * len(NAMES))
        steps = 6 * at
        flat = raw[n].rearrange("p a b -> p (a b)")
        parts = flat.rearrange("p (s w) -> p s w", w=S.WB)

        def spread(t):
            return t[:].unsqueeze(2).broadcast_to([128, BLOCKS, S.WB])

        nc.vector.tensor_reduce(amax[:], parts, AX.X, ALU.max, apply_absolute_value=True).then_inc(step, 1)
        dve.wait_ge(step, steps + 1)
        nc.vector.tensor_scalar(scale[:], amax[:], 1.0 / 7.0, 1e-12, ALU.mult, ALU.max).then_inc(step, 1)
        dve.wait_ge(step, steps + 2)
        nc.vector.reciprocal(inverse[:], scale[:]).then_inc(step, 1)
        dve.wait_ge(step, steps + 3)
        nc.vector.tensor_tensor(parts, parts, spread(inverse), ALU.mult).then_inc(step, 1)
        dve.wait_ge(step, steps + 4)
        nc.vector.tensor_scalar(levels[:], flat, 7.0, -8.0, ALU.min, ALU.max).then_inc(step, 1)
        dve.wait_ge(step, steps + 5)
        nc.vector.tensor_tensor(parts, levels[:].rearrange("p (s w) -> p s w", w=S.WB), spread(scale),
                                ALU.mult).then_inc(step, 1)
        dve.wait_ge(step, steps + 6)
        nc.vector.engine_nop().then_inc(quantized, 1)

    def turn_all(pe, quantized, turned, lo_made):
        for k, (n, pieces, _, _) in enumerate(jobs):
            pe.wait_ge(quantized, NAMES.index(n) + 1)
            if k >= len(banks):
                pe.wait_ge(lo_made, k - len(banks) + 1)
            for j, piece in enumerate(pieces):
                last = nc.tensor.transpose(banks[k % len(banks)][:, j * 128:(j + 1) * 128], piece, ident)
            last.then_inc(turned, 1)

    def high_halves(act, turned, hi_made):
        for k, (_, pieces, hi, _) in enumerate(jobs):
            act.wait_ge(turned, k + 1)
            nc.scalar.activation(hi, banks[k % len(banks)][:, 0:128 * len(pieces)], ACT.Copy,
                                 scale=S.WSCALE).then_inc(hi_made, 1)

    def low_halves(dve, hi_made, lo_made):
        for k, (_, pieces, hi, lo) in enumerate(jobs):
            dve.wait_ge(hi_made, k + 1)
            nc.vector.scalar_tensor_tensor(out=lo, in0=banks[k % len(banks)][:, 0:128 * len(pieces)],
                                           scalar=S.WSCALE, in1=hi, op0=ALU.mult,
                                           op1=ALU.subtract).then_inc(lo_made, 1)

    return quantize, turn_all, high_halves, low_halves


def global_scale(nc, keep, peaks, unit, name, outputs):
    from contextlib import ExitStack
    import concourse.mybir as mybir
    import concourse.bass as bass
    S = sizes()
    F = mybir.dt.float32
    ALU, AX = mybir.AluOpType, mybir.AxisListType
    scale, ratio = keep["scale_" + name], keep["ratio_" + name]
    with ExitStack() as ctx:
        own = ctx.enter_context(nc.sbuf_tensor(f"own_{name}", [128, 1], F))
        top = ctx.enter_context(nc.sbuf_tensor(f"top_{name}", [128, 1], F))
        inverse = ctx.enter_context(nc.sbuf_tensor(f"inverse_{name}", [128, 1], F))
        step = ctx.enter_context(nc.semaphore(f"step_{name}"))
        reduced = ctx.enter_context(nc.semaphore(f"reduced_{name}"))
        block = ctx.enter_context(nc.Block())

        @block.gpsimd
        def _(pool):
            pool.wait_ge(step, 1)
            nc.gpsimd.partition_all_reduce(top[:], own[:], 128, bass.bass_isa.ReduceOp.max).then_inc(reduced, 1)

        @block.vector
        def _(dve):
            nc.vector.tensor_reduce(own[:], peaks, AX.X, ALU.max).then_inc(step, 1)
            dve.wait_ge(reduced, 1)
            u = 1.0 if unit is None else unit[:, 0:1]
            nc.vector.tensor_scalar(scale[:], top[:], u, 1.0 / S.QMAX, ALU.mult, ALU.mult).then_inc(step, 1)
            dve.wait_ge(step, 2)
            nc.vector.tensor_scalar(scale[:], scale[:], 1e-12, None, ALU.max).then_inc(step, 1)
            dve.wait_ge(step, 3)
            nc.vector.reciprocal(inverse[:], scale[:]).then_inc(step, 1)
            dve.wait_ge(step, 4)
            nc.vector.tensor_scalar(ratio[:], inverse[:], u, None, ALU.mult).then_inc(step, 1)
            for tile, factor, other in outputs:
                o = 1.0 if other is None else other[:, 0:1]
                nc.vector.tensor_scalar(tile[:], scale[:], factor, o, ALU.mult, ALU.mult).then_inc(step, 1)


def inner_products(nc, keep, out, col, i):
    S = sizes()
    x_hi, x_lo, w_hi, w_lo = keep["x_hi"], keep["x_lo"], keep["wi_hi"], keep["wi_lo"]
    pairs = [(c, w, x) for c in range(S.KC) for w, x in ((w_hi, x_hi), (w_hi, x_lo), (w_lo, x_hi))]
    for k, (c, w, x) in enumerate(pairs):
        last = nc.tensor.matmul(out, w[:, c, col:col + 128], x[:, c, i, :], start=k == 0, stop=k == len(pairs) - 1)
    return last


def peak_block(nc, keep):
    from contextlib import ExitStack
    import concourse.mybir as mybir
    S = sizes()
    SEED = S.SEED
    F, I16 = mybir.dt.float32, mybir.dt.int16
    ACT, ALU, AX = mybir.ActivationFunctionType, mybir.AluOpType, mybir.AxisListType
    B, KC, N = S.B, S.KC, S.N
    with ExitStack() as ctx:
        ps = [ctx.enter_context(nc.psum_tensor(f"kbank{i}", [128, 2, 512], F)) for i in range(4)]
        ready = [ctx.enter_context(nc.semaphore(f"k_ready{i}")) for i in range(3)]
        read = [ctx.enter_context(nc.semaphore(f"k_read{i}")) for i in range(3)]
        loaded, rounded, hi_made, lo_made, passed = (
            ctx.enter_context(nc.semaphore(f"k_{n}")) for n in ("loaded", "rounded", "hi_made", "lo_made", "passed"))
        xn = ctx.enter_context(nc.sbuf_tensor("k_xn", [128, KC, N], F))
        levels = ctx.enter_context(nc.sbuf_tensor("k_levels", [128, KC, N], I16))
        block = ctx.enter_context(nc.Block())

        @block.sync
        def _(sp):
            sp.dma_start(xn[:, :, :], keep["xn_dram"][:, 0, :, :]).then_inc(loaded, 16)
            with sp.Fori(1, B) as i:
                sp.wait_ge(rounded, i)
                sp.dma_start(xn[:, :, :], keep["xn_dram"][:, i, :, :]).then_inc(loaded, 16)

        @block.tensor
        def _(pe):
            with pe.Fori(0, B) as i:
                pe.wait_ge(lo_made, i + 1)
                for m in range(S.MI):
                    b = m % 3
                    pe.wait_ge(read[b], SEED + 2 * i + m // 3)
                    for half in range(2):
                        last = inner_products(nc, keep, ps[b][:, half, :], half * S.I + m * 128, i)
                    last.then_inc(ready[b], 1)

        @block.scalar
        def _(act):
            with act.Fori(0, B) as i:
                act.wait_ge(rounded, i + 1)
                pass_waits(act, passed)
                nc.scalar.activation(keep["x_hi"][:, :, i, :], levels[:, :, :], ACT.Copy).then_inc(hi_made, 1)

        @block.vector
        def _(dve):
            for s in read:
                dve.sem_inc(s, SEED)

            def round_batch(b):
                dve.wait_ge(loaded, 16 * (b + 1))
                nc.vector.tensor_scalar(levels[:, :, :], xn[:, :, :], keep["ratio_x"][:, 0:1], None,
                                        ALU.mult).then_inc(rounded, 1)

            def low_halves(b):
                dve.wait_ge(hi_made, b + 1)
                nc.vector.tensor_tensor(keep["x_lo"][:, :, b, :], levels[:, :, :], keep["x_hi"][:, :, b, :],
                                        ALU.subtract).then_inc(lo_made, 1)

            def peaks(i, m):
                b = m % 3
                dve.wait_ge(ready[b], 2 * i + m // 3 + 1)
                nc.vector.tensor_reduce(keep["peak_ug"][:, i, m, :], ps[b][:, :, :], AX.X, ALU.max,
                                        apply_absolute_value=True).then_inc(read[b], 1)

            round_batch(0)
            low_halves(0)
            with dve.Fori(0, B - 1) as i:
                dve.wait_ge(lo_made, i + 1)
                for m in range(S.MI):
                    peaks(i, m)
                    if m == 1:
                        round_batch(i + 1)
                    if m == 3:
                        low_halves(i + 1)
            for m in range(S.MI):
                peaks(B - 1, m)


def gate_block(nc, keep):
    from contextlib import ExitStack
    import concourse.mybir as mybir
    S = sizes()
    SEED, DMA_SEED = S.SEED, S.DMA_SEED
    F, I16 = mybir.dt.float32, mybir.dt.int16
    ACT, ALU, AX = mybir.ActivationFunctionType, mybir.AluOpType, mybir.AxisListType
    PAIRS = S.MI // 2
    room = keep["gated_levels"][:].rearrange("p b m n -> p (b m n)").bitcast(F)
    tanh, product = (room[:, w * PAIRS * 1024:(w + 1) * PAIRS * 1024].rearrange("p (k g n) -> p k g n", k=PAIRS, g=2)
                     for w in range(2))
    with ExitStack() as ctx:
        def sb(name, shape, dt=F):
            return ctx.enter_context(nc.sbuf_tensor(name, shape, dt))

        def sem(name):
            return ctx.enter_context(nc.semaphore(name))

        ps = [ctx.enter_context(nc.psum_tensor(f"gbank{i}", [128, 2, 512], F)) for i in range(3)]
        gate = sb("g_gate", [128, PAIRS, 2, 512], I16)
        sig = sb("g_sig", [128, PAIRS, 2, 512], I16)
        ready, levels_made, tanh_made, sig_made, product_made, peak_made, stored = (
            [sem(f"g_{n}{k}") for k in range(PAIRS)]
            for n in ("ready", "levels", "tanh", "sig", "product", "peak", "stored"))
        block = ctx.enter_context(nc.Block())

        @block.tensor
        def _(pe):
            with pe.Fori(0, S.B) as i:
                for k in range(PAIRS):
                    pe.wait_ge(levels_made[k], SEED + i)
                    for half in range(2):
                        last = inner_products(nc, keep, ps[k][:, half, :], S.I + (2 * k + half) * 128, i)
                    last.then_inc(ready[k], 1)

        @block.scalar
        def _(act):
            for s in levels_made:
                act.sem_inc(s, SEED)
            with act.Fori(0, S.B) as i:
                for k in range(PAIRS):
                    act.wait_ge(ready[k], i + 1)
                    act.wait_ge(product_made[k], SEED + i)
                    nc.scalar.activation(gate[:, k, :, :], ps[k][:, :, :], ACT.Copy,
                                         scale=keep["ratio_gate"][:, 0:1]).then_inc(levels_made[k], 1)
                    act.wait_ge(levels_made[k], SEED + i + 1)
                    nc.scalar.activation(tanh[:, k, :, :], gate[:, k, :, :], ACT.Tanh,
                                         scale=keep["half_gate"][:, 0:1]).then_inc(tanh_made[k], 1)

        @block.vector
        def _(dve):
            for s in product_made:
                dve.sem_inc(s, SEED)

            def round_sigmoid(i, k):
                dve.wait_ge(tanh_made[k], i + 1)
                nc.vector.tensor_scalar(sig[:, k, :, :], tanh[:, k, :, :], 32768.0, 32767.0, ALU.mult,
                                        ALU.min).then_inc(sig_made[k], 1)

            def multiply(i, k):
                dve.wait_ge(sig_made[k], i + 1)
                dve.wait_ge(stored[k], DMA_SEED + 16 * i)
                nc.vector.scalar_tensor_tensor(out=product[:, k, :, :], in0=sig[:, k, :, :], scalar=32768.0,
                                               in1=gate[:, k, :, :], op0=ALU.add,
                                               op1=ALU.mult).then_inc(product_made[k], 1)

            def peak(i, k):
                dve.wait_ge(product_made[k], SEED + i + 1)
                nc.vector.tensor_reduce(keep["peak_g2"][:, i, k:k + 1], product[:, k, :, :], AX.XY, ALU.max,
                                        apply_absolute_value=True).then_inc(peak_made[k], 1)

            with dve.Fori(0, S.B) as i:
                round_sigmoid(i, 0)
                round_sigmoid(i, 1)
                multiply(i, 0)
                round_sigmoid(i, 2)
                multiply(i, 1)
                peak(i, 0)
                multiply(i, 2)
                peak(i, 1)
                peak(i, 2)

        @block.sync
        def _(sp):
            for s in stored:
                sp.sem_inc(s, DMA_SEED)
            with sp.Fori(0, S.B) as i:
                for k in range(PAIRS):
                    sp.wait_ge(product_made[k], SEED + i + 1)
                    sp.dma_start(keep["gated_dram"][:, i, 2 * k:2 * k + 2, :], product[:, k, :, :]).then_inc(stored[k], 16)
            for k in range(PAIRS):
                sp.wait_ge(stored[k], DMA_SEED + 16 * S.B)
                sp.wait_ge(peak_made[k], S.B)


def product_block(nc, keep):
    from contextlib import ExitStack
    import concourse.mybir as mybir
    S = sizes()
    SEED, DMA_SEED = S.SEED, S.DMA_SEED
    F, I16 = mybir.dt.float32, mybir.dt.int16
    ACT, ALU, AX = mybir.ActivationFunctionType, mybir.AluOpType, mybir.AxisListType
    PAIRS = S.MI // 2
    levels = keep["gated_levels"]
    with ExitStack() as ctx:
        def sb(name, shape, dt=F):
            return ctx.enter_context(nc.sbuf_tensor(name, shape, dt))

        def sem(name):
            return ctx.enter_context(nc.semaphore(name))

        ps = [ctx.enter_context(nc.psum_tensor(f"pbank{i}", [128, 2, 512], F)) for i in range(3)]
        up = sb("p_up", [128, PAIRS, 2, 512], I16)
        gated = sb("p_gated", [128, PAIRS, 2, 512])
        product = sb("p_product", [128, 2, 2, 512])
        ready, up_made, levels_made, loaded, stored, used = (
            [sem(f"p_{n}{k}") for k in range(PAIRS)]
            for n in ("ready", "up", "levels", "loaded", "stored", "used"))
        product_made, peak_made, passed = sem("p_product_made"), sem("p_peak_made"), sem("p_passed")
        block = ctx.enter_context(nc.Block())

        @block.tensor
        def _(pe):
            with pe.Fori(0, S.B) as i:
                for k in range(PAIRS):
                    pe.wait_ge(up_made[k], SEED + i)
                    for half in range(2):
                        last = inner_products(nc, keep, ps[k][:, half, :], (2 * k + half) * 128, i)
                    last.then_inc(ready[k], 1)

        @block.scalar
        def _(act):
            for s in up_made:
                act.sem_inc(s, SEED)
            for s in levels_made:
                act.sem_inc(s, SEED)
            for s in stored:
                act.sem_inc(s, DMA_SEED)
            with act.Fori(0, S.B) as i:
                for k in range(PAIRS):
                    act.wait_ge(loaded[k], 16 * (i + 1))
                    pass_waits(act, passed)
                    nc.scalar.activation(levels[:, i, 2 * k:2 * k + 2, :], gated[:, k, :, :], ACT.Copy,
                                         scale=keep["ratio_g2"][:, 0:1]).then_inc(levels_made[k], 1)
                    act.wait_ge(ready[k], i + 1)
                    act.wait_ge(used[k], SEED + i)
                    act.wait_ge(stored[k], DMA_SEED + 16 * i)
                    nc.scalar.activation(up[:, k, :, :], ps[k][:, :, :], ACT.Copy,
                                         scale=keep["ratio_up"][:, 0:1]).then_inc(up_made[k], 1)

        @block.vector
        def _(dve):
            for s in used:
                dve.sem_inc(s, SEED)
            dve.sem_inc(peak_made, SEED)

            def multiply(i, k):
                dve.wait_ge(levels_made[k], SEED + i + 1)
                dve.wait_ge(up_made[k], SEED + i + 1)
                dve.wait_ge(peak_made, SEED + PAIRS * i + (0, 0, 1)[k])
                nc.vector.tensor_tensor(product[:, k % 2, :, :], levels[:, i, 2 * k:2 * k + 2, :], up[:, k, :, :],
                                        ALU.mult).then_inc(used[k], 1)

            def peak(i, k):
                dve.wait_ge(used[k], SEED + i + 1)
                nc.vector.tensor_reduce(keep["peak_o"][:, i, k:k + 1], product[:, k % 2, :, :], AX.XY, ALU.max,
                                        apply_absolute_value=True).then_inc(peak_made, 1)

            with dve.Fori(0, S.B) as i:
                multiply(i, 0)
                multiply(i, 1)
                peak(i, 0)
                multiply(i, 2)
                peak(i, 1)
                peak(i, 2)

        @block.sync
        def _(sp):
            def load(i, k):
                sp.dma_start(gated[:, k, :, :], keep["gated_dram"][:, i, 2 * k:2 * k + 2, :]).then_inc(loaded[k], 16)

            def store(i, k):
                sp.wait_ge(up_made[k], SEED + i + 1)
                pass_waits(sp, passed)
                sp.dma_start(keep["up_dram"][:, i, 2 * k:2 * k + 2, :], up[:, k, :, :]).then_inc(stored[k], 16)

            for k in range(PAIRS):
                load(0, k)
            with sp.Fori(0, S.B - 1) as i:
                for k in range(PAIRS):
                    sp.wait_ge(levels_made[k], SEED + i + 1)
                    pass_waits(sp, passed)
                    load(i + 1, k)
                    store(i, k)
            for k in range(PAIRS):
                store(S.B - 1, k)
            for k in range(PAIRS):
                sp.wait_ge(stored[k], DMA_SEED + 16 * S.B)


def down_block(nc, keep, out):
    from contextlib import ExitStack
    import concourse.mybir as mybir
    S = sizes()
    F, H16, I16 = mybir.dt.float32, mybir.dt.float16, mybir.dt.int16
    ACT, ALU = mybir.ActivationFunctionType, mybir.AluOpType
    B, T, C, MI = S.B, S.T, S.C, S.MI
    out_v = out.rearrange("b (t p) c -> p b t c", p=128)
    with ExitStack() as ctx:
        def sb(name, shape, dt=F):
            return ctx.enter_context(nc.sbuf_tensor(name, shape, dt))

        def sem(name):
            return ctx.enter_context(nc.semaphore(name))

        ps = [[ctx.enter_context(nc.psum_tensor(f"dbank{s}{i}", [128, 2, C], F)) for i in range(2)] for s in range(2)]
        up = sb("d_up", [128, 2, MI, 512], I16)
        product = sb("d_product", [128, MI, 512])
        h = sb("d_h", [128, 2, T, C])
        levels = sb("d_levels", [128, 2, MI, 512], I16)
        hi = sb("d_hi", [128, 2, MI, 512], H16)
        lo = sb("d_lo", [128, 2, MI, 512], H16)
        y = sb("d_y", [128, 2, T, C])
        up_loaded, h_loaded, stored = ([sem(f"d_{n}{s}") for s in range(2)] for n in ("up_loaded", "h_loaded", "stored"))
        product_made, rounded, hi_made, lo_made = sem("d_product"), sem("d_rounded"), sem("d_hi_made"), sem("d_lo_made")
        ready, summed, y_free, passed = sem("d_ready"), sem("d_summed"), sem("d_y_free"), sem("d_passed")
        READY0, SUMMED0, FREE0 = 4, 4, 2
        block = ctx.enter_context(nc.Block())

        @block.sync
        def _(sp):
            def load_up(b, s):
                wait_past(sp, product_made, b - 1)
                pass_waits(sp, passed)
                sp.dma_start(up[:, s, :, :], keep["up_dram"][:, b, :, :]).then_inc(up_loaded[s], 16)

            def load_h(b, s):
                sp.wait_ge(summed, SUMMED0 + 2 * (b - 1))
                pass_waits(sp, passed)
                sp.dma_start(h[:, s, :, :], keep["h_dram"][:, b, :, :]).then_inc(h_loaded[s], 16)

            for s in range(2):
                load_up(s, s)
            with sp.Fori(0, (B - 2) // 2) as i:
                for s in range(2):
                    load_h(2 * i + s, s)
                    load_up(2 * i + 2 + s, s)
            for s in range(2):
                load_h(B - 2 + s, s)

        @block.gpsimd
        def _(pool):
            pool.sem_inc(y_free, FREE0)
            with pool.Fori(0, B // 2) as i:
                for s in range(2):
                    pool.wait_ge(summed, SUMMED0 + 2 * (2 * i + s) + 2)
                    pool.dma_start(out_v[:, 2 * i + s, :, :], y[:, s, :, :]).then_inc(stored[s], 16)
                    pool.wait_ge(stored[s], 16 * (i + 1))
                    pool.sem_inc(y_free, 1)

        @block.scalar
        def _(act):
            def round_product(b, s):
                act.wait_ge(product_made, b + 1)
                wait_past(act, lo_made, b - 1)
                nc.scalar.activation(levels[:, s, :, :], product[:, :, :], ACT.Copy,
                                     scale=keep["ratio_o"][:, 0:1]).then_inc(rounded, 1)

            def high_halves(b, s):
                act.wait_ge(rounded, b + 1)
                act.wait_ge(ready, READY0 + 2 * (b - 1))
                nc.scalar.activation(hi[:, s, :, :], levels[:, s, :, :], ACT.Copy).then_inc(hi_made, 1)

            round_product(0, 0)
            high_halves(0, 0)
            round_product(1, 1)
            with act.Fori(0, (B - 2) // 2) as i:
                for s in range(2):
                    high_halves(2 * i + s + 1, 1 - s)
                    round_product(2 * i + s + 2, s)
            high_halves(B - 1, 1)

        @block.vector
        def _(dve):
            dve.sem_inc(summed, SUMMED0)

            def multiply(b, s, i):
                dve.wait_ge(up_loaded[s], 16 * (i + 1))
                wait_past(dve, rounded, b)
                nc.vector.tensor_tensor(product[:, :, :], keep["gated_levels"][:, b, :, :], up[:, s, :, :],
                                        ALU.mult).then_inc(product_made, 1)

            def low_halves(b, s):
                dve.wait_ge(hi_made, b + 1)
                nc.vector.tensor_tensor(lo[:, s, :, :], levels[:, s, :, :], hi[:, s, :, :],
                                        ALU.subtract).then_inc(lo_made, 1)

            def add_residual(b, s, i):
                dve.wait_ge(h_loaded[s], 16 * (i + 1))
                dve.wait_ge(y_free, FREE0 + b - 1)
                for half in range(2):
                    dve.wait_ge(ready, READY0 + 2 * b + half + 1)
                    nc.vector.scalar_tensor_tensor(out=y[:, s, 2 * half:2 * half + 2, :], in0=ps[s][half][:, :, :],
                                                   scalar=keep["out_unit"][:, 0:1],
                                                   in1=h[:, s, 2 * half:2 * half + 2, :], op0=ALU.mult,
                                                   op1=ALU.add).then_inc(summed, 1)

            multiply(0, 0, 0)
            multiply(1, 1, 0)
            low_halves(0, 0)
            with dve.Fori(0, (B - 2) // 2) as i:
                for s in range(2):
                    multiply(2 * i + s + 2, s, i + 1)
                    low_halves(2 * i + s + 1, 1 - s)
                    add_residual(2 * i + s, s, i)
            low_halves(B - 1, 1)
            for s in range(2):
                add_residual(B - 2 + s, s, B // 2 - 1)

        @block.tensor
        def _(pe):
            pe.sem_inc(ready, READY0)
            with pe.Fori(0, B // 2) as i:
                for s in range(2):
                    b = 2 * i + s
                    pe.wait_ge(lo_made, b + 1)
                    pe.wait_ge(summed, SUMMED0 + 2 * (b - 1))
                    for t in range(T):
                        tok = slice(t * 128, (t + 1) * 128)
                        pairs = [(m, a, w) for m in range(MI) for a, w in
                                 ((hi, keep["wo_hi"]), (lo, keep["wo_hi"]), (hi, keep["wo_lo"]))]
                        for k, (m, a, w) in enumerate(pairs):
                            last = nc.tensor.matmul(ps[s][t // 2][:, t % 2, :], a[:, s, m, tok], w[:, m, :],
                                                    start=k == 0, stop=k == len(pairs) - 1)
                        if t % 2:
                            last.then_inc(ready, 1)


def ffn(nc, io, keep, out):
    from contextlib import ExitStack
    import concourse.mybir as mybir
    S = sizes()
    F, H16, I16 = mybir.dt.float32, mybir.dt.float16, mybir.dt.int16
    B, T, C, KC, MI, N = S.B, S.T, S.C, S.KC, S.MI, S.N
    with ExitStack() as ctx:
        def sb(name, shape, dt=F):
            keep[name] = ctx.enter_context(nc.sbuf_tensor(name, shape, dt))
            return keep[name]

        for name in ("x", "up", "gate", "g2", "o"):
            sb("scale_" + name, [128, 1])
            sb("ratio_" + name, [128, 1])
        for name in ("unit_x", "half_gate", "unit_g2", "unit_o", "out_unit"):
            sb(name, [128, 1])
        sb("peak_ug", [128, B, MI, 2])
        sb("peak_g2", [128, B, MI // 2])
        sb("peak_o", [128, B, MI // 2])
        sb("gated_levels", [128, B, MI, N], I16)
        with ExitStack() as inner:
            for name in ("x_hi", "x_lo"):
                keep[name] = inner.enter_context(nc.sbuf_tensor(name, [128, KC, B, N], H16))
            global_scale(nc, keep, keep["peak_x"][:, :], None, "x", [(keep["unit_x"], 1.0 / S.WSCALE, None)])
            peak_block(nc, keep)
            peaks = keep["peak_ug"]
            global_scale(nc, keep, peaks[:, :, :, 0].rearrange("p b m -> p (b m)"), keep["unit_x"], "up", [])
            global_scale(nc, keep, peaks[:, :, :, 1].rearrange("p b m -> p (b m)"), keep["unit_x"], "gate",
                         [(keep["half_gate"], 0.5, None), (keep["unit_g2"], 1.0 / 65536.0, None)])
            gate_block(nc, keep)
            global_scale(nc, keep, keep["peak_g2"][:].rearrange("p b m -> p (b m)"), keep["unit_g2"], "g2",
                         [(keep["unit_o"], 1.0, keep["scale_up"])])
            product_block(nc, keep)
        global_scale(nc, keep, keep["peak_o"][:].rearrange("p b m -> p (b m)"), keep["unit_o"], "o",
                     [(keep["out_unit"], 1.0 / S.WSCALE, None)])
        down_block(nc, keep, out)


def build(nc, io, out):
    from contextlib import ExitStack
    import concourse.mybir as mybir
    S = sizes()
    F, H16 = mybir.dt.float32, mybir.dt.float16
    keep = {"h_dram": nc.dram_tensor("h_stream", (128, S.B, S.T, S.C), F, kind="Internal").ap(),
            "xn_dram": nc.dram_tensor("xn_stream", (128, S.B, S.KC, S.N), F, kind="Internal").ap(),
            "gated_dram": nc.dram_tensor("gated", (128, S.B, S.MI, S.N), F, kind="Internal").ap(),
            "up_dram": nc.dram_tensor("up_levels", (128, S.B, S.MI, S.N), mybir.dt.int16, kind="Internal").ap()}
    with ExitStack() as ctx:
        for name, shape, dt in (("peak_x", [128, S.B], F),
                                ("wi_hi", [128, S.KC, 2 * S.I], H16), ("wi_lo", [128, S.KC, 2 * S.I], H16),
                                ("wo_hi", [128, S.MI, S.C], H16), ("wo_lo", [128, S.MI, S.C], H16)):
            keep[name] = ctx.enter_context(nc.sbuf_tensor(name, shape, dt))
        attention_block(nc, io, keep)
        ffn(nc, io, keep, out)


def kernel(x, L0_tok_embeddings, L0_tok_project_kernel, L0_attn_w_qkv, L0_attn_w_proj, L0_attn_b_proj,
           L0_ffn_w_gate, L0_ffn_w_up, L0_ffn_w_down):
    import numpy as np
    import concourse.bacc as bacc
    from concourse import mybir
    from concourse.bass_utils import run_bass_kernel_spmd

    S = sizes()

    def rows_to_partitions(a):
        return np.ascontiguousarray(a.reshape(-1, 128, a.shape[1]).transpose(1, 0, 2))

    w_qkv = np.asarray(L0_attn_w_qkv)
    big, token = 60000.0, np.arange(S.N)
    tile_of = token // 128 == np.arange(S.T)[:, None]
    tail = np.zeros((32, 3, S.N), np.float16)
    tail[0:S.T, 0:2] = np.where(tile_of & (token % 128 >= S.BLOCK), big, 0.0)[:, None]
    tail[S.T, 0] = tail[S.T + 1, 1] = 1.0
    tail[0:S.T, 2] = np.where(tile_of & (token % 128 < S.BLOCK), -big, 0.0)
    early = np.ascontiguousarray(-tail[0:S.T, 2].reshape(S.T, S.T, 128).transpose(2, 1, 0))
    arrays = {
        "ids": np.ascontiguousarray(np.asarray(x).reshape(S.B * S.T, 128).T),
        "table": np.asarray(L0_tok_embeddings),
        "w_tok": np.asarray(L0_tok_project_kernel),
        "w_attn": np.ascontiguousarray(np.stack(
            [rows_to_partitions(w.T) for w in (w_qkv[S.C:2 * S.C], w_qkv[0:S.C], w_qkv[2 * S.C:],
                                               np.asarray(L0_attn_w_proj))], axis=1)),
        "bias": np.asarray(L0_attn_b_proj).reshape(1, S.C),
        "tail": tail,
        "early": early,
        "ident": np.eye(128, dtype=np.float32),
        "w_up": rows_to_partitions(np.asarray(L0_ffn_w_up)),
        "w_gate": rows_to_partitions(np.asarray(L0_ffn_w_gate)),
        "w_down": rows_to_partitions(np.asarray(L0_ffn_w_down)),
    }
    nc = bacc.Bacc("TRN2", target_bir_lowering=False, num_devices=1)
    io = {n: nc.dram_tensor(f"in_{n}", a.shape, mybir.dt.from_np(a.dtype), kind="ExternalInput").ap()
          for n, a in arrays.items()}
    out = nc.dram_tensor("out", (S.B, S.N, S.C), mybir.dt.float32, kind="ExternalOutput").ap()
    build(nc, io, out)
    r = run_bass_kernel_spmd(nc, [{f"in_{n}": a for n, a in arrays.items()}], core_ids=[0])
    return r.results[0]["out"]
```
